# Optimizing a Trainium2 kernel written in Bass

```python
import numpy as np
import jax
import jax.numpy as jnp

def _softmax(x, axis=-1):
    return jax.nn.softmax(x, axis=axis)

def _gelu(x):
    return jax.nn.gelu(x, approximate=True)

def _silu(x):
    return jax.nn.silu(x)

def _sigmoid(x):
    return jax.nn.sigmoid(x)

def _layernorm(x, axis=-1, eps=1e-05):
    m = jnp.mean(x, axis=axis, keepdims=True)
    v = jnp.var(x, axis=axis, keepdims=True)
    return (x - m) / jnp.sqrt(v + eps)

def _scatter_add(tgt, idx, src, axis=0):
    return tgt.at[idx].add(src)

def _segment_sum(src, seg, n):
    return jax.ops.segment_sum(src, seg, n)
kernel_name = 'mk_gnn_ffn_d1_gnn_r8_d28e84'

def setup_inputs(seed: int=0):
    np.random.seed(seed)
    _w = jnp.asarray

    def _rec_inputs():
        import jax
        import jax.numpy as jnp
        _gk = jax.random.key(seed)
        x = -0.0002117 + 1 * jax.random.normal(jax.random.fold_in(_gk, 1), (12500, 256), jnp.float32)
        src = jax.random.randint(jax.random.fold_in(_gk, 2), (200000,), 0, 12500, jnp.int32)
        dst = jnp.minimum((12500 * jax.random.uniform(jax.random.fold_in(_gk, 3), (200000,)) ** 2.0).astype(jnp.int32), 99999)
        _o = jnp.argsort(dst, stable=True)
        src = src[_o]
        dst = dst[_o]
        edge_weight = jax.random.uniform(jax.random.fold_in(_gk, 12), (200000,), jnp.float32, 0.0, 1)
        return (x, src, dst, edge_weight)
    x, src, dst, edge_weight = _rec_inputs()

    def _L0_gnn_setup():
        import jax, jax.numpy as jnp
        import numpy as np
        N = 12500
        F_IN = 256
        B = 4
        F_OUT = 256
        E = 400000
        EPS = 1e-05
        key = jax.random.key(seed)
        ks = jax.random.split(key, 6)
        atom_features = jax.random.normal(ks[0], (N, F_IN), dtype=jnp.float32)
        bn_gamma = jnp.ones((F_IN,), dtype=jnp.float32)
        bn_beta = jnp.zeros((F_IN,), dtype=jnp.float32)
        W = jax.random.normal(ks[1], (B * F_OUT, F_IN), dtype=jnp.float32) * (1.0 / np.sqrt(F_IN))
        b = jnp.zeros((B * F_OUT,), dtype=jnp.float32)
        edge_row = jax.random.randint(ks[2], (E,), 0, N, dtype=jnp.int32)
        edge_col = jax.random.randint(ks[3], (E,), 0, B * N, dtype=jnp.int32)
        edge_val = jax.random.uniform(ks[4], (E,), dtype=jnp.float32)
        return {'atom_features': atom_features, 'bn_gamma': bn_gamma, 'bn_beta': bn_beta, 'W': W, 'b': b, 'edge_row': edge_row, 'edge_col': edge_col, 'edge_val': edge_val}
    _L0_gnn_all = _L0_gnn_setup()
    _L0_gnn_in = {k: v for k, v in _L0_gnn_all.items() if k in ('bn_gamma', 'bn_beta', 'W', 'b')}
    del _L0_gnn_all

    def _L0_ffn_setup():
        import jax, jax.numpy as jnp
        import numpy as np
        BN_EPS = 0.001

        def _bn(h, g, b, m, v):
            return g * (h - m) * jax.lax.rsqrt(v + BN_EPS) + b
        key = jax.random.key(seed)
        ks = jax.random.split(key, 8)
        B, F, Df = (256, 64, 256)
        E, H, D = (8, 256, 256)
        s1 = 1.0 / np.sqrt(Df)
        s2 = 1.0 / np.sqrt(H)
        return {'x': jax.random.normal(ks[0], (B, F, Df), jnp.float32), 'Wr': jax.random.normal(ks[1], (Df, E), jnp.float32) * s1, 'br': jnp.zeros((E,), jnp.float32), 'W1': jax.random.normal(ks[2], (E, Df, H), jnp.float32) * s1, 'b1': jnp.zeros((E, H), jnp.float32), 'g1': jnp.ones((E, H), jnp.float32), 'be1': jnp.zeros((E, H), jnp.float32), 'm1': jnp.zeros((E, H), jnp.float32), 'v1': jnp.ones((E, H), jnp.float32), 'W2': jax.random.normal(ks[3], (E, H, H), jnp.float32) * s2, 'b2': jnp.zeros((E, H), jnp.float32), 'g2': jnp.ones((E, H), jnp.float32), 'be2': jnp.zeros((E, H), jnp.float32), 'm2': jnp.zeros((E, H), jnp.float32), 'v2': jnp.ones((E, H), jnp.float32), 'Wo': jax.random.normal(ks[4], (E, H, D), jnp.float32) * s2, 'bo': jnp.zeros((E, D), jnp.float32)}
    _L0_ffn_all = _L0_ffn_setup()
    _L0_ffn_in = {k: v for k, v in _L0_ffn_all.items() if k in ('Wr', 'br', 'W1', 'b1', 'g1', 'be1', 'm1', 'v1', 'W2', 'b2', 'g2', 'be2', 'm2', 'v2', 'Wo', 'bo')}
    del _L0_ffn_all
    return {'x': x, 'src': src, 'dst': dst, 'edge_weight': edge_weight, 'L0_gnn_bn_gamma': _L0_gnn_in['bn_gamma'], 'L0_gnn_bn_beta': _L0_gnn_in['bn_beta'], 'L0_gnn_W': _L0_gnn_in['W'], 'L0_gnn_b': _L0_gnn_in['b'], 'L0_ffn_Wr': _L0_ffn_in['Wr'], 'L0_ffn_br': _L0_ffn_in['br'], 'L0_ffn_W1': _L0_ffn_in['W1'], 'L0_ffn_b1': _L0_ffn_in['b1'], 'L0_ffn_g1': _L0_ffn_in['g1'], 'L0_ffn_be1': _L0_ffn_in['be1'], 'L0_ffn_m1': _L0_ffn_in['m1'], 'L0_ffn_v1': _L0_ffn_in['v1'], 'L0_ffn_W2': _L0_ffn_in['W2'], 'L0_ffn_b2': _L0_ffn_in['b2'], 'L0_ffn_g2': _L0_ffn_in['g2'], 'L0_ffn_be2': _L0_ffn_in['be2'], 'L0_ffn_m2': _L0_ffn_in['m2'], 'L0_ffn_v2': _L0_ffn_in['v2'], 'L0_ffn_Wo': _L0_ffn_in['Wo'], 'L0_ffn_bo': _L0_ffn_in['bo']}

def reference(x, src, dst, edge_weight, L0_gnn_bn_gamma, L0_gnn_bn_beta, L0_gnn_W, L0_gnn_b, L0_ffn_Wr, L0_ffn_br, L0_ffn_W1, L0_ffn_b1, L0_ffn_g1, L0_ffn_be1, L0_ffn_m1, L0_ffn_v1, L0_ffn_W2, L0_ffn_b2, L0_ffn_g2, L0_ffn_be2, L0_ffn_m2, L0_ffn_v2, L0_ffn_Wo, L0_ffn_bo):
    import jax
    import jax.numpy as jnp

    def _L0_gnn_ref(atom_features, bn_gamma, bn_beta, W, b, edge_row, edge_col, edge_val):
        import jax, jax.numpy as jnp
        import numpy as np
        N = 12500
        F_IN = 256
        B = 4
        F_OUT = 256
        E = 400000
        EPS = 1e-05
        mean = jnp.mean(atom_features, axis=0)
        var = jnp.mean(jnp.square(atom_features - mean), axis=0)
        x = (atom_features - mean) * (bn_gamma / jnp.sqrt(var + EPS)) + bn_beta
        x = jax.nn.elu(x)
        h = x @ W.T + b
        h = h.reshape(N, B, F_OUT).transpose(1, 0, 2).reshape(B * N, F_OUT)
        msgs = edge_val[:, None] * h[edge_col]
        out = jax.ops.segment_sum(msgs, edge_row, num_segments=N)
        return out

    def _L0_ffn_ref(x, Wr, br, W1, b1, g1, be1, m1, v1, W2, b2, g2, be2, m2, v2, Wo, bo):
        import jax, jax.numpy as jnp
        import numpy as np
        BN_EPS = 0.001

        def _bn(h, g, b, m, v):
            return g * (h - m) * jax.lax.rsqrt(v + BN_EPS) + b
        feat = jnp.mean(x, axis=0)
        w = jax.nn.softmax(feat @ Wr + br, axis=-1)
        h = jnp.einsum('bfd,edh->bfeh', x, W1) + b1
        h = jax.nn.relu(_bn(h, g1, be1, m1, v1))
        h = jnp.einsum('bfeh,ehk->bfek', h, W2) + b2
        h = jax.nn.relu(_bn(h, g2, be2, m2, v2))
        y = jnp.einsum('bfeh,ehd->bfed', h, Wo) + bo
        return jnp.einsum('bfed,fe->bfd', y, w)
    x = x + _L0_gnn_ref(_layernorm(x, axis=-1), L0_gnn_bn_gamma, L0_gnn_bn_beta, L0_gnn_W, L0_gnn_b, src, dst, edge_weight)
    x = x + _L0_ffn_ref(_layernorm(x, axis=-1)[None], L0_ffn_Wr, L0_ffn_br, L0_ffn_W1, L0_ffn_b1, L0_ffn_g1, L0_ffn_be1, L0_ffn_m1, L0_ffn_v1, L0_ffn_W2, L0_ffn_b2, L0_ffn_g2, L0_ffn_be2, L0_ffn_m2, L0_ffn_v2, L0_ffn_Wo, L0_ffn_bo)[0]
    return x

_drawn_inputs = setup_inputs


def setup_inputs(seed=0):
    import zlib

    import numpy as np

    out = dict(_drawn_inputs(seed))
    spreads = {'L0_gnn_bn_gamma': (1.0, 0.2),
     'L0_gnn_bn_beta': (0.0, 0.1),
     'L0_gnn_b': (0.0, 0.1),
     'L0_ffn_br': (0.0, 0.797),
     'L0_ffn_b1': (0.0, 0.8),
     'L0_ffn_g1': (1.0, 0.6),
     'L0_ffn_be1': (0.0, 0.8),
     'L0_ffn_m1': (0.0, 0.8),
     'L0_ffn_v1': (1.0, 0.6),
     'L0_ffn_b2': (0.0, 0.674),
     'L0_ffn_g2': (1.0, 0.6),
     'L0_ffn_be2': (0.0, 0.684),
     'L0_ffn_m2': (0.0, 0.663),
     'L0_ffn_v2': (1.0, 0.6),
     'L0_ffn_bo': (0.0, 0.486)}
    factors = {}
    for name, (base, spread) in spreads.items():
        noise = np.random.default_rng([zlib.crc32(name.encode()), seed]).standard_normal(out[name].shape)
        drawn = base * np.exp(spread * noise) if base else spread * noise
        out[name] = jnp.asarray(drawn.astype(out[name].dtype))
    for name, factor in factors.items():
        out[name] = (out[name] * factor).astype(out[name].dtype)
    return out
```

```python
from contextlib import ExitStack

import concourse.bass as bass
from concourse import mybir

F32 = mybir.dt.float32
F32R = mybir.dt.float32r
I32 = mybir.dt.int32
ALU = mybir.AluOpType
ACT = mybir.ActivationFunctionType
AX = mybir.AxisListType.X

P = 128
D = 256
KD = D // P
GROUP = 512
TG = GROUP // P
LN_EPS = 1e-5
GNN_EPS = 1e-5
FFN_EPS = 1e-3
NACC = 4
UN = 8
HALF = 4
WIN = 32
BANDS = 4
TW = 125
TGROUP = 4 * TW
SRC, WGT, REL, DST = range(4)


def in_pairs(eng, n, body):
    with eng.Fori(0, n // 2) as j:
        for par in range(2):
            body(j, par, 2 * j + par)
    body(n // 2, 0, n - 1)


def alone(eng, passed):
    eng.sem_inc(passed, 1)


class Stage:

    def __init__(self, nc):
        self.nc = nc
        self.ctx = ExitStack()
        self.semaphores = []

    def __enter__(self):
        self.ctx.__enter__()
        return self

    def __exit__(self, *a):
        if self.semaphores:
            self.nc.clear_and_free_semaphores(self.semaphores)
            self.nc.all_engine_barrier()
        return self.ctx.__exit__(*a)

    def sb(self, name, shape, dt=F32):
        return self.ctx.enter_context(self.nc.sbuf_tensor(name, shape, dt))

    def ps(self, name, shape):
        return self.ctx.enter_context(self.nc.psum_tensor(name, shape, F32))

    def sem(self, name):
        self.semaphores.append(self.nc.alloc_semaphore(name=name))
        return self.semaphores[-1]

    def sems(self, name, n):
        return [self.sem(f"{name}{i}") for i in range(n)]


def stage_setup(nc, T):
    with Stage(nc) as S:
        wl = S.sb("w_rows", [P, T.OC, D])
        zeros = S.sb("zeros", [P, 4096])
        ones = S.sb("ones_sq", [P, P])
        ps = S.ps("ps_w", [P, 2, GROUP])
        vectors_loaded, w_loaded, zeroed, ones_set, consts, ident_ready, zero_stored, turned, copied = [
            S.sem(n) for n in ("vectors_loaded", "w_loaded", "zeroed", "ones_set", "consts", "ident_ready",
                               "zero_stored", "turned", "copied")]
        with nc.Block() as block:

            @block.sync
            def _(sp):
                sp.dma_start(wl[:, :, :], T.W.rearrange("(o p) d -> p o d", p=P)).then_inc(w_loaded, 16)
                with nc.allow_non_contiguous_dma(reason="two vectors of 256 as columns"):
                    sp.dma_start(T.gam[:, :], T.gamma.rearrange("(k p) -> p k", p=P)).then_inc(vectors_loaded, 16)
                    sp.dma_start(T.bet[:, :], T.beta.rearrange("(k p) -> p k", p=P)).then_inc(vectors_loaded, 16)
                sp.dma_start(T.bias_bc[:, :], T.b.rearrange("(a n) -> a n", a=1).to_broadcast([P, BANDS * D])) \
                    .then_inc(vectors_loaded, 16)
                sp.wait_ge(zeroed, 1)
                sp.dma_start(T.table[T.N:T.N + WIN, :], zeros[0:WIN, 0:D]).then_inc(zero_stored, 16)
                n = 1
                for acc in T.acc:
                    flat = acc.rearrange("r d -> (r d)")
                    total, at = T.ACC_ROWS * D, 0
                    while at < total:
                        w = min(4096, (total - at) // P)
                        sp.dma_start(flat[at:at + P * w].rearrange("(p w) -> p w", p=P), zeros[:, 0:w]) \
                            .then_inc(zero_stored, 16)
                        at += P * w
                        n += 1
                sp.wait_ge(vectors_loaded, 48)
                sp.wait_ge(zero_stored, 16 * n)

            @block.gpsimd
            def _(pool):
                pool.memset(ones[:, :], 1.0).then_inc(ones_set, 1)
                pool.wait_ge(ones_set, 1)
                pool.affine_select(out=T.ident[:, :], in_=ones[:, :], compare_op=ALU.is_equal, fill=0.0, base=0,
                                   pattern=[[-1, P]], channel_multiplier=1).then_inc(ident_ready, 1)
                pool.memset(zeros[:, :], 0.0).then_inc(zeroed, 1)
                pool.affine_select(out=T.before[:, :], in_=ones[:, :], compare_op=ALU.is_gt, fill=0.0, base=0,
                                   pattern=[[-1, P]], channel_multiplier=1).then_inc(consts, 1)
                pool.iota(T.iota_win[:, :], [[1, WIN]], base=0, channel_multiplier=0,
                          allow_small_or_imprecise_dtypes=True).then_inc(consts, 1)
                pool.iota(T.spare[:, :], [[0, HALF]], base=T.N, channel_multiplier=1,
                          allow_small_or_imprecise_dtypes=True).then_inc(consts, 1)
                pool.memset(T.eps_ln[:, :], LN_EPS).then_inc(consts, 1)
                pool.memset(T.eps_ffn[:, :], FFN_EPS).then_inc(consts, 1)
                pool.wait_ge(consts, 5)

            @block.tensor
            def _(pe):
                pe.wait_ge(ident_ready, 1)
                pe.wait_ge(w_loaded, 16)
                for o in range(T.OC):
                    if o >= 2:
                        pe.wait_ge(copied, o - 1)
                    for k in range(KD):
                        last = pe.transpose(ps[:, o % 2, k * P:(k + 1) * P], wl[:, o, k * P:(k + 1) * P],
                                            T.ident[:, :])
                    last.then_inc(turned, 1)

            @block.scalar
            def _(act):
                for o in range(T.OC):
                    act.wait_ge(turned, o + 1)
                    act.copy(T.wt[:, :, o * P:(o + 1) * P],
                             ps[:, o % 2, 0:D].rearrange("p (k n) -> p k n", k=KD)).then_inc(copied, 1)


def stage_norm(nc, T):
    with Stage(nc) as S:
        xin = S.sb("ln_x", [P, 2, TG, D])
        xl = S.sb("ln_y", [P, 2, TG, D])
        stats = S.sb("ln_stats", [P, TG, 6])
        mv = S.sb("ln_mv", [P, TG, 2])
        std = S.sb("ln_std", [P, TG, 1])
        rstd = S.sb("ln_rstd", [P, TG, 1])
        ps = S.ps("ps_ln", [P, 4, GROUP])
        x_ready, y_ready, turned, bank_copied = [S.sems(n, 2) for n in ("x_ready", "y_ready", "x_turned", "xt_copied")]
        passed = S.sem("n_passed")
        stats_done, var_ready, std_ready, rstd_ready = [
            S.sem(n) for n in ("stats_done", "var_ready", "std_ready", "rstd_ready")]

        with nc.Block() as block:

            @block.sync
            def _(sp):
                def load(j, par, g):
                    row = sp.snap(T.first_row(g)) if not isinstance(g, int) else T.first_row(g)
                    sp.wait_ge(y_ready[par], j)
                    sp.dma_start(xin[:, par, :, :],
                                 T.x[bass.ds(row, GROUP), :].rearrange("(p t) d -> p t d", t=TG)) \
                        .then_inc(x_ready[par], 16)
                in_pairs(sp, T.NG, load)

            @block.vector
            def _(dve):
                def normalise(j, par, g):
                    dve.wait_ge(x_ready[par], 16 * (j + 1))
                    for t in range(TG):
                        last = dve.bn_stats(stats[:, t, :], xin[:, par, t, :])
                    last.then_inc(stats_done, 1)
                    dve.wait_ge(stats_done, g + 1)
                    alone(dve, passed)
                    for t in range(TG):
                        last = dve.bn_aggr(mv[:, t, :], stats[:, t, :])
                    last.then_inc(var_ready, 1)
                    dve.wait_ge(var_ready, g + 1)
                    dve.wait_ge(std_ready, g + 1)
                    dve.reciprocal(rstd[:, :, :], std[:, :, :]).then_inc(rstd_ready, 1)
                    dve.wait_ge(rstd_ready, g + 1)
                    dve.wait_ge(turned[par], KD * j)
                    for t in range(TG):
                        last = dve.tensor_scalar(xl[:, par, t, :], xin[:, par, t, :], mv[:, t, 0:1], rstd[:, t, :],
                                                 ALU.subtract, ALU.mult)
                    last.then_inc(y_ready[par], 1)
                in_pairs(dve, T.NG, normalise)

            @block.tensor
            def _(pe):
                def turn(j, par, g):
                    pe.wait_ge(y_ready[par], j + 1)
                    pe.wait_ge(bank_copied[par], KD * j)
                    for k in range(KD):
                        for t in range(TG):
                            last = pe.transpose(ps[:, 2 * par + k, t * P:(t + 1) * P],
                                                xl[:, par, t, k * P:(k + 1) * P], T.ident[:, :])
                        last.then_inc(turned[par], 1)
                in_pairs(pe, T.NG, turn)

            @block.scalar
            def _(act):
                def copy_out(j, par, g):
                    act.wait_ge(var_ready, g + 1)
                    act.activation(std[:, :, :], mv[:, :, 1:2], ACT.Sqrt, bias=T.eps_ln[:, :]).then_inc(std_ready, 1)
                    for k in range(KD):
                        act.wait_ge(turned[par], KD * j + k + 1)
                        act.copy(T.xt[:, k, bass.ds(T.first_row(g), GROUP)].rearrange("f (p t) -> f t p", t=TG),
                                 ps[:, 2 * par + k, :].rearrange("f (t p) -> f t p", t=TG)) \
                            .then_inc(bank_copied[par], 1)
                in_pairs(act, T.NG, copy_out)


def stage_edges(nc, T):
    B = T.EDGE_BLOCKS
    full = T.E // P // P
    whole = T.E // P - full * P
    rest = T.E - (full * P + whole) * P
    assert full == B - 1 and 0 < rest < P and whole < P - 1
    with Stage(nc) as S:
        srci, dsti = S.sb("edge_src_i", [P, B, P], I32), S.sb("edge_dst_i", [P, B, P], I32)
        fields = S.sb("edge_fields", [P, 4, B, P])
        least, base = S.sb("edge_least", [P, B]), S.sb("edge_base", [P, B])
        most = S.sb("edge_most", [P, 2])
        base_t = S.sb("edge_base_t", [B, P], I32)
        flag_f = S.sb("flag_f", [1, 2])
        ps = S.ps("ps_edges", [P, 2, 4, P])
        ps_small = S.ps("ps_small", [P, GROUP])
        padded, loaded, filled, step, turned, copied, base_ready, base_stored, base_loaded, small = [
            S.sem(n) for n in ("edge_padded", "edge_loaded", "edge_filled", "edge_step", "edge_turned", "edge_copied",
                               "base_ready", "base_stored", "base_loaded", "small_turned")]

        def blocks_of(a):
            return a[0:full * P * P].rearrange("(b c e) -> c b e", c=P, e=P)

        def rows_of(a):
            return a[full * P * P:(full * P + whole) * P].rearrange("(c e) -> c e", e=P)

        def tail_of(a):
            return a[T.E - rest:T.E].rearrange("(a e) -> a e", a=1)

        with nc.Block() as block:

            @block.sync
            def _(sp):
                sp.wait_ge(padded, 3)
                for dst, a in ((srci, T.src), (dsti, T.dst), (fields[:, WGT], T.ew)):
                    sp.dma_start(dst[:, 0:full, :], blocks_of(a)).then_inc(loaded, 16)
                    sp.dma_start(dst[0:whole, full, :], rows_of(a)).then_inc(loaded, 16)
                    sp.dma_start(dst[whole:whole + 1, full, 0:rest], tail_of(a)).then_inc(loaded, 16)
                sp.dma_start(dsti[whole:whole + 1, full, rest:P],
                             T.dst[T.E - (P - rest):T.E].rearrange("(a e) -> a e", a=1)).then_inc(loaded, 16)
                sp.wait_ge(base_ready, 1)
                sp.dma_start(T.base_dram.rearrange("(b c) -> b c", c=P), base_t[:, :]).then_inc(base_stored, 16)
                sp.wait_ge(base_stored, 16)
                sp.dma_start(T.base_row[:, :], T.base_dram.rearrange("(a c) -> a c", a=1)).then_inc(base_loaded, 16)
                sp.wait_ge(base_loaded, 16)

            @block.vector
            def _(dve):
                dve.memset(srci[:, full, :], T.N).then_inc(padded, 1)
                dve.memset(dsti[:, full, :], 0).then_inc(padded, 1)
                dve.memset(fields[:, WGT, full, :], 0.0).then_inc(padded, 1)
                dve.wait_ge(padded, 3)
                dve.wait_ge(loaded, 160)
                dve.tensor_scalar(fields[:, SRC], srci[:, :, :], T.N, None, ALU.min).then_inc(step, 1)
                dve.tensor_scalar(fields[:, DST], dsti[:, :, :], BANDS * T.N - 1, None, ALU.min).then_inc(step, 1)
                dve.wait_ge(step, 2)
                dve.tensor_reduce(least[:, :], fields[:, DST], AX, ALU.min).then_inc(step, 1)
                dve.wait_ge(step, 3)
                dve.tensor_scalar(base[:, :], least[:, :], BANDS * T.N - WIN, None, ALU.min).then_inc(step, 1)
                dve.wait_ge(step, 4)
                dve.tensor_tensor(fields[:, REL], fields[:, DST],
                                  base[:, :].rearrange("p (b a) -> p b a", a=1).to_broadcast([P, B, P]),
                                  ALU.subtract).then_inc(step, 1)
                dve.wait_ge(step, 5)
                for i, f in enumerate((DST, REL)):
                    dve.tensor_reduce(most[:, i:i + 1], fields[:, f].rearrange("p b e -> p (b e)"), AX, ALU.max) \
                        .then_inc(filled, 1)
                dve.wait_ge(small, 3)
                dve.tensor_copy(base_t[:, :], ps_small[0:B, 0:P]).then_inc(base_ready, 1)
                for i in range(2):
                    dve.tensor_reduce(flag_f[:, i:i + 1], ps_small[0:1, (i + 1) * P:(i + 2) * P], AX, ALU.max) \
                        .then_inc(step, 1)
                dve.wait_ge(step, 7)
                dve.tensor_scalar(T.flags[:, 0:1], flag_f[:, 0:1], T.N, None, ALU.is_ge).then_inc(step, 1)
                dve.tensor_scalar(T.flags[:, 1:2], flag_f[:, 1:2], WIN, None, ALU.is_ge).then_inc(step, 1)
                dve.wait_ge(step, 9)

            @block.tensor
            def _(pe):
                pe.wait_ge(filled, 2)
                pe.transpose(ps_small[0:B, 0:P], base[:, :], T.ident[:, :]).then_inc(small, 1)
                for i in range(2):
                    pe.transpose(ps_small[0:1, (i + 1) * P:(i + 2) * P], most[:, i:i + 1], T.ident[:, :]) \
                        .then_inc(small, 1)
                for b in range(B):
                    if b >= 2:
                        pe.wait_ge(copied, b - 1)
                    for f in range(4):
                        last = pe.transpose(ps[:, b % 2, f, :], fields[:, f, b, :], T.ident[:, :])
                    last.then_inc(turned, 1)

            @block.scalar
            def _(act):
                n = P // HALF
                for b in range(B):
                    act.wait_ge(turned, b + 1)
                    act.copy(T.edges[:, b * n:(b + 1) * n, :, :].rearrange("p q f i -> p f q i"),
                             ps[:, b % 2, :, :].rearrange("p f (q i) -> p f q i", i=HALF)).then_inc(copied, 1)


def stage_stats(nc, T):
    NS = 25
    W = T.N // NS
    assert NS * W == T.N and W <= 512
    with Stage(nc) as S:
        stats = S.sb("bn_stats", [P, KD, NS, 6])
        mv = S.sb("bn_mv", [P, KD, 2])
        std, tmp = S.sb("bn_std", [P, KD, 1]), S.sb("bn_tmp", [P, KD, 1])
        step, std_ready = S.sem("bn_step"), S.sem("bn_std_ready")
        with nc.Block() as block:

            @block.vector
            def _(dve):
                for k in range(KD):
                    for n in range(NS):
                        last = dve.bn_stats(stats[:, k, n, :], T.xt[:, k, n * W:(n + 1) * W])
                last.then_inc(step, 1)
                dve.wait_ge(step, 1)
                for k in range(KD):
                    last = dve.bn_aggr(mv[:, k, :], stats[:, k, :, :])
                last.then_inc(step, 1)
                dve.wait_ge(step, 2)
                dve.wait_ge(std_ready, 1)
                dve.reciprocal(tmp[:, :, :], std[:, :, :]).then_inc(step, 1)
                dve.wait_ge(step, 3)
                dve.tensor_tensor(T.bn_scale[:, :], T.gam[:, :], tmp[:, :, 0], ALU.mult).then_inc(step, 1)
                dve.wait_ge(step, 4)
                dve.tensor_tensor(tmp[:, :, 0], mv[:, :, 0], T.bn_scale[:, :], ALU.mult).then_inc(step, 1)
                dve.wait_ge(step, 5)
                dve.tensor_tensor(T.bn_shift[:, :], T.bet[:, :], tmp[:, :, 0], ALU.subtract).then_inc(step, 1)
                dve.wait_ge(step, 6)
                dve.tensor_scalar(T.bn_neg[:, 0:KD], T.bn_scale[:, :], -1.0, None, ALU.mult).then_inc(step, 1)
                dve.tensor_scalar(T.bn_neg[:, KD:2 * KD], T.bn_shift[:, :], -1.0, None, ALU.mult).then_inc(step, 1)
                dve.wait_ge(step, 8)

            @block.scalar
            def _(act):
                act.wait_ge(step, 2)
                act.activation(std[:, :, :], mv[:, :, 1:2], ACT.Sqrt, bias=T.eps_ln[:, :]).then_inc(std_ready, 1)


def stage_table(nc, T, extra):
    tag = "x_" if extra else ""
    NTG = T.N // TGROUP
    assert NTG * TGROUP == T.N and NTG % 2 == 1
    per = [NTG // 2 + 1, NTG // 2]
    with Stage(nc) as S:
        pos = S.sb(tag + "elu_pos", [P, 2, KD, TGROUP])
        neg = S.sb(tag + "elu_neg", [P, 2, KD, TGROUP])
        xe = S.sb(tag + "elu", [P, 2, KD, TGROUP])
        rows = S.sb(tag + "table_rows", [P, 2, 4, D])
        ps = S.ps(tag + "ps_table", [P, 4, GROUP])
        neg_ready, parts_ready, elu_ready, products, bank_read, rows_ready, stored = [
            S.sems(tag + n, 2) for n in ("neg_ready", "parts_ready", "elu_ready", "products", "bank_read",
                                         "rows_ready", "rows_stored")]

        def bands(eng, run):
            if not extra:
                run(0, (0, 0))
                return
            flag = eng.value_load(T.flags[0:1, 0:1], min_val=0, max_val=1)
            with eng.If(flag):
                with eng.Fori(1, BANDS) as band:
                    run(band, [(band - 1) * per[0], (band - 1) * per[1]])

        with nc.Block() as block:

            @block.scalar
            def _(act):
                def run(band, before):
                    def parts(j, par, g):
                        turn = before[par] + j
                        cols = bass.ds(g * TGROUP, TGROUP)
                        act.wait_ge(elu_ready[par], turn)
                        for k in range(KD):
                            last = act.activation(neg[:, par, k, :], T.xt[:, k, cols], ACT.Relu,
                                                  bias=T.bn_neg[:, KD + k:KD + k + 1], scale=T.bn_neg[:, k:k + 1])
                        last.then_inc(neg_ready[par], 1)
                        for k in range(KD):
                            act.activation(pos[:, par, k, :], T.xt[:, k, cols], ACT.Relu,
                                           bias=T.bn_shift[:, k:k + 1], scale=T.bn_scale[:, k:k + 1])
                        act.wait_ge(neg_ready[par], turn + 1)
                        act.activation(neg[:, par, :, :], neg[:, par, :, :], ACT.Exp, scale=-1.0) \
                            .then_inc(parts_ready[par], 1)
                    in_pairs(act, NTG, parts)
                bands(act, run)

            @block.vector
            def _(dve):
                def run(band, before):
                    bias = T.bias_bc[:, bass.ds(band * D, D)] if extra else T.bias_bc[:, 0:D]

                    def combine(j, par):
                        turn = before[par] + j
                        dve.wait_ge(parts_ready[par], turn + 1)
                        dve.wait_ge(products[par], 2 * turn)
                        dve.scalar_tensor_tensor(out=xe[:, par, :, :], in0=neg[:, par, :, :], scalar=-1.0,
                                                 in1=pos[:, par, :, :], op0=ALU.add, op1=ALU.add) \
                            .then_inc(elu_ready[par], 1)

                    def add_bias(j, par):
                        turn = before[par] + j
                        dve.wait_ge(stored[par], 16 * turn)
                        for i in range(2):
                            dve.wait_ge(products[par], 2 * turn + i + 1)
                            for t in (2 * i, 2 * i + 1):
                                last = dve.tensor_tensor(rows[0:TW, par, t, :],
                                                         ps[0:TW, 2 * par + i, (t % 2) * D:(t % 2 + 1) * D],
                                                         bias[0:TW, :], ALU.add)
                            last.then_inc(bank_read[par], 1)

                    combine(0, 0)
                    with dve.Fori(0, NTG // 2) as j:
                        combine(j, 1)
                        add_bias(j, 0)
                        combine(j + 1, 0)
                        add_bias(j, 1)
                    add_bias(NTG // 2, 0)
                bands(dve, run)

            @block.tensor
            def _(pe):
                def run(band, before):
                    def multiply(j, par, g):
                        turn = before[par] + j
                        pe.wait_ge(elu_ready[par], turn + 1)
                        pe.wait_ge(bank_read[par], 2 * turn)
                        for i in range(2):
                            for t in (2 * i, 2 * i + 1):
                                for k in range(KD):
                                    w = T.wt[:, k, bass.ds(band * D, D)] if extra else T.wt[:, k, 0:D]
                                    last = pe.matmul(ps[0:TW, 2 * par + i, (t % 2) * D:(t % 2 + 1) * D],
                                                     xe[:, par, k, t * TW:(t + 1) * TW], w,
                                                     start=(k == 0), stop=(k == KD - 1))
                            last.then_inc(products[par], 1)
                    in_pairs(pe, NTG, multiply)
                bands(pe, run)

            @block.sync
            def _(sp):
                def run(band, before):
                    def store(j, par, g):
                        turn = before[par] + j
                        row = band * T.N + g * TGROUP
                        if not isinstance(row, int):
                            row = sp.snap(row)
                        sp.wait_ge(bank_read[par], 2 * (turn + 1))
                        sp.dma_start(T.table[bass.ds(row, TGROUP), :].rearrange("(t p) d -> p t d", p=TW),
                                     rows[0:TW, par, :, :]).then_inc(stored[par], 16)
                    in_pairs(sp, NTG, store)
                bands(sp, run)
                if not extra:
                    for par in range(2):
                        sp.wait_ge(stored[par], 16 * per[par])

            if extra:
                @block.gpsimd
                def _(pool):
                    flag = pool.value_load(T.flags[0:1, 0:1], min_val=0, max_val=1)
                    with pool.If(flag):
                        for par in range(2):
                            pool.wait_ge(stored[par], 16 * per[par] * (BANDS - 1))


def stage_weights(nc, T):
    EX = T.EX
    R = EX * KD
    mats = ((T.W1, T.w1), (T.W2, T.w2), (T.Wo, T.wo))
    vecs = T.vec_inputs
    with Stage(nc) as S:
        raw = S.sb("w_raw", [P, 2, EX, D])
        v = S.sb("vectors", [R, 10, P])
        sc = S.sb("vec_scale", [R, 2, P])
        sh = S.sb("vec_shift", [R, 2, P])
        wr = S.sb("wr_raw", [P, KD, EX])
        ps = S.ps("ps_vec", [P, 4, R])
        w_loaded = S.sems("we_loaded", 2)
        hi_ready, lo_ready, v_loaded, step, std_ready, turned, wr_loaded = [
            S.sem(n) for n in ("hi_ready", "lo_ready", "vec_loaded", "vec_step", "vec_std", "vec_turned", "wr_loaded")]
        with nc.Block() as block:

            @block.sync
            def _(sp):
                for i, a in enumerate(vecs):
                    sp.dma_start(v[:, i, :], a.rearrange("e (k p) -> (e k) p", p=P)).then_inc(v_loaded, 16)
                with nc.allow_non_contiguous_dma(reason="gate weights, small"):
                    sp.dma_start(wr[:, :, :], T.Wr.rearrange("(k p) e -> p k e", p=P)).then_inc(wr_loaded, 16)
                sp.dma_start(T.br_bc[:, :], T.br.rearrange("(a n) -> a n", a=1).to_broadcast([P, EX])) \
                    .then_inc(wr_loaded, 16)
                sp.dma_start(T.bo_sb[:, :], T.bo).then_inc(wr_loaded, 16)
                n = 0
                for a, _ in mats:
                    for k in range(KD):
                        if n >= 2:
                            sp.wait_ge(lo_ready, n - 1)
                        sp.dma_start(raw[:, n % 2, :, :], a[:, k * P:(k + 1) * P, :].rearrange("e p h -> p e h")) \
                            .then_inc(w_loaded[n % 2], 16)
                        n += 1

            @block.vector
            def _(dve):
                n = 0
                for _, (hi, lo) in mats:
                    for k in range(KD):
                        dve.wait_ge(hi_ready, n + 1)
                        dve.tensor_tensor(lo[:, k, :, :], raw[:, n % 2, :, :], hi[:, k, :, :].bitcast(F32),
                                          ALU.subtract).then_inc(lo_ready, 1)
                        n += 1
                dve.wait_ge(hi_ready, n + 1)
                dve.tensor_tensor(T.wr[1][:, :, :], wr[:, :, :], T.wr[0][:, :, :].bitcast(F32), ALU.subtract) \
                    .then_inc(lo_ready, 1)
                dve.wait_ge(std_ready, 1)
                dve.reciprocal(sh[:, :, :], sc[:, :, :]).then_inc(step, 1)
                dve.wait_ge(step, 1)
                for i in range(2):
                    dve.tensor_tensor(sc[:, i, :], v[:, 5 * i + 1, :], sh[:, i, :], ALU.mult).then_inc(step, 1)
                dve.wait_ge(step, 3)
                for i in range(2):
                    dve.tensor_tensor(sh[:, i, :], v[:, 5 * i, :], v[:, 5 * i + 3, :], ALU.subtract).then_inc(step, 1)
                dve.wait_ge(step, 5)
                for i in range(2):
                    dve.tensor_tensor(sh[:, i, :], sh[:, i, :], sc[:, i, :], ALU.mult).then_inc(step, 1)
                dve.wait_ge(step, 7)
                for i in range(2):
                    dve.tensor_tensor(sh[:, i, :], sh[:, i, :], v[:, 5 * i + 2, :], ALU.add).then_inc(step, 1)
                dve.wait_ge(step, 9)
                dve.wait_ge(turned, 1)
                dve.tensor_copy(T.vec_cols[:, :, :], ps[:, :, :]).then_inc(step, 1)
                dve.wait_ge(step, 10)

            @block.scalar
            def _(act):
                n = 0
                for _, (hi, _) in mats:
                    for k in range(KD):
                        act.wait_ge(w_loaded[n % 2], 16 * (n // 2 + 1))
                        act.copy(hi[:, k, :, :], raw[:, n % 2, :, :]).then_inc(hi_ready, 1)
                        n += 1
                act.wait_ge(wr_loaded, 48)
                act.copy(T.wr[0][:, :, :], wr[:, :, :]).then_inc(hi_ready, 1)
                act.wait_ge(v_loaded, 160)
                for i in range(2):
                    last = act.activation(sc[:, i, :], v[:, 5 * i + 4, :], ACT.Sqrt, bias=T.eps_ffn[0:R, :])
                last.then_inc(std_ready, 1)

            @block.tensor
            def _(pe):
                pe.wait_ge(step, 9)
                for i in range(2):
                    pe.transpose(ps[:, 2 * i, :], sc[:, i, :], T.ident[0:R, 0:R])
                    last = pe.transpose(ps[:, 2 * i + 1, :], sh[:, i, :], T.ident[0:R, 0:R])
                last.then_inc(turned, 1)


def stage_messages(nc, T):
    ROUNDS = T.CHUNKS // UN
    NH = UN // HALF
    with Stage(nc) as S:
        edge = S.sb("edge_cols", [P, NH, 4, HALF])
        same = S.sb("same_target", [P, UN, P])
        select = S.sb("select", [P, UN, WIN])
        spread = S.sb("spread", [WIN, UN, P])
        win = S.sb("window", [WIN, UN, D])
        gathered = S.sb("gathered", [P, UN, D])
        sums = S.sb("chunk_sums", [P, UN, D])
        scratch = S.sb("earlier_scratch", [P, 2, P])
        earlier = S.sb("earlier_same", [P, NH, HALF])
        away = S.sb("away", [P, NH, HALF])
        target = S.sb("target_row", [P, NH, HALF], I32)
        rowi = S.sb("table_row_i", [P, NH, HALF], I32)
        ps_src = S.ps("ps_src", [P, 2, GROUP])
        ps_spread = S.ps("ps_spread", [P, 2, GROUP])
        ps_sum = S.ps("ps_sum", [P, 2, GROUP])

        def run(S, tag, windows):
            edge_ready, target_ready, rowi_ready, earlier_ready, away_ready = [
                S.sems(tag + n, NH) for n in ("edge_ready", "target_ready", "rowi_ready", "earlier_ready", "away_ready")]
            src_ready, src_read, spread_ready, sum_copied = [
                S.sems(tag + n, 2) for n in ("src_ready", "src_read", "spread_copied", "sum_copied")]
            rows_ready, select_ready, spread_done, sum_ready, added = [
                S.sems(tag + n, UN) for n in ("rows_ready", "select_ready", "spread_done", "sum_ready", "added")]

            passed = S.sem(tag + "passed")

            def slots():
                for u in range(UN):
                    yield u, u // HALF, u % HALF, u % 2, u // 2

            def sync(sp):
                if not windows:
                    return
                with sp.Fori(0, ROUNDS) as r:
                    for u, h, i, bank, n in slots():
                        row = sp.value_load(T.base_row[0:1, bass.ds(r * UN + u, 1)], min_val=0,
                                            max_val=BANDS * T.N - WIN)
                        sp.wait_ge(sum_ready[u], r)
                        sp.dma_start(win[:, u, :], T.table[bass.ds(row, WIN), :]).then_inc(rows_ready[u], 16)

            def scalar(act):
                def fetch(r, h):
                    act.wait_ge(target_ready[h], r)
                    act.copy(edge[:, h, :, :], T.edges[:, NH * r + h, :, :]).then_inc(edge_ready[h], 1)

                def spread_out(r, u, bank, n):
                    act.wait_ge(spread_done[u], r + 1)
                    act.copy(spread[:, u, :], ps_spread[0:WIN, bank, 0:P]).then_inc(spread_ready[bank], 1)

                def sum_out(r, u, bank, n):
                    act.wait_ge(sum_ready[u], r + 1)
                    act.wait_ge(added[u], 16 * r)
                    act.copy(sums[:, u, :], ps_sum[:, bank, 0:D]).then_inc(sum_copied[bank], 1)

                with act.Fori(0, ROUNDS) as r:
                    for h in range(NH):
                        fetch(r, h)
                    every = list(slots())
                    for u, h, i, bank, n in every:
                        if windows:
                            spread_out(r, u, bank, n)
                            if u >= 1:
                                sum_out(r, u - 1, *every[u - 1][3:])
                        else:
                            sum_out(r, u, bank, n)
                    if windows:
                        sum_out(r, UN - 1, *every[-1][3:])

            def tensor(pe):
                def bring_src(r, u, h, i, bank, n):
                    if i == 0:
                        pe.wait_ge(edge_ready[h], r + 1)
                    pe.wait_ge(src_read[bank], 4 * r + n)
                    pe.matmul(ps_src[:, bank, 0:P], edge[:, h, SRC, i:i + 1].to_broadcast([P, P]), T.ident[:, :],
                              start=True, stop=True).then_inc(src_ready[bank], 1)

                def spread_rows(r, u, bank, n):
                    pe.wait_ge(select_ready[u], r + 1)
                    pe.wait_ge(spread_ready[bank], 4 * r + n)
                    pe.matmul(ps_spread[0:WIN, bank, 0:P], select[:, u, :], same[:, u, :], start=True, stop=True) \
                        .then_inc(spread_done[u], 1)

                def sum_rows(r, u, bank, n):
                    pe.wait_ge(sum_copied[bank], 4 * r + n)
                    pe.wait_ge(rows_ready[u], 16 * (r + 1))
                    if windows:
                        pe.wait_ge(spread_ready[bank], 4 * r + n + 1)
                        mm = pe.matmul(ps_sum[:, bank, 0:D], spread[:, u, :], win[:, u, :], start=True, stop=True)
                    else:
                        pe.wait_ge(select_ready[u], r + 1)
                        mm = pe.matmul(ps_sum[:, bank, 0:D], same[:, u, :], gathered[:, u, :], start=True, stop=True)
                    mm.then_inc(sum_ready[u], 1)

                with pe.Fori(0, ROUNDS) as r:
                    every = list(slots())
                    for u in range(UN + 2):
                        if u < UN:
                            bring_src(r, *every[u])
                        if windows and 1 <= u <= UN:
                            spread_rows(r, u - 1, *every[u - 1][3:])
                        if u >= 2:
                            sum_rows(r, u - 2, *every[u - 2][3:])

            def vector(dve):
                with dve.Fori(0, ROUNDS) as r:
                    for u, h, i, bank, n in slots():
                        def col(f):
                            return edge[:, h, f, i:i + 1]
                        if i == 0:
                            dve.wait_ge(edge_ready[h], r + 1)
                            if not windows:
                                for k in range(HALF):
                                    dve.wait_ge(rows_ready[HALF * h + k], 16 * r)
                                dve.tensor_copy(rowi[:, h, :], edge[:, h, DST, :]).then_inc(rowi_ready[h], 1)
                        dve.wait_ge(src_ready[bank], 4 * r + n + 1)
                        if windows:
                            dve.wait_ge(spread_done[u], r)
                            dve.tensor_scalar(same[:, u, :], ps_src[:, bank, 0:P], col(SRC), None, ALU.is_equal)
                            dve.tensor_scalar(select[:, u, :], T.iota_win[:, :], col(REL), col(WGT), ALU.is_equal,
                                              ALU.mult).then_inc(select_ready[u], 1)
                        else:
                            dve.wait_ge(sum_ready[u], r)
                            dve.tensor_scalar(same[:, u, :], ps_src[:, bank, 0:P], col(SRC), col(WGT), ALU.is_equal,
                                              ALU.mult).then_inc(select_ready[u], 1)
                        dve.scalar_tensor_tensor(out=scratch[:, bank, :], in0=ps_src[:, bank, 0:P], scalar=col(SRC),
                                                 in1=T.before[:, :], op0=ALU.is_equal, op1=ALU.mult,
                                                 accum_out=earlier[:, h, i:i + 1]).then_inc(src_read[bank], 1)
                        if i == HALF - 1:
                            dve.tensor_tensor(away[:, h, :], T.spare[:, :], edge[:, h, SRC, :], ALU.subtract) \
                                .then_inc(away_ready[h], 1)
                            for b in range(2):
                                dve.wait_ge(src_read[b], 4 * r + 2 * (h + 1))
                            dve.tensor_scalar(earlier[:, h, :], earlier[:, h, :], 1.0, None, ALU.min) \
                                .then_inc(earlier_ready[h], 1)
                            dve.wait_ge(earlier_ready[h], r + 1)
                            dve.wait_ge(away_ready[h], 2 * r + 1)
                            dve.tensor_tensor(away[:, h, :], away[:, h, :], earlier[:, h, :], ALU.mult) \
                                .then_inc(away_ready[h], 1)
                            dve.wait_ge(away_ready[h], 2 * r + 2)
                            for k in range(HALF):
                                dve.wait_ge(added[HALF * h + k], 16 * r)
                            dve.tensor_tensor(target[:, h, :], away[:, h, :], edge[:, h, SRC, :], ALU.add) \
                                .then_inc(target_ready[h], 1)

            def gpsimd(pool):
                def gather(r, u, h, i):
                    if i == 0:
                        pool.wait_ge(rowi_ready[h], r + 1)
                    pool.wait_ge(sum_ready[u], r)
                    alone(pool, passed)
                    pool.indirect_dma_start(gathered[:, u, :], None, T.table,
                                            bass.IndirectOffsetOnAxis(ap=rowi[:, h, i:i + 1], axis=0)) \
                        .then_inc(rows_ready[u], 16)

                def add(r, u, h, i, bank, n):
                    if i == 0:
                        pool.wait_ge(target_ready[h], r + 1)
                    pool.wait_ge(sum_copied[bank], 4 * r + n + 1)
                    if u < NACC:
                        pool.wait_ge(added[u + NACC], 16 * r)
                    else:
                        pool.wait_ge(added[u - NACC], 16 * (r + 1))
                    alone(pool, passed)
                    pool.indirect_dma_start(T.acc[u % NACC], bass.IndirectOffsetOnAxis(ap=target[:, h, i:i + 1], axis=0),
                                            sums[:, u, :], None, compute_op=ALU.add).then_inc(added[u], 16)

                with pool.Fori(0, ROUNDS) as r:
                    every = list(slots())
                    if windows:
                        for s in every:
                            add(r, *s)
                    else:
                        for s in range(UN + HALF):
                            if s < UN:
                                gather(r, *every[s][0:3])
                            if s >= HALF:
                                add(r, *every[s - HALF])
                for u in range(UN):
                    pool.wait_ge(added[u], 16 * ROUNDS)

            return sync, scalar, tensor, vector, gpsimd

        one_by_one = run(S, "g_", False)
        by_window = run(S, "w_", True)

        def either(eng, k):
            flag = eng.value_load(T.flags[0:1, 1:2], min_val=0, max_val=1)
            with eng.If(flag):
                one_by_one[k](eng)
            with eng.Else():
                by_window[k](eng)

        with nc.Block() as block:

            @block.sync
            def _(sp):
                either(sp, 0)

            @block.scalar
            def _(act):
                either(act, 1)

            @block.tensor
            def _(pe):
                either(pe, 2)

            @block.vector
            def _(dve):
                either(dve, 3)

            @block.gpsimd
            def _(pool):
                either(pool, 4)


def stage_mixture(nc, T):
    EX, NZ = T.EX, 4
    STEPS = EX + 2
    with Stage(nc) as S:
        y = S.sb("y", [P, 2, TG, D])
        spent = T.edges[:, :, :, :].rearrange("p q f i -> p (q f i)")
        part = spent[:, 0:2 * TG * D].rearrange("p (s t d) -> p s t d", s=2, t=TG)
        act_f = spent[:, 2 * TG * D:2 * TG * D + NZ * GROUP].rearrange("p (z n) -> p z n", z=NZ)
        xl = S.sb("xl", [P, TG, D])
        xhi = S.sb("xl_t_hi", [P, 2, KD, GROUP], F32R)
        xlo = S.sb("xl_t_lo", [P, 2, KD, GROUP], F32R)
        h_hi = [S.sb(f"h{l}_hi", [P, 2, KD, GROUP], F32R) for l in (1, 2)]
        h_lo = [S.sb(f"h{l}_lo", [P, 2, KD, GROUP], F32R) for l in (1, 2)]
        stats, mv = S.sb("m_stats", [P, TG, 6]), S.sb("m_mv", [P, TG, 2])
        std, rstd = S.sb("m_std", [P, TG, 1]), S.sb("m_rstd", [P, TG, 1])
        lg = S.sb("logits", [P, TG, EX])
        red = S.sb("gate_red", [P, 3, TG, 1])
        gate = S.sb("gate", [P, 2, TG, EX])
        gate_t = S.sb("gate_t", [EX, TG, P])
        z = [S.ps(f"z{i}", [P, GROUP]) for i in range(NZ)]
        o = [S.ps(f"o{i}", [P, 2, D]) for i in range(2)]
        tr = S.ps("tr", [P, GROUP])
        misc = S.ps("misc", [P, GROUP])

        x_loaded, y_ready, stored = [S.sems(n, 2) for n in ("mx_loaded", "my_ready", "m_stored")]
        part_loaded, part_added = S.sems("part_loaded", 2), S.sems("part_added", 2)
        z_ready, z_split, lo_ready = [S.sems(n, NZ) for n in ("z_ready", "z_split", "lo_ready")]
        o_ready, o_added = S.sems("o_ready", 2), S.sems("o_added", 2)
        passed = S.sem("m_passed")
        (stats_done, var_ready, std_ready, rstd_ready, xl_ready, tr_ready, tr_hi, tr_read, lg_ready, gate_step, exp_ready,
         gate_ready, gate_turned, gate_t_ready, bo_ready, bo_added, l2_done, l3_done) = [
            S.sem("m_" + n) for n in ("stats_done", "var_ready", "std_ready", "rstd_ready", "xl_ready", "tr_ready",
                                      "tr_hi", "tr_read", "lg_ready", "gate_step", "exp_ready", "gate_ready",
                                      "gate_turned", "gate_t_ready", "bo_ready", "bo_added", "l2_done", "l3_done")]

        def units(s):
            n = max(0, 4 * s - 2) if s > 0 else 0
            found = []
            if s < EX:
                found += [(1, s, m) for m in range(KD)]
            if 1 <= s <= EX:
                found += [(2, s - 1, m) for m in range(KD)]
            return [(n + i, *f) for i, f in enumerate(found)]

        PER = 2 * KD * EX
        TURNS = PER // NZ
        assert [u[0] for s in range(STEPS) for u in units(s)] == list(range(PER))

        def first_count(e, layer):
            return next(u[0] for s in range(STEPS) for u in units(s) if u[1:3] == (layer, e))

        def pipelined(eng, prepare, step):
            for k in range(STEPS):
                prepare(k, 0, 0, 0)
            with eng.Fori(0, T.NG // 2) as j:
                for par in range(2):
                    for s in range(STEPS):
                        step(s, j, par, 2 * j + par)
                        prepare(s, j + par, 1 - par, 2 * j + par + 1)
            for s in range(STEPS):
                step(s, T.NG // 2, 0, T.NG - 1)

        with nc.Block() as block:

            @block.sync
            def _(sp):
                def rows(a, row):
                    return a[bass.ds(row, GROUP), :].rearrange("(p t) d -> p t d", t=TG)

                def load(j, par, g):
                    row = T.first_row(g)
                    if not isinstance(row, int):
                        row = sp.snap(row)
                    sp.wait_ge(stored[par], 16 * j)
                    sp.dma_start(y[:, par, :, :], rows(T.x, row)).then_inc(x_loaded[par], 16)
                    for k in range(NACC):
                        sp.wait_ge(part_added[k % 2], NACC // 2 * g + k // 2)
                        sp.dma_start(part[:, k % 2, :, :], rows(T.acc[k], row)).then_inc(part_loaded[k % 2], 16)

                def store(j, par, g):
                    row = T.first_row(g)
                    if not isinstance(row, int):
                        row = sp.snap(row)
                    for i in range(2):
                        sp.wait_ge(o_added[i], EX * (g + 1))
                    sp.dma_start(rows(T.out, row), y[:, par, :, :]).then_inc(stored[par], 16)

                load(0, 0, 0)
                load(0, 1, 1)
                with sp.Fori(0, T.NG // 2 - 1) as j:
                    for par in range(2):
                        store(j, par, 2 * j + par)
                        load(j + 1, par, 2 * j + par + 2)
                n = T.NG // 2 - 1
                store(n, 0, 2 * n)
                load(n + 1, 0, 2 * n + 2)
                store(n, 1, 2 * n + 1)
                sp.wait_ge(stored[1], 16 * (n + 1))
                store(n + 1, 0, 2 * n + 2)
                sp.wait_ge(stored[0], 16 * (n + 2))

            @block.gpsimd
            def _(pool):
                def add_parts(j, par, g):
                    pool.wait_ge(x_loaded[par], 16 * (j + 1))
                    for k in range(NACC):
                        pool.wait_ge(part_loaded[k % 2], 16 * (NACC // 2 * g + k // 2 + 1))
                        if k:
                            pool.wait_ge(part_added[(k - 1) % 2], NACC // 2 * g + (k - 1) // 2 + 1)
                        pool.tensor_tensor(y[:, par, :, :], y[:, par, :, :], part[:, k % 2, :, :], ALU.add) \
                            .then_inc(part_added[k % 2], 1)
                in_pairs(pool, T.NG, add_parts)

            @block.tensor
            def _(pe):
                def split_products(out, pairs):
                    passes = [(l[a], r[b]) for l, r in pairs for a, b in ((0, 0), (1, 0), (0, 1))]
                    for n, (l, r) in enumerate(passes):
                        last = pe.matmul(out, l, r, start=(n == 0), stop=(n == len(passes) - 1))
                    return last

                def prepare(k, j, par, g):
                    if k in (4, 5):
                        half = k - 4
                        pe.wait_ge(xl_ready, g + 1)
                        if half == 0:
                            pe.wait_ge(bo_added, 2 * g)
                        else:
                            pe.wait_ge(tr_read, 2 * g + 1)
                        for t in range(TG):
                            last = pe.transpose(tr[:, t * P:(t + 1) * P], xl[:, t, half * P:(half + 1) * P],
                                                T.ident[:, :])
                        last.then_inc(tr_ready, 1)
                    if k == 6:
                        pe.wait_ge(tr_read, 2 * g + 2)
                        for t in range(TG):
                            last = split_products(misc[:, t * EX:(t + 1) * EX],
                                                  [([xhi[:, par, q, t * P:(t + 1) * P], xlo[:, par, q, t * P:(t + 1) * P]],
                                                    [T.wr[0][:, q, :], T.wr[1][:, q, :]]) for q in range(KD)])
                        last.then_inc(lg_ready, 1)
                    if k == 8:
                        pe.wait_ge(gate_ready, g + 1)
                        for t in range(TG):
                            last = pe.transpose(misc[0:EX, t * P:(t + 1) * P], gate[:, par, t, :], T.ident[:, :])
                        last.then_inc(gate_turned, 1)
                    if k == 9:
                        pe.wait_ge(gate_t_ready, g + 1)
                        for t in range(TG):
                            bank = tr if t < 2 else misc
                            last = pe.matmul(bank[:, (t % 2) * D:(t % 2 + 1) * D], gate_t[:, t, :], T.bo_sb[:, :],
                                             start=True, stop=True)
                        last.then_inc(bo_ready, 1)

                def step(s, j, par, g):
                    for n, layer, e, m in units(s):
                        b = n % NZ
                        cols = slice(m * P, (m + 1) * P)
                        if layer == 1:
                            w, src = T.w1, (xhi[:, par], xlo[:, par])
                            pe.wait_ge(tr_read, 2 * g + 2)
                        else:
                            w, src = T.w2, (h_hi[0][:, e % 2], h_lo[0][:, e % 2])
                            if m == 0:
                                for q in range(KD):
                                    c = first_count(e, 1) + q
                                    pe.wait_ge(lo_ready[c % NZ], TURNS * g + c // NZ + 1)
                        pe.wait_ge(z_split[b], TURNS * g + n // NZ)
                        last = split_products(z[b][:, :], [([w[0][:, q, e, cols], w[1][:, q, e, cols]],
                                                            [src[0][:, q, :], src[1][:, q, :]]) for q in range(KD)])
                        last.then_inc(z_ready[b], 1)
                    if s >= 2:
                        e = s - 2
                        for q in range(KD):
                            c = first_count(e, 2) + q
                            pe.wait_ge(lo_ready[c % NZ], TURNS * g + c // NZ + 1)
                        for i in range(2):
                            pe.wait_ge(o_added[i], EX * g + e)
                            for t in (2 * i, 2 * i + 1):
                                rows = slice(t * P, (t + 1) * P)
                                last = split_products(o[i][:, t % 2, :],
                                                      [([h_hi[1][:, e % 2, q, rows], h_lo[1][:, e % 2, q, rows]],
                                                        [T.wo[0][:, q, e, :], T.wo[1][:, q, e, :]]) for q in range(KD)])
                            last.then_inc(o_ready[i], 1)
                pipelined(pe, prepare, step)

            @block.scalar
            def _(act):
                def prepare(k, j, par, g):
                    if k == 3:
                        act.wait_ge(var_ready, g + 1)
                        act.activation(std[:, :, :], mv[:, :, 1:2], ACT.Sqrt, bias=T.eps_ln[:, :]).then_inc(std_ready, 1)
                    if k in (4, 5):
                        act.wait_ge(tr_ready, 2 * g + (k - 4) + 1)
                        act.copy(xhi[:, par, k - 4, :], tr[:, :]).then_inc(tr_hi, 1)
                    if k == 7:
                        act.wait_ge(gate_step, 3 * g + 3)
                        act.activation(lg[:, :, :], lg[:, :, :], ACT.Exp).then_inc(exp_ready, 1)
                    if k == 8:
                        act.wait_ge(gate_turned, g + 1)
                        act.copy(gate_t[:, :, :], misc[0:EX, :]).then_inc(gate_t_ready, 1)

                def step(s, j, par, g):
                    for n, layer, e, m in units(s):
                        b = n % NZ
                        col = T.vec_cols[:, 2 * (layer - 1), KD * e + m:KD * e + m + 1]
                        shift = T.vec_cols[:, 2 * (layer - 1) + 1, KD * e + m:KD * e + m + 1]
                        act.wait_ge(z_ready[b], TURNS * g + n // NZ + 1)
                        act.wait_ge(lo_ready[b], TURNS * g + n // NZ)
                        if m == 0:
                            if layer == 1 and e >= 2:
                                for q in range(KD):
                                    c = first_count(e - 2, 2) + q
                                    act.wait_ge(z_ready[c % NZ], TURNS * g + c // NZ + 1)
                            if layer == 2:
                                for i in range(2):
                                    if e >= 2:
                                        act.wait_ge(o_ready[i], EX * g + e - 1)
                                    else:
                                        act.wait_ge(o_ready[i], EX * g)
                            if layer == 1 and e < 2:
                                for c in range(PER - 2 * KD * 1, PER):
                                    act.wait_ge(z_ready[c % NZ], TURNS * g)
                        act.activation(act_f[:, b, :], z[b][:, :], ACT.Relu, bias=shift, scale=col)
                        act.activation(h_hi[layer - 1][:, e % 2, m, :], z[b][:, :], ACT.Relu, bias=shift, scale=col) \
                            .then_inc(z_split[b], 1)
                pipelined(act, prepare, step)

            @block.vector
            def _(dve):
                def prepare(k, j, par, g):
                    if k == 3:
                        for q in range(2):
                            dve.wait_ge(part_added[q], NACC // 2 * (g + 1))
                        for t in range(TG):
                            last = dve.bn_stats(stats[:, t, :], y[:, par, t, :])
                        last.then_inc(stats_done, 1)
                        dve.wait_ge(stats_done, g + 1)
                        alone(dve, passed)
                        for t in range(TG):
                            last = dve.bn_aggr(mv[:, t, :], stats[:, t, :])
                        last.then_inc(var_ready, 1)
                        dve.wait_ge(var_ready, g + 1)
                        dve.wait_ge(std_ready, g + 1)
                        dve.reciprocal(rstd[:, :, :], std[:, :, :]).then_inc(rstd_ready, 1)
                        dve.wait_ge(rstd_ready, g + 1)
                        dve.wait_ge(tr_ready, 2 * g)
                        for t in range(TG):
                            last = dve.tensor_scalar(xl[:, t, :], y[:, par, t, :], mv[:, t, 0:1], rstd[:, t, :],
                                                     ALU.subtract, ALU.mult)
                        last.then_inc(xl_ready, 1)
                    if k in (4, 5):
                        dve.wait_ge(tr_hi, 2 * g + (k - 4) + 1)
                        dve.tensor_tensor(xlo[:, par, k - 4, :], tr[:, :], xhi[:, par, k - 4, :].bitcast(F32),
                                          ALU.subtract).then_inc(tr_read, 1)
                    if k == 6:
                        def bc(i):
                            return red[:, i, :, :].to_broadcast([P, TG, EX])
                        dve.wait_ge(lg_ready, g + 1)
                        dve.tensor_tensor(lg[:, :, :], misc[:, 0:TG * EX].rearrange("p (t e) -> p t e", e=EX),
                                          T.br_bc[:, :].rearrange("p (a e) -> p a e", a=1).to_broadcast([P, TG, EX]),
                                          ALU.add).then_inc(gate_step, 1)
                        dve.wait_ge(gate_step, 3 * g + 1)
                        dve.tensor_reduce(red[:, 0, :, :], lg[:, :, :], AX, ALU.max).then_inc(gate_step, 1)
                        dve.wait_ge(gate_step, 3 * g + 2)
                        dve.tensor_tensor(lg[:, :, :], lg[:, :, :], bc(0), ALU.subtract).then_inc(gate_step, 1)
                    if k == 7:
                        dve.wait_ge(exp_ready, 3 * g + 1)
                        dve.tensor_reduce(red[:, 1, :, :], lg[:, :, :], AX, ALU.add).then_inc(exp_ready, 1)
                        dve.wait_ge(exp_ready, 3 * g + 2)
                        dve.reciprocal(red[:, 2, :, :], red[:, 1, :, :]).then_inc(exp_ready, 1)
                        dve.wait_ge(exp_ready, 3 * g + 3)
                        dve.tensor_tensor(gate[:, par, :, :], lg[:, :, :], red[:, 2, :, :].to_broadcast([P, TG, EX]),
                                          ALU.mult).then_inc(gate_ready, 1)
                    if k == 9:
                        dve.wait_ge(bo_ready, g + 1)
                        for i, bank in enumerate((tr, misc)):
                            dve.tensor_tensor(y[:, par, 2 * i:2 * i + 2, :],
                                              y[:, par, 2 * i:2 * i + 2, :],
                                              bank[:, :].rearrange("p (t d) -> p t d", d=D), ALU.add) \
                                .then_inc(bo_added, 1)

                def step(s, j, par, g):
                    for n, layer, e, m in units(s):
                        b = n % NZ
                        dve.wait_ge(z_split[b], TURNS * g + n // NZ + 1)
                        dve.tensor_tensor(h_lo[layer - 1][:, e % 2, m, :], act_f[:, b, :],
                                          h_hi[layer - 1][:, e % 2, m, :].bitcast(F32), ALU.subtract) \
                            .then_inc(lo_ready[b], 1)
                    if s >= 2:
                        e = s - 2
                        dve.wait_ge(gate_ready, g + 1)
                        dve.wait_ge(bo_added, 2 * g + 2)
                        for i in range(2):
                            dve.wait_ge(o_ready[i], EX * g + e + 1)
                            dve.wait_ge(o_added[i], EX * g + e)
                            for t in (2 * i, 2 * i + 1):
                                last = dve.scalar_tensor_tensor(out=y[:, par, t, :], in0=o[i][:, t % 2, :],
                                                                scalar=gate[:, par, t, e:e + 1],
                                                                in1=y[:, par, t, :], op0=ALU.mult, op1=ALU.add)
                            last.then_inc(o_added[i], 1)
                pipelined(dve, prepare, step)


class Tensors:
    pass


INPUTS = ("x", "src", "dst", "edge_weight", "L0_gnn_bn_gamma", "L0_gnn_bn_beta", "L0_gnn_W", "L0_gnn_b",
          "L0_ffn_Wr", "L0_ffn_br", "L0_ffn_W1", "L0_ffn_b1", "L0_ffn_g1", "L0_ffn_be1", "L0_ffn_m1", "L0_ffn_v1",
          "L0_ffn_W2", "L0_ffn_b2", "L0_ffn_g2", "L0_ffn_be2", "L0_ffn_m2", "L0_ffn_v2", "L0_ffn_Wo", "L0_ffn_bo")


def gnn_and_mixture(nc, a, out):
    T = Tensors()
    T.x, T.src, T.dst, T.ew, T.gamma, T.beta, T.W, T.b = [a[n] for n in INPUTS[:8]]
    T.Wr, T.br, T.W1, T.W2, T.Wo, T.bo = [a["L0_ffn_" + n] for n in ("Wr", "br", "W1", "W2", "Wo", "bo")]
    T.vec_inputs = [a["L0_ffn_" + n] for n in ("b1", "g1", "be1", "m1", "v1", "b2", "g2", "be2", "m2", "v2")]
    T.out = out
    T.N, T.E, T.EX = T.x.shape[0], T.src.shape[0], T.Wr.shape[1]
    T.OC = T.W.shape[0] // P
    T.NG = (T.N + GROUP - 1) // GROUP
    assert T.NG % 2 == 1 and T.x.shape[1] == D and T.W.shape[0] == BANDS * D
    T.first_row = lambda g: g * GROUP if not isinstance(g, int) else min(g * GROUP, T.N - GROUP)
    T.CHUNKS = -(-T.E // (P * UN)) * UN
    T.EDGE_BLOCKS = -(-T.CHUNKS // P)
    T.ACC_ROWS = T.N + P + (-(T.N + P)) % P

    T.table = nc.dram_tensor("node_table", [BANDS * T.N, D], F32, kind="Internal").ap()
    T.acc = [nc.dram_tensor(f"message_sum{i}", [T.ACC_ROWS, D], F32, kind="Internal").ap() for i in range(NACC)]
    T.base_dram = nc.dram_tensor("window_rows", [T.EDGE_BLOCKS * P], I32, kind="Internal").ap()

    with Stage(nc) as K:
        T.ident, T.before = K.sb("ident", [P, P]), K.sb("before", [P, P])
        T.iota_win, T.spare = K.sb("iota_win", [P, WIN]), K.sb("spare_row", [P, HALF])
        T.eps_ln, T.eps_ffn = K.sb("eps_ln", [P, 1]), K.sb("eps_ffn", [P, 1])
        T.base_row = K.sb("base_row", [1, T.EDGE_BLOCKS * P], I32)
        T.flags = K.sb("flags", [1, 2], I32)
        T.edges = K.sb("edges", [P, T.EDGE_BLOCKS * P // HALF, 4, HALF])
        with Stage(nc) as G:
            T.gam, T.bet = G.sb("gamma", [P, KD]), G.sb("beta", [P, KD])
            T.bn_scale, T.bn_shift, T.bn_neg = G.sb("bn_scale", [P, KD]), G.sb("bn_shift", [P, KD]), G.sb("bn_neg", [P, 2 * KD])
            T.bias_bc = G.sb("bias_bc", [P, BANDS * D])
            T.wt = G.sb("w_turned", [P, KD, BANDS * D])
            stage_setup(nc, T)
            stage_edges(nc, T)
            T.xt = G.sb("xt", [P, KD, T.N])
            stage_norm(nc, T)
            stage_stats(nc, T)
            stage_table(nc, T, False)
            stage_table(nc, T, True)
        T.w1, T.w2, T.wo = [[K.sb(f"{n}_{h}", [P, KD, T.EX, D], F32R) for h in ("hi", "lo")] for n in ("w1", "w2", "wo")]
        T.wr = [K.sb(f"wr_{h}", [P, KD, T.EX], F32R) for h in ("hi", "lo")]
        T.br_bc, T.bo_sb = K.sb("br_bc", [P, T.EX]), K.sb("bo_sb", [T.EX, D])
        T.vec_cols = K.sb("vec_cols", [P, 4, T.EX * KD])
        stage_weights(nc, T)
        stage_messages(nc, T)
        stage_mixture(nc, T)


def kernel(**inputs):
    import numpy as _np
    import concourse.bacc as _bacc
    from concourse import mybir as _mybir
    from concourse.bass_utils import run_bass_kernel_spmd as _run

    nc = _bacc.Bacc("TRN2", target_bir_lowering=False, num_devices=1)
    arrays, args = {}, {}
    for name in INPUTS:
        v = _np.ascontiguousarray(inputs[name])
        arrays[f"in_{name}_dram"] = v
        args[name] = nc.dram_tensor(f"in_{name}_dram", v.shape, _mybir.dt.from_np(v.dtype), kind="ExternalInput").ap()
    out = nc.dram_tensor("out_0_dram", inputs["x"].shape, F32, kind="ExternalOutput").ap()
    gnn_and_mixture(nc, args, out)
    r = _run(nc, [arrays], core_ids=[0])
    return r.results[0]["out_0_dram"]
```

```python
from contextlib import ExitStack

import concourse.bass as bass
from concourse import mybir

F32 = mybir.dt.float32
F32R = mybir.dt.float32r
I32 = mybir.dt.int32
U16 = mybir.dt.uint16
ALU = mybir.AluOpType
ACT = mybir.ActivationFunctionType
AX = mybir.AxisListType.X

P = 128
D = 256
KD = D // P
GROUP = 512
TG = GROUP // P
LN_EPS = 1e-5
GNN_EPS = 1e-5
FFN_EPS = 1e-3
NACC = 4
UN = 8
HALF = 4
WIN = 64
PAIR = 2
BANDS = 4
SRC, WGT, DST = range(3)
FIELDS = 3


def wait_turns(eng, sem, n):
    if not isinstance(n, int) or n > 0:
        eng.wait_ge(sem, n)


def in_pairs(eng, n, body):
    for par in range(2):
        body(0, par, par)
    with eng.Fori(1, n // 2) as j:
        for par in range(2):
            body(j, par, 2 * j + par)
    body(n // 2, 0, n - 1)


def alone(eng, passed):
    eng.sem_inc(passed, 1)


class Stage:

    def __init__(self, nc):
        self.nc = nc
        self.ctx = ExitStack()
        self.semaphores = []

    def __enter__(self):
        self.ctx.__enter__()
        return self

    def __exit__(self, *a):
        if self.semaphores:
            self.nc.clear_and_free_semaphores(self.semaphores)
            self.nc.all_engine_barrier()
        return self.ctx.__exit__(*a)

    def sb(self, name, shape, dt=F32):
        return self.ctx.enter_context(self.nc.sbuf_tensor(name, shape, dt))

    def ps(self, name, shape):
        return self.ctx.enter_context(self.nc.psum_tensor(name, shape, F32))

    def sem(self, name):
        self.semaphores.append(self.nc.alloc_semaphore(name=name))
        return self.semaphores[-1]

    def sems(self, name, n):
        return [self.sem(f"{name}{i}") for i in range(n)]


def stage_setup(nc, T):
    with Stage(nc) as S:
        wl = S.sb("w_rows", [P, T.OC, D])
        ones = S.sb("ones_sq", [P, P])
        ps = S.ps("ps_w", [P, 2, GROUP])
        vectors_loaded, w_loaded, zeroed, ones_set, consts, ident_ready, zero_stored, turned, copied = [
            S.sem(n) for n in ("vectors_loaded", "w_loaded", "zeroed", "ones_set", "consts", "ident_ready",
                               "zero_stored", "turned", "copied")]
        with nc.Block() as block:

            @block.sync
            def _(sp):
                sp.dma_start(wl[:, :, :], T.W.rearrange("(o p) d -> p o d", p=P)).then_inc(w_loaded, 16)
                with nc.allow_non_contiguous_dma(reason="two vectors of 256 as columns"):
                    sp.dma_start(T.gam[:, :], T.gamma.rearrange("(k p) -> p k", p=P)).then_inc(vectors_loaded, 16)
                    sp.dma_start(T.bet[:, :], T.beta.rearrange("(k p) -> p k", p=P)).then_inc(vectors_loaded, 16)
                sp.dma_start(T.bias_bc[:, :], T.b.rearrange("(a n) -> a n", a=1).to_broadcast([P, BANDS * D])) \
                    .then_inc(vectors_loaded, 16)
                sp.wait_ge(zeroed, 1)
                sp.dma_start(T.table[T.N:T.N + WIN, :], T.zeros[0:WIN, 0:2 * D]).then_inc(zero_stored, 16)
                sp.dma_start(T.acc[0][T.N:T.N + P, :], T.zeros[:, 0:D]).then_inc(zero_stored, 16)
                sp.wait_ge(vectors_loaded, 48)
                sp.wait_ge(zero_stored, 32)

            @block.gpsimd
            def _(pool):
                pool.memset(ones[:, :], 1.0).then_inc(ones_set, 1)
                pool.memset(T.zeros[:, :], 0.0).then_inc(zeroed, 1)
                pool.wait_ge(ones_set, 1)
                pool.affine_select(out=T.ident[:, :], in_=ones[:, :], compare_op=ALU.is_equal, fill=0.0, base=0,
                                   pattern=[[-1, P]], channel_multiplier=1).then_inc(ident_ready, 1)
                pool.wait_ge(ident_ready, 1)
                for i in range(2):
                    if i:
                        pool.wait_ge(consts, i)
                    pool.iota(T.win_row[i * WIN:(i + 1) * WIN, :], [[0, 1]], base=0, channel_multiplier=1,
                              allow_small_or_imprecise_dtypes=True).then_inc(consts, 1)
                pool.wait_ge(consts, 2)
                pool.iota(T.spare[:, :], [[0, HALF]], base=T.N, channel_multiplier=1,
                          allow_small_or_imprecise_dtypes=True).then_inc(consts, 1)
                pool.iota(T.rank[:, :].bitcast(I32), [[0, 1]], base=(127 + 63) << 23, channel_multiplier=-(1 << 23)) \
                    .then_inc(consts, 1)
                pool.iota(T.unrank[:, :].bitcast(I32), [[0, 1]], base=(127 - 63) << 23, channel_multiplier=1 << 23) \
                    .then_inc(consts, 1)
                pool.memset(T.eps_ln[:, :], LN_EPS).then_inc(consts, 1)
                pool.memset(T.eps_ffn[:, :], FFN_EPS).then_inc(consts, 1)
                pool.wait_ge(consts, 7)

            @block.tensor
            def _(pe):
                pe.wait_ge(ident_ready, 1)
                pe.wait_ge(w_loaded, 16)
                for o in range(T.OC):
                    if o >= 2:
                        pe.wait_ge(copied, o - 1)
                    for k in range(KD):
                        last = pe.transpose(ps[:, o % 2, k * P:(k + 1) * P], wl[:, o, k * P:(k + 1) * P],
                                            T.ident[:, :])
                    last.then_inc(turned, 1)

            @block.scalar
            def _(act):
                act.wait_ge(ident_ready, 1)
                act.copy(T.ident_r[:, :], T.ident[:, :])
                for o in range(T.OC):
                    act.wait_ge(turned, o + 1)
                    act.copy(T.wt[:, :, o * P:(o + 1) * P],
                             ps[:, o % 2, 0:D].rearrange("p (k n) -> p k n", k=KD)).then_inc(copied, 1)


def zero_rows(sp, T, acc, row, done):
    sp.dma_start(acc[bass.ds(row, GROUP), :].rearrange("(p t) d -> p (t d)", t=TG), T.zeros[:, :]).then_inc(done, 16)


def stage_norm(nc, T):
    with Stage(nc) as S:
        xin = S.sb("ln_x", [P, 2, TG, D])
        xl = S.sb("ln_y", [P, 2, TG, D])
        stats = S.sb("ln_stats", [P, 2, TG, 6])
        mv = S.sb("ln_mv", [P, 2, TG, 2])
        std = S.sb("ln_std", [P, 2, TG, 1])
        rstd = S.sb("ln_rstd", [P, 2, TG, 1])
        ps = S.ps("ps_ln", [P, 4, GROUP])
        x_ready, x_copied, y_ready, turned, bank_copied, stats_done, var_ready, std_ready, rstd_ready = [
            S.sems(n, 2) for n in ("x_ready", "x_copied", "y_ready", "x_turned", "xt_copied", "stats_done",
                                   "var_ready", "std_ready", "rstd_ready")]
        zero_stored, passed, sp_passed = [S.sem(n) for n in ("n_zero_stored", "n_passed", "n_sp_passed")]

        def group_rows(a, row):
            return a[bass.ds(row, GROUP), :].rearrange("(p t) d -> p t d", t=TG)

        with nc.Block() as block:

            @block.sync
            def _(sp):
                def load(j, par, g):
                    row, zero_row = T.first_row(g), g * GROUP
                    if not isinstance(row, int):
                        row = zero_row = sp.snap(row)
                    wait_turns(sp, y_ready[par], j)
                    alone(sp, sp_passed)
                    wait_turns(sp, x_copied[par], 16 * j)
                    sp.dma_start(xin[:, par, :, :], group_rows(T.x, row)).then_inc(x_ready[par], 16)
                    for acc in T.acc[1:NACC - 1]:
                        zero_rows(sp, T, acc, zero_row, zero_stored)
                in_pairs(sp, T.NG, load)
                sp.wait_ge(zero_stored, 16 * T.NG * (NACC - 2))

            @block.gpsimd
            def _(pool):
                def copy_x(j, par, g):
                    pool.wait_ge(x_ready[par], 16 * (j + 1))
                    if isinstance(g, int) and g == T.NG - 1:
                        pool.wait_ge(x_copied[1 - par], 16 * (T.NG // 2))
                    pool.dma_start(group_rows(T.acc[0], T.first_row(g)), xin[:, par, :, :]).then_inc(x_copied[par], 16)
                in_pairs(pool, T.NG, copy_x)
                for par in range(2):
                    pool.wait_ge(x_copied[par], 16 * (T.NG // 2 + 1 - par))

            @block.vector
            def _(dve):
                def measure(j, par):
                    dve.wait_ge(x_ready[par], 16 * (j + 1))
                    for t in range(TG):
                        last = dve.bn_stats(stats[:, par, t, :], xin[:, par, t, :])
                    last.then_inc(stats_done[par], 1)
                    dve.wait_ge(stats_done[par], j + 1)
                    alone(dve, passed)
                    for t in range(TG):
                        last = dve.bn_aggr(mv[:, par, t, :], stats[:, par, t, :])
                    last.then_inc(var_ready[par], 1)

                def normalise(j, par):
                    dve.wait_ge(std_ready[par], j + 1)
                    dve.reciprocal(rstd[:, par, :, :], std[:, par, :, :]).then_inc(rstd_ready[par], 1)
                    dve.wait_ge(rstd_ready[par], j + 1)
                    wait_turns(dve, turned[par], KD * j)
                    for t in range(TG):
                        last = dve.tensor_scalar(xl[:, par, t, :], xin[:, par, t, :], mv[:, par, t, 0:1],
                                                 rstd[:, par, t, :], ALU.subtract, ALU.mult)
                    last.then_inc(y_ready[par], 1)

                measure(0, 0)
                measure(0, 1)
                normalise(0, 0)
                with dve.Fori(1, T.NG // 2) as j:
                    measure(j, 0)
                    normalise(j - 1, 1)
                    measure(j, 1)
                    normalise(j, 0)
                n = T.NG // 2
                measure(n, 0)
                normalise(n - 1, 1)
                normalise(n, 0)

            @block.tensor
            def _(pe):
                def turn(j, par, g):
                    pe.wait_ge(y_ready[par], j + 1)
                    wait_turns(pe, bank_copied[par], KD * j)
                    for k in range(KD):
                        for t in range(TG):
                            last = pe.transpose(ps[:, 2 * par + k, t * P:(t + 1) * P],
                                                xl[:, par, t, k * P:(k + 1) * P], T.ident[:, :])
                        last.then_inc(turned[par], 1)
                in_pairs(pe, T.NG, turn)

            @block.scalar
            def _(act):
                def root(j, par):
                    act.wait_ge(var_ready[par], j + 1)
                    act.activation(std[:, par, :, :], mv[:, par, :, 1:2], ACT.Sqrt, bias=T.eps_ln[:, :]) \
                        .then_inc(std_ready[par], 1)

                def copy_out(j, par, row):
                    for k in range(KD):
                        act.wait_ge(turned[par], KD * j + k + 1)
                        act.copy(T.xt[:, k, bass.ds(row, GROUP)].rearrange("f (p t) -> f t p", t=TG),
                                 ps[:, 2 * par + k, :].rearrange("f (t p) -> f t p", t=TG)) \
                            .then_inc(bank_copied[par], 1)

                root(0, 0)
                root(0, 1)
                copy_out(0, 0, 0)
                with act.Fori(1, T.NG // 2) as j:
                    root(j, 0)
                    copy_out(j - 1, 1, (2 * j - 1) * GROUP)
                    root(j, 1)
                    copy_out(j, 0, 2 * j * GROUP)
                n = T.NG // 2
                root(n, 0)
                copy_out(n - 1, 1, (2 * n - 1) * GROUP)
                act.wait_ge(bank_copied[1], KD * n)
                copy_out(n, 0, T.N - GROUP)


def stage_edges(nc, T):
    B = T.EDGE_BLOCKS
    L = PAIR * P
    full = T.E // L // P
    whole = T.E // L - full * P
    rest = T.E - (full * P + whole) * L
    assert full == B - 1 and 0 < rest < L and whole < P - 1 and T.N + P < 1 << 15
    with Stage(nc) as S:
        srci, dsti = S.sb("edge_src_i", [P, B, L], I32), S.sb("edge_dst_i", [P, B, L], I32)
        fields = S.sb("edge_fields", [P, FIELDS, B, L])
        rel = S.sb("edge_rel", [P, B, L])
        row16 = S.sb("edge_rows16", [P, B, PAIR, 2, P], U16)
        least, base = S.sb("edge_least", [P, B]), S.sb("edge_base", [P, B])
        most = S.sb("edge_most", [P, 2])
        base_t = S.sb("edge_base_t", [B, P], I32)
        flag_f = S.sb("flag_f", [1, 2])
        ps = S.ps("ps_edges", [P, 2, 4, P])
        ps_small = S.ps("ps_small", [P, GROUP])
        (padded, src_loaded, dst_loaded, w_loaded, filled, step, turned, copied, base_ready, base_stored, base_loaded,
         small, row16_ready, rows_stored, zero_stored) = [
            S.sem("e_" + n) for n in ("padded", "src_loaded", "dst_loaded", "w_loaded", "filled", "step", "turned",
                                      "copied", "base_ready", "base_stored", "base_loaded", "small_turned",
                                      "row16_ready", "rows_stored", "zero_stored")]

        def blocks_of(a):
            return a[0:full * P * L].rearrange("(b c e) -> c b e", c=P, e=L)

        def rows_of(a):
            return a[full * P * L:(full * P + whole) * L].rearrange("(c e) -> c e", e=L)

        def tail_of(a):
            return a[T.E - rest:T.E].rearrange("(a e) -> a e", a=1)

        with nc.Block() as block:

            @block.sync
            def _(sp):
                sp.wait_ge(padded, 3)
                for dst, a, done in ((dsti, T.dst, dst_loaded), (srci, T.src, src_loaded),
                                     (fields[:, WGT], T.ew, w_loaded)):
                    sp.dma_start(dst[:, 0:full, :], blocks_of(a)).then_inc(done, 16)
                    sp.dma_start(dst[0:whole, full, :], rows_of(a)).then_inc(done, 16)
                    sp.dma_start(dst[whole:whole + 1, full, 0:rest], tail_of(a)).then_inc(done, 16)
                    if a is T.dst:
                        sp.dma_start(dsti[whole:whole + 1, full, rest:L],
                                     T.dst[T.E - (L - rest):T.E].rearrange("(a e) -> a e", a=1)).then_inc(done, 16)
                n = 0
                for row in range(0, T.ACC_ROWS, GROUP):
                    zero_rows(sp, T, T.acc[NACC - 1], row, zero_stored)
                    n += 1
                sp.wait_ge(row16_ready, 2)
                sp.dma_start(T.rows16.rearrange("(b c s) f e -> c b (s f e)", c=P, s=PAIR),
                             row16[:, :, :, :, :].rearrange("p b s f e -> p b (s f e)")).then_inc(rows_stored, 16)
                sp.wait_ge(base_ready, 1)
                sp.dma_start(T.base_dram.rearrange("(b c) -> b c", c=P), base_t[:, :]).then_inc(base_stored, 16)
                sp.wait_ge(base_stored, 16)
                sp.dma_start(T.base_row[:, :], T.base_dram.rearrange("(a c) -> a c", a=1)).then_inc(base_loaded, 16)
                sp.wait_ge(base_loaded, 16)
                sp.wait_ge(rows_stored, 16)
                sp.wait_ge(zero_stored, 16 * n)

            @block.vector
            def _(dve):
                dve.memset(srci[:, full, :], T.N).then_inc(padded, 1)
                dve.memset(dsti[:, full, :], 0).then_inc(padded, 1)
                dve.memset(fields[:, WGT, full, :], 0.0).then_inc(padded, 1)
                dve.wait_ge(padded, 3)
                dve.wait_ge(dst_loaded, 64)
                dve.tensor_scalar(fields[:, DST], dsti[:, :, :], BANDS * T.N - 1, None, ALU.min).then_inc(step, 1)
                dve.wait_ge(src_loaded, 48)
                dve.tensor_scalar(fields[:, SRC], srci[:, :, :], T.N, None, ALU.min).then_inc(step, 1)
                dve.wait_ge(step, 2)
                dve.tensor_reduce(least[:, :], fields[:, DST], AX, ALU.min).then_inc(step, 1)
                dve.wait_ge(step, 3)
                dve.tensor_scalar(base[:, :], least[:, :], BANDS * T.N - WIN, None, ALU.min).then_inc(step, 1)
                dve.wait_ge(step, 4)
                dve.tensor_tensor(rel[:, :, :], fields[:, DST],
                                  base[:, :].rearrange("p (b a) -> p b a", a=1).to_broadcast([P, B, L]),
                                  ALU.subtract).then_inc(step, 1)
                dve.wait_ge(step, 5)
                for i, f in enumerate((fields[:, DST], rel[:, :, :])):
                    dve.tensor_reduce(most[:, i:i + 1], f.rearrange("p b e -> p (b e)"), AX, ALU.max) \
                        .then_inc(filled, 1)
                dve.wait_ge(small, 3)
                dve.tensor_copy(base_t[:, :], ps_small[0:B, 0:P]).then_inc(base_ready, 1)
                for i in range(2):
                    dve.tensor_reduce(flag_f[:, i:i + 1], ps_small[0:1, (i + 1) * P:(i + 2) * P], AX, ALU.max) \
                        .then_inc(step, 1)
                dve.wait_ge(step, 7)
                dve.tensor_scalar(T.flags[:, 0:1], flag_f[:, 0:1], T.N, None, ALU.is_ge).then_inc(step, 1)
                dve.tensor_scalar(T.flags[:, 1:2], flag_f[:, 1:2], WIN, None, ALU.is_ge).then_inc(step, 1)
                dve.wait_ge(step, 9)

            @block.gpsimd
            def _(pool):
                pool.wait_ge(step, 5)
                pool.tensor_copy(row16[:, :, :, 0, :], fields[:, SRC].rearrange("p b (s e) -> p b s e", s=PAIR)) \
                    .then_inc(row16_ready, 1)
                pool.tensor_scalar(row16[:, :, :, 1, :], rel[:, :, :].rearrange("p b (s e) -> p b s e", s=PAIR),
                                   float(WIN), None, ALU.min).then_inc(row16_ready, 1)

            @block.tensor
            def _(pe):
                pe.wait_ge(filled, 2)
                pe.wait_ge(w_loaded, 48)
                pe.transpose(ps_small[0:B, 0:P], base[:, :], T.ident[:, :]).then_inc(small, 1)
                for i in range(2):
                    pe.transpose(ps_small[0:1, (i + 1) * P:(i + 2) * P], most[:, i:i + 1], T.ident[:, :]) \
                        .then_inc(small, 1)
                for n in range(B * PAIR):
                    b, s = n // PAIR, n % PAIR
                    if n >= 2:
                        pe.wait_ge(copied, n - 1)
                    for f in range(FIELDS):
                        last = pe.transpose(ps[:, n % 2, f, :], fields[:, f, b, s * P:(s + 1) * P], T.ident[:, :])
                    last.then_inc(turned, 1)

            @block.scalar
            def _(act):
                halves = P * PAIR // HALF
                for n in range(B * PAIR):
                    b, s = n // PAIR, n % PAIR
                    act.wait_ge(turned, n + 1)
                    for a in range(HALF // PAIR):
                        last = act.copy(T.edges[:, b * halves:(b + 1) * halves, :, PAIR * a + s]
                                        .rearrange("p q f -> p f q"),
                                        ps[:, n % 2, 0:FIELDS, :].rearrange("p f (q a) -> p f q a", a=HALF // PAIR)
                                        [:, :, :, a])
                    last.then_inc(copied, 1)


def stage_stats(nc, T):
    NS = 25
    W = T.N // NS
    assert NS * W == T.N and W <= 512
    with Stage(nc) as S:
        stats = S.sb("bn_stats", [P, KD, NS, 6])
        mv = S.sb("bn_mv", [P, KD, 2])
        std, tmp = S.sb("bn_std", [P, KD, 1]), S.sb("bn_tmp", [P, KD, 1])
        step, std_ready = S.sem("bn_step"), S.sem("bn_std_ready")
        with nc.Block() as block:

            @block.vector
            def _(dve):
                for k in range(KD):
                    for n in range(NS):
                        last = dve.bn_stats(stats[:, k, n, :], T.xt[:, k, n * W:(n + 1) * W])
                last.then_inc(step, 1)
                dve.wait_ge(step, 1)
                for k in range(KD):
                    last = dve.bn_aggr(mv[:, k, :], stats[:, k, :, :])
                last.then_inc(step, 1)
                dve.wait_ge(step, 2)
                dve.wait_ge(std_ready, 1)
                dve.reciprocal(tmp[:, :, :], std[:, :, :]).then_inc(step, 1)
                dve.wait_ge(step, 3)
                dve.tensor_tensor(T.bn_scale[:, :], T.gam[:, :], tmp[:, :, 0], ALU.mult).then_inc(step, 1)
                dve.wait_ge(step, 4)
                dve.tensor_tensor(tmp[:, :, 0], mv[:, :, 0], T.bn_scale[:, :], ALU.mult).then_inc(step, 1)
                dve.wait_ge(step, 5)
                dve.tensor_tensor(T.bn_shift[:, :], T.bet[:, :], tmp[:, :, 0], ALU.subtract).then_inc(step, 1)
                dve.wait_ge(step, 6)
                dve.tensor_scalar(T.bn_neg[:, 0:KD], T.bn_scale[:, :], -1.0, None, ALU.mult).then_inc(step, 1)
                dve.tensor_scalar(T.bn_neg[:, KD:2 * KD], T.bn_shift[:, :], -1.0, None, ALU.mult).then_inc(step, 1)
                dve.wait_ge(step, 8)

            @block.scalar
            def _(act):
                act.wait_ge(step, 2)
                act.activation(std[:, :, :], mv[:, :, 1:2], ACT.Sqrt, bias=T.eps_ln[:, :]).then_inc(std_ready, 1)


def stage_table(nc, T, extra):
    tag = "x_" if extra else ""
    per = [T.NG // 2 + 1, T.NG // 2]
    with Stage(nc) as S:
        pos = S.sb(tag + "elu_pos", [P, 2, KD, GROUP])
        neg = S.sb(tag + "elu_neg", [P, 2, KD, GROUP])
        xe = S.sb(tag + "elu", [P, 2, KD, GROUP])
        rows = S.sb(tag + "table_rows", [P, 2, TG, D])
        parts = S.sb(tag + "table_parts", [P, 2, TG, 2, D], F32R)
        ps = S.ps(tag + "ps_table", [P, 4, GROUP])
        neg_ready, elu_parts, elu_ready, products, bank_read, rows_hi, rows_lo, stored = [
            S.sems(tag + n, 2) for n in ("neg_ready", "elu_parts", "elu_ready", "products", "bank_read",
                                         "rows_hi", "rows_lo", "rows_stored")]
        zero_stored = S.sem(tag + "t_zero_stored")

        def bands(eng, run):
            if not extra:
                run(0, (0, 0))
                return
            flag = eng.value_load(T.flags[0:1, 0:1], min_val=0, max_val=1)
            with eng.If(flag):
                for band in range(1, BANDS):
                    run(band, [(band - 1) * per[0], (band - 1) * per[1]])

        with nc.Block() as block:

            @block.scalar
            def _(act):
                def run(band, before):
                    def elu_terms(j, par, g):
                        turn = before[par] + j
                        cols = bass.ds(T.first_row(g), GROUP)
                        wait_turns(act, elu_ready[par], turn)
                        for k in range(KD):
                            last = act.activation(neg[:, par, k, :], T.xt[:, k, cols], ACT.Relu,
                                                  bias=T.bn_neg[:, KD + k:KD + k + 1], scale=T.bn_neg[:, k:k + 1])
                        last.then_inc(neg_ready[par], 1)
                        for k in range(KD):
                            act.activation(pos[:, par, k, :], T.xt[:, k, cols], ACT.Relu,
                                           bias=T.bn_shift[:, k:k + 1], scale=T.bn_scale[:, k:k + 1])
                        act.wait_ge(neg_ready[par], turn + 1)
                        act.activation(neg[:, par, :, :], neg[:, par, :, :], ACT.Exp, scale=-1.0) \
                            .then_inc(elu_parts[par], 1)

                    def rows_high(j, par):
                        turn = before[par] + j
                        act.wait_ge(bank_read[par], 2 * (turn + 1))
                        wait_turns(act, stored[par], 16 * turn)
                        act.copy(parts[:, par, :, 0, :], rows[:, par, :, :]).then_inc(rows_hi[par], 1)

                    elu_terms(0, 0, 0)
                    elu_terms(0, 1, 1)
                    rows_high(0, 0)
                    with act.Fori(1, T.NG // 2) as j:
                        elu_terms(j, 0, 2 * j)
                        rows_high(j - 1, 1)
                        elu_terms(j, 1, 2 * j + 1)
                        rows_high(j, 0)
                    elu_terms(T.NG // 2, 0, T.NG - 1)
                    rows_high(T.NG // 2 - 1, 1)
                    rows_high(T.NG // 2, 0)
                bands(act, run)

            @block.vector
            def _(dve):
                def run(band, before):
                    bias = T.bias_bc[:, band * D:(band + 1) * D].rearrange("p (a d) -> p a d", a=1) \
                        .to_broadcast([P, 2, D])

                    def combine(j, par):
                        turn = before[par] + j
                        dve.wait_ge(elu_parts[par], turn + 1)
                        wait_turns(dve, products[par], 2 * turn)
                        dve.scalar_tensor_tensor(out=xe[:, par, :, :], in0=neg[:, par, :, :], scalar=-1.0,
                                                 in1=pos[:, par, :, :], op0=ALU.add, op1=ALU.add) \
                            .then_inc(elu_ready[par], 1)

                    def add_bias(j, par):
                        turn = before[par] + j
                        wait_turns(dve, rows_lo[par], turn)
                        for i in range(2):
                            dve.wait_ge(products[par], 2 * turn + i + 1)
                            dve.tensor_tensor(rows[:, par, 2 * i:2 * i + 2, :],
                                              ps[:, 2 * par + i, :].rearrange("p (t d) -> p t d", d=D),
                                              bias, ALU.add).then_inc(bank_read[par], 1)

                    combine(0, 0)
                    combine(0, 1)
                    add_bias(0, 0)
                    with dve.Fori(1, T.NG // 2) as j:
                        combine(j, 0)
                        add_bias(j - 1, 1)
                        combine(j, 1)
                        add_bias(j, 0)
                    combine(T.NG // 2, 0)
                    add_bias(T.NG // 2 - 1, 1)
                    add_bias(T.NG // 2, 0)
                bands(dve, run)

            @block.gpsimd
            def _(pool):
                def run(band, before):
                    def rows_low(j, par, g):
                        turn = before[par] + j
                        pool.wait_ge(rows_hi[par], turn + 1)
                        pool.tensor_tensor(parts[:, par, :, 1, :], rows[:, par, :, :],
                                           parts[:, par, :, 0, :].bitcast(F32), ALU.subtract).then_inc(rows_lo[par], 1)
                    in_pairs(pool, T.NG, rows_low)
                bands(pool, run)

            @block.tensor
            def _(pe):
                def run(band, before):
                    def multiply(j, par, g):
                        turn = before[par] + j
                        pe.wait_ge(elu_ready[par], turn + 1)
                        wait_turns(pe, bank_read[par], 2 * turn)
                        for i in range(2):
                            for t in (2 * i, 2 * i + 1):
                                for k in range(KD):
                                    last = pe.matmul(ps[:, 2 * par + i, (t % 2) * D:(t % 2 + 1) * D],
                                                     xe[:, par, k, t * P:(t + 1) * P],
                                                     T.wt[:, k, band * D:(band + 1) * D],
                                                     start=(k == 0), stop=(k == KD - 1))
                            last.then_inc(products[par], 1)
                    in_pairs(pe, T.NG, multiply)
                bands(pe, run)

            @block.sync
            def _(sp):
                def run(band, before):
                    def store(j, par, g):
                        turn = before[par] + j
                        row, zero_row = band * T.N + T.first_row(g), g * GROUP
                        if not isinstance(row, int):
                            row = sp.snap(row)
                            zero_row = row
                        if isinstance(g, int) and g == T.NG - 1:
                            sp.wait_ge(stored[1], 16 * (before[1] + per[1]))
                        sp.wait_ge(rows_lo[par], turn + 1)
                        sp.dma_start(T.table[bass.ds(row, GROUP), :].rearrange("(t p) d -> p t d", p=P),
                                     parts[:, par, :, :, :].rearrange("p t h d -> p t (h d)").bitcast(F32)) \
                            .then_inc(stored[par], 16)
                    in_pairs(sp, T.NG, store)
                    for par in range(2):
                        sp.wait_ge(stored[par], 16 * (before[par] + per[par]))
                bands(sp, run)


def stage_weights(nc, T):
    EX = T.EX
    R = EX * KD
    mats = ((T.W1, T.w1), (T.W2, T.w2), (T.Wo, T.wo))
    vecs = T.vec_inputs
    with Stage(nc) as S:
        raw = S.sb("w_raw", [P, 2, EX, D])
        v = S.sb("vectors", [R, 10, P])
        sc = S.sb("vec_scale", [R, 2, P])
        sh = S.sb("vec_shift", [R, 2, P])
        wr = S.sb("wr_raw", [P, KD, EX])
        ps = S.ps("ps_vec", [P, 4, R])
        w_loaded = S.sems("we_loaded", 2)
        hi_ready, lo_ready, v_loaded, step, std_ready, turned, wr_loaded = [
            S.sem(n) for n in ("hi_ready", "lo_ready", "vec_loaded", "vec_step", "vec_std", "vec_turned", "wr_loaded")]
        with nc.Block() as block:

            @block.sync
            def _(sp):
                for i, a in enumerate(vecs):
                    sp.dma_start(v[:, i, :], a.rearrange("e (k p) -> (e k) p", p=P)).then_inc(v_loaded, 16)
                with nc.allow_non_contiguous_dma(reason="gate weights, small"):
                    sp.dma_start(wr[:, :, :], T.Wr.rearrange("(k p) e -> p k e", p=P)).then_inc(wr_loaded, 16)
                sp.dma_start(T.br_bc[:, :], T.br.rearrange("(a n) -> a n", a=1).to_broadcast([P, EX])) \
                    .then_inc(wr_loaded, 16)
                sp.dma_start(T.bo_sb[:, :], T.bo).then_inc(wr_loaded, 16)
                n = 0
                for a, _ in mats:
                    for k in range(KD):
                        if n >= 2:
                            sp.wait_ge(lo_ready, n - 1)
                        sp.dma_start(raw[:, n % 2, :, :], a[:, k * P:(k + 1) * P, :].rearrange("e p h -> p e h")) \
                            .then_inc(w_loaded[n % 2], 16)
                        n += 1

            @block.vector
            def _(dve):
                n = 0
                for _, (hi, lo) in mats:
                    for k in range(KD):
                        dve.wait_ge(hi_ready, n + 1)
                        dve.tensor_tensor(lo[:, k, :, :], raw[:, n % 2, :, :], hi[:, k, :, :].bitcast(F32),
                                          ALU.subtract).then_inc(lo_ready, 1)
                        n += 1
                dve.wait_ge(hi_ready, n + 1)
                dve.tensor_tensor(T.wr[1][:, :, :], wr[:, :, :], T.wr[0][:, :, :].bitcast(F32), ALU.subtract) \
                    .then_inc(lo_ready, 1)
                dve.wait_ge(std_ready, 1)
                dve.reciprocal(sh[:, :, :], sc[:, :, :]).then_inc(step, 1)
                dve.wait_ge(step, 1)
                for i in range(2):
                    dve.tensor_tensor(sc[:, i, :], v[:, 5 * i + 1, :], sh[:, i, :], ALU.mult).then_inc(step, 1)
                dve.wait_ge(step, 3)
                for i in range(2):
                    dve.tensor_tensor(sh[:, i, :], v[:, 5 * i, :], v[:, 5 * i + 3, :], ALU.subtract).then_inc(step, 1)
                dve.wait_ge(step, 5)
                for i in range(2):
                    dve.tensor_tensor(sh[:, i, :], sh[:, i, :], sc[:, i, :], ALU.mult).then_inc(step, 1)
                dve.wait_ge(step, 7)
                for i in range(2):
                    dve.tensor_tensor(sh[:, i, :], sh[:, i, :], v[:, 5 * i + 2, :], ALU.add).then_inc(step, 1)
                dve.wait_ge(step, 9)
                dve.wait_ge(turned, 1)
                dve.tensor_copy(T.vec_cols[:, :, :], ps[:, :, :]).then_inc(step, 1)
                dve.wait_ge(step, 10)

            @block.scalar
            def _(act):
                n = 0
                for _, (hi, _) in mats:
                    for k in range(KD):
                        act.wait_ge(w_loaded[n % 2], 16 * (n // 2 + 1))
                        act.copy(hi[:, k, :, :], raw[:, n % 2, :, :]).then_inc(hi_ready, 1)
                        n += 1
                act.wait_ge(wr_loaded, 48)
                act.copy(T.wr[0][:, :, :], wr[:, :, :]).then_inc(hi_ready, 1)
                act.wait_ge(v_loaded, 160)
                for i in range(2):
                    last = act.activation(sc[:, i, :], v[:, 5 * i + 4, :], ACT.Sqrt, bias=T.eps_ffn[0:R, :])
                last.then_inc(std_ready, 1)

            @block.tensor
            def _(pe):
                pe.wait_ge(step, 9)
                for i in range(2):
                    pe.transpose(ps[:, 2 * i, :], sc[:, i, :], T.ident[0:R, 0:R])
                    last = pe.transpose(ps[:, 2 * i + 1, :], sh[:, i, :], T.ident[0:R, 0:R])
                last.then_inc(turned, 1)


def stage_messages(nc, T):
    ROUNDS = T.CHUNKS // UN
    NH = UN // HALF
    NB = 4
    C = D + 2
    with Stage(nc) as S:
        edge = S.sb("edge_cols", [P, NH, FIELDS, HALF])
        row16 = S.sb("edge_row16", [P, NH, HALF, 2, P], U16)
        same = S.sb("same_target", [P, UN, P], F32R)
        spread = S.sb("spread", [P, UN, P], F32R)
        win = S.sb("window", [P, UN // PAIR, D], F32R)
        gathered = S.sb("gathered", [P, UN, 2, D], F32R)
        w_hi = S.sb("weighted_hi", [P, UN, C], F32R)
        w_lo = S.sb("weighted_lo", [P, UN, C], F32R)
        sums = S.sb("chunk_sums", [P, UN, C])
        later = S.sb("later", [P, NH, HALF])
        own = S.sb("own_target", [P, NH, HALF])
        away = S.sb("away", [P, NH, HALF])
        target = S.sb("target_row", [P, NH, HALF], I32)
        rowi = S.sb("table_row_i", [P, NH, HALF], I32)
        ps_rows = S.ps("ps_rows", [P, NB, GROUP])
        ps_sum = S.ps("ps_sum", [P, NB, GROUP])
        ranked, zero_col = S.sem("ranked"), S.sem("zero_col")

        edge_ready, row16_loaded, target_ready, rowi_ready, later_ready, own_ready, away_ready = [
            S.sems(n, NH) for n in ("edge_ready", "row16_loaded", "target_ready", "rowi_ready", "later_ready",
                                    "own_ready", "away_ready")]
        rows_read, sum_copied = [S.sems(n, NB) for n in ("rows_read", "sum_copied")]
        rows_ready, spread_ready, same_ready, rows_out, hi_ready, sum_ready, added = [
            S.sems(n, UN) for n in ("rows_ready", "spread_ready", "same_ready", "rows_out", "hi_ready",
                                    "sum_ready", "added")]
        passed = S.sem("m_passed")

        def run(windows):
            def slots():
                return [(u, u // HALF, u % HALF, u % NB, u // NB) for u in range(UN)]

            PB = UN // NB

            def rounds(eng, *ops):
                def body(r, first=False):
                    for u in range(UN):
                        for delay, op in ops:
                            if u >= delay:
                                op(r, *slots()[u - delay])
                            elif not first:
                                op(r - 1, *slots()[u - delay + UN])
                body(0, True)
                with eng.Fori(1, ROUNDS) as r:
                    body(r)
                for u in range(max(delay for delay, _ in ops)):
                    for delay, op in ops:
                        if u < delay:
                            op(ROUNDS - 1, *slots()[u - delay + UN])

            def sync(sp):
                def load(r, u, h, i, bank, n):
                    if i == 0:
                        chunk = r * UN + h * HALF
                        if not isinstance(chunk, int):
                            chunk = sp.snap(chunk)
                        wait_turns(sp, same_ready[HALF * h + HALF - 1], r)
                        sp.dma_start(row16[:, h, :, :, :].rearrange("p c f e -> p (c f e)"),
                                     T.rows16[bass.ds(chunk, HALF), :, :].rearrange("(a c) f e -> a (c f e)", a=1)
                                     .to_broadcast([P, HALF * 2 * P])).then_inc(row16_loaded[h], 16)
                    if windows and i % PAIR == 0:
                        w = u // PAIR
                        row = sp.value_load(T.base_row[0:1, bass.ds(r * (UN // PAIR) + w, 1)], min_val=0,
                                            max_val=BANDS * T.N - WIN)
                        wait_turns(sp, rows_out[u + PAIR - 1], r)
                        sp.dma_start(win[:, w, :].bitcast(F32),
                                     T.table[bass.ds(row, WIN), :].rearrange("r (k d) -> k r d", k=2)) \
                            .then_inc(rows_ready[u], 16)
                rounds(sp, (0, load))

            def scalar(act):
                def fetch(r, u, h, i, bank, n):
                    if i:
                        return
                    wait_turns(act, rows_read[NB - 1], PB * r + h - 1 if not isinstance(r, int) else (PB * (r - 1) + h + 1) * min(r, 1))
                    act.copy(edge[:, h, :, :], T.edges[:, NH * r + h, :, :]).then_inc(edge_ready[h], 1)

                def weight_rows(r, u, h, i, bank, n):
                    if i == 0:
                        act.wait_ge(edge_ready[h], r + 1)
                    act.wait_ge(rows_out[u], r + 1)
                    wait_turns(act, sum_ready[u], r)
                    act.activation(w_hi[:, u, 0:D], ps_rows[:, bank, 0:D], ACT.Copy, scale=edge[:, h, WGT, i:i + 1]) \
                        .then_inc(hi_ready[u], 1)

                def sum_out(r, u, h, i, bank, n):
                    act.wait_ge(sum_ready[u], r + 1)
                    wait_turns(act, added[u], 16 * r)
                    act.copy(sums[:, u, 0:D + 1], ps_sum[:, bank, 0:D + 1]).then_inc(sum_copied[bank], 1)

                rounds(act, (0, fetch), (1, weight_rows), (6, sum_out))

            def tensor(pe):
                def bring_rows(r, u, h, i, bank, n):
                    wait_turns(pe, rows_read[bank], PB * r + n)
                    if windows:
                        pe.wait_ge(spread_ready[u], r + 1)
                        if i % PAIR == 0:
                            pe.wait_ge(rows_ready[u], 16 * (r + 1))
                        mm = pe.matmul(ps_rows[:, bank, 0:D], spread[:, u, :], win[:, u // PAIR, :],
                                       start=True, stop=True)
                    else:
                        pe.wait_ge(rows_ready[u], 16 * (r + 1))
                        pe.matmul(ps_rows[:, bank, 0:D], T.ident_r[:, :], gathered[:, u, 0, :], start=True, stop=False)
                        mm = pe.matmul(ps_rows[:, bank, 0:D], T.ident_r[:, :], gathered[:, u, 1, :],
                                       start=False, stop=True)
                    mm.then_inc(rows_out[u], 1)

                def sum_rows(r, u, h, i, bank, n):
                    wait_turns(pe, sum_copied[bank], PB * r + n)
                    pe.wait_ge(same_ready[u], r + 1)
                    pe.wait_ge(rows_read[bank], PB * r + n + 1)
                    pe.matmul(ps_sum[:, bank, 0:C], same[:, u, :], w_hi[:, u, :], start=True, stop=False)
                    pe.matmul(ps_sum[:, bank, 0:C], same[:, u, :], w_lo[:, u, :], start=False, stop=True) \
                        .then_inc(sum_ready[u], 1)

                pe.wait_ge(zero_col, 1)
                pe.wait_ge(ranked, 1)
                rounds(pe, (0, bring_rows), (4, sum_rows))

            def vector(dve):
                def compare(r, u, h, i, bank, n):
                    if i == 0:
                        dve.wait_ge(edge_ready[h], r + 1)
                        dve.wait_ge(row16_loaded[h], 16 * (r + 1))
                        if not windows:
                            for k in range(HALF):
                                wait_turns(dve, rows_ready[HALF * h + k], 16 * r)
                            dve.tensor_copy(rowi[:, h, :], edge[:, h, DST, :]).then_inc(rowi_ready[h], 1)
                    if windows:
                        wait_turns(dve, rows_out[u], r)
                        dve.tensor_scalar(spread[:, u, :], row16[:, h, i, 1, :], T.win_row[:, :], None, ALU.is_equal) \
                            .then_inc(spread_ready[u], 1)
                    wait_turns(dve, sum_ready[u], r)
                    dve.tensor_scalar(same[:, u, :], row16[:, h, i, 0, :], edge[:, h, SRC, i:i + 1], None,
                                      ALU.is_equal).then_inc(same_ready[u], 1)

                def keep(r, u, h, i, bank, n):
                    if i == 0:
                        wait_turns(dve, target_ready[h], r)
                        dve.tensor_copy(own[:, h, :], edge[:, h, SRC, :]).then_inc(own_ready[h], 1)
                        dve.tensor_tensor(away[:, h, :], T.spare[:, :], edge[:, h, SRC, :], ALU.subtract) \
                            .then_inc(away_ready[h], 1)

                def weight_low(r, u, h, i, bank, n):
                    dve.wait_ge(hi_ready[u], r + 1)
                    dve.scalar_tensor_tensor(out=w_lo[:, u, 0:D], in0=ps_rows[:, bank, 0:D],
                                             scalar=edge[:, h, WGT, i:i + 1], in1=w_hi[:, u, 0:D].bitcast(F32),
                                             op0=ALU.mult, op1=ALU.subtract).then_inc(rows_read[bank], 1)

                def targets(r, u, h, i, bank, n):
                    if i < HALF - 1:
                        return
                    for _, hh, _, b, m in slots():
                        if hh == h:
                            dve.wait_ge(sum_copied[b], PB * r + m + 1)
                    ranks = sums[:, HALF * h:HALF * (h + 1), D]
                    dve.tensor_scalar(later[:, h, :], ranks, T.unrank[:, :], 2.5, ALU.mult, ALU.is_ge) \
                        .then_inc(later_ready[h], 1)
                    dve.wait_ge(later_ready[h], r + 1)
                    dve.wait_ge(away_ready[h], 2 * r + 1)
                    dve.tensor_tensor(away[:, h, :], away[:, h, :], later[:, h, :], ALU.mult) \
                        .then_inc(away_ready[h], 1)
                    dve.wait_ge(away_ready[h], 2 * r + 2)
                    for k in range(HALF):
                        wait_turns(dve, added[HALF * h + k], 16 * r)
                    dve.tensor_tensor(target[:, h, :], away[:, h, :], own[:, h, :], ALU.add) \
                        .then_inc(target_ready[h], 1)

                rounds(dve, (0, compare), (7, targets), (3, keep), (3, weight_low))

            def gpsimd(pool):
                def gather(r, u, h, i, bank, n):
                    if i == 0:
                        pool.wait_ge(rowi_ready[h], r + 1)
                    wait_turns(pool, rows_out[u], r)
                    alone(pool, passed)
                    pool.indirect_dma_start(gathered[:, u, :, :].rearrange("p h d -> p (h d)").bitcast(F32), None, T.table,
                                            bass.IndirectOffsetOnAxis(ap=rowi[:, h, i:i + 1], axis=0)) \
                        .then_inc(rows_ready[u], 16)

                def add(r, u, h, i, bank, n):
                    if i == 0:
                        pool.wait_ge(target_ready[h], r + 1)
                    if u < NACC:
                        wait_turns(pool, added[u + NACC], 16 * r)
                    else:
                        pool.wait_ge(added[u - NACC], 16 * (r + 1))
                    alone(pool, passed)
                    pool.indirect_dma_start(T.acc[u % NACC], bass.IndirectOffsetOnAxis(ap=target[:, h, i:i + 1], axis=0),
                                            sums[:, u, 0:D], None, compute_op=ALU.add).then_inc(added[u], 16)

                if windows:
                    rounds(pool, (0, add))
                else:
                    rounds(pool, (0, gather), (UN, add))
                for u in range(UN):
                    pool.wait_ge(added[u], 16 * ROUNDS)

            return sync, scalar, tensor, vector, gpsimd

        one_by_one = run(False)
        by_window = run(True)

        def either(eng, k):
            flag = eng.value_load(T.flags[0:1, 1:2], min_val=0, max_val=1)
            with eng.If(flag):
                one_by_one[k](eng)
            with eng.Else():
                by_window[k](eng)

        with nc.Block() as block:

            @block.sync
            def _(sp):
                either(sp, 0)

            @block.scalar
            def _(act):
                act.copy(w_hi[:, :, D:D + 1], T.rank[:, :].rearrange("p (a b) -> p a b", a=1).to_broadcast([P, UN, 1])) \
                    .then_inc(ranked, 1)
                either(act, 1)

            @block.tensor
            def _(pe):
                either(pe, 2)

            @block.vector
            def _(dve):
                zero = T.zeros[:, 0:2 * UN].rearrange("p (u c) -> p u c", u=UN)
                dve.tensor_copy(w_hi[:, :, D + 1:C], zero[:, :, 0:1])
                dve.tensor_copy(w_lo[:, :, D:C], zero).then_inc(zero_col, 1)
                either(dve, 3)

            @block.gpsimd
            def _(pool):
                either(pool, 4)


def stage_mixture(nc, T):
    EX, NZ = T.EX, 4
    STEPS = EX + 2
    with Stage(nc) as S:
        y = S.sb("y", [P, 2, TG, D])
        spent = T.edges[:, :, :, :].rearrange("p q f i -> p (q f i)")
        part = spent[:, 0:(NACC - 1) * TG * D].rearrange("p (s t d) -> p s t d", s=NACC - 1, t=TG)
        act_f = S.sb("act_f", [P, NZ, GROUP])
        xl = S.sb("xl", [P, TG, D])
        xhi = S.sb("xl_t_hi", [P, 2, KD, GROUP], F32R)
        xlo = S.sb("xl_t_lo", [P, 2, KD, GROUP], F32R)
        h_hi = [S.sb(f"h{l}_hi", [P, 2, KD, GROUP], F32R) for l in (1, 2)]
        h_lo = [S.sb(f"h{l}_lo", [P, 2, KD, GROUP], F32R) for l in (1, 2)]
        stats, mv = S.sb("m_stats", [P, TG, 6]), S.sb("m_mv", [P, TG, 2])
        std, rstd = S.sb("m_std", [P, TG, 1]), S.sb("m_rstd", [P, TG, 1])
        lg = S.sb("logits", [P, TG, EX])
        red = S.sb("gate_red", [P, 3, TG, 1])
        gate = S.sb("gate", [P, 2, TG, EX])
        gate_t = S.sb("gate_t", [EX, TG, P])
        z = [S.ps(f"z{i}", [P, GROUP]) for i in range(NZ)]
        o = [S.ps(f"o{i}", [P, 2, D]) for i in range(2)]
        tr = S.ps("tr", [P, GROUP])
        misc = S.ps("misc", [P, GROUP])

        x_loaded, y_ready, stored = [S.sems(n, 2) for n in ("mx_loaded", "my_ready", "m_stored")]
        part_loaded, part_added = S.sems("part_loaded", NACC - 1), S.sems("part_added", NACC - 1)
        z_ready, z_split, lo_ready = [S.sems(n, NZ) for n in ("z_ready", "z_split", "lo_ready")]
        o_ready, o_added = S.sems("o_ready", 2), S.sems("o_added", 2)
        passed = S.sem("mix_passed")
        (stats_done, var_ready, std_ready, rstd_ready, xl_ready, tr_ready, tr_hi, tr_read, lg_ready, gate_step, exp_ready,
         gate_ready, gate_turned, gate_t_ready, bo_ready, bo_added, l2_done, l3_done) = [
            S.sem("m_" + n) for n in ("stats_done", "var_ready", "std_ready", "rstd_ready", "xl_ready", "tr_ready",
                                      "tr_hi", "tr_read", "lg_ready", "gate_step", "exp_ready", "gate_ready",
                                      "gate_turned", "gate_t_ready", "bo_ready", "bo_added", "l2_done", "l3_done")]

        def units(s):
            n = max(0, 4 * s - 2) if s > 0 else 0
            found = []
            if s < EX:
                found += [(1, s, m) for m in range(KD)]
            if 1 <= s <= EX:
                found += [(2, s - 1, m) for m in range(KD)]
            return [(n + i, *f) for i, f in enumerate(found)]

        PER = 2 * KD * EX
        TURNS = PER // NZ
        assert [u[0] for s in range(STEPS) for u in units(s)] == list(range(PER))

        def first_count(e, layer):
            return next(u[0] for s in range(STEPS) for u in units(s) if u[1:3] == (layer, e))

        def pipelined(eng, prepare, step):
            for k in range(STEPS):
                prepare(k, 0, 0, 0)
            def pair(j):
                for par in range(2):
                    for s in range(STEPS):
                        step(s, j, par, 2 * j + par)
                        prepare(s, j + par, 1 - par, 2 * j + par + 1)
            pair(0)
            with eng.Fori(1, T.NG // 2) as j:
                pair(j)
            for s in range(STEPS):
                step(s, T.NG // 2, 0, T.NG - 1)

        with nc.Block() as block:

            @block.sync
            def _(sp):
                def rows(a, row):
                    return a[bass.ds(row, GROUP), :].rearrange("(p t) d -> p t d", t=TG)

                def load(j, par, g):
                    row = T.first_row(g)
                    if not isinstance(row, int):
                        row = sp.snap(row)
                    wait_turns(sp, stored[par], 16 * j)
                    sp.dma_start(y[:, par, :, :], rows(T.acc[0], row)).then_inc(x_loaded[par], 16)
                    for k in range(NACC - 1):
                        wait_turns(sp, part_added[k], g)
                        sp.dma_start(part[:, k, :, :], rows(T.acc[k + 1], row)).then_inc(part_loaded[k], 16)

                def store(j, par, g):
                    row = T.first_row(g)
                    if not isinstance(row, int):
                        row = sp.snap(row)
                    for i in range(2):
                        sp.wait_ge(o_added[i], EX * (g + 1))
                    sp.dma_start(rows(T.out, row), y[:, par, :, :]).then_inc(stored[par], 16)

                load(0, 0, 0)
                load(0, 1, 1)
                for par in range(2):
                    store(0, par, par)
                    load(1, par, par + 2)
                with sp.Fori(1, T.NG // 2 - 1) as j:
                    for par in range(2):
                        store(j, par, 2 * j + par)
                        load(j + 1, par, 2 * j + par + 2)
                n = T.NG // 2 - 1
                store(n, 0, 2 * n)
                load(n + 1, 0, 2 * n + 2)
                store(n, 1, 2 * n + 1)
                sp.wait_ge(stored[1], 16 * (n + 1))
                store(n + 1, 0, 2 * n + 2)
                sp.wait_ge(stored[0], 16 * (n + 2))

            @block.gpsimd
            def _(pool):
                def add_parts(j, par, g):
                    pool.wait_ge(x_loaded[par], 16 * (j + 1))
                    for k in range(NACC - 1):
                        pool.wait_ge(part_loaded[k], 16 * (g + 1))
                        if k:
                            pool.wait_ge(part_added[k - 1], g + 1)
                        pool.tensor_tensor(y[:, par, :, :], y[:, par, :, :], part[:, k, :, :], ALU.add) \
                            .then_inc(part_added[k], 1)
                in_pairs(pool, T.NG, add_parts)

            @block.tensor
            def _(pe):
                def split_products(out, pairs):
                    passes = [(l[a], r[b]) for l, r in pairs for a, b in ((0, 0), (1, 0), (0, 1))]
                    for n, (l, r) in enumerate(passes):
                        last = pe.matmul(out, l, r, start=(n == 0), stop=(n == len(passes) - 1))
                    return last

                def prepare(k, j, par, g):
                    if k in (4, 5):
                        half = k - 4
                        pe.wait_ge(xl_ready, g + 1)
                        if half == 0:
                            wait_turns(pe, bo_added, 2 * g)
                        else:
                            pe.wait_ge(tr_read, 2 * g + 1)
                        for t in range(TG):
                            last = pe.transpose(tr[:, t * P:(t + 1) * P], xl[:, t, half * P:(half + 1) * P],
                                                T.ident[:, :])
                        last.then_inc(tr_ready, 1)
                    if k == 6:
                        pe.wait_ge(tr_read, 2 * g + 2)
                        for t in range(TG):
                            last = split_products(misc[:, t * EX:(t + 1) * EX],
                                                  [([xhi[:, par, q, t * P:(t + 1) * P], xlo[:, par, q, t * P:(t + 1) * P]],
                                                    [T.wr[0][:, q, :], T.wr[1][:, q, :]]) for q in range(KD)])
                        last.then_inc(lg_ready, 1)
                    if k == 8:
                        pe.wait_ge(gate_ready, g + 1)
                        for t in range(TG):
                            last = pe.transpose(misc[0:EX, t * P:(t + 1) * P], gate[:, par, t, :], T.ident[:, :])
                        last.then_inc(gate_turned, 1)
                    if k == 9:
                        pe.wait_ge(gate_t_ready, g + 1)
                        for t in range(TG):
                            bank = tr if t < 2 else misc
                            last = pe.matmul(bank[:, (t % 2) * D:(t % 2 + 1) * D], gate_t[:, t, :], T.bo_sb[:, :],
                                             start=True, stop=True)
                        last.then_inc(bo_ready, 1)

                def step(s, j, par, g):
                    for n, layer, e, m in units(s):
                        b = n % NZ
                        cols = slice(m * P, (m + 1) * P)
                        if layer == 1:
                            w, src = T.w1, (xhi[:, par], xlo[:, par])
                            pe.wait_ge(tr_read, 2 * g + 2)
                        else:
                            w, src = T.w2, (h_hi[0][:, e % 2], h_lo[0][:, e % 2])
                            if m == 0:
                                for q in range(KD):
                                    c = first_count(e, 1) + q
                                    pe.wait_ge(lo_ready[c % NZ], TURNS * g + c // NZ + 1)
                        wait_turns(pe, z_split[b], TURNS * g + n // NZ)
                        last = split_products(z[b][:, :], [([w[0][:, q, e, cols], w[1][:, q, e, cols]],
                                                            [src[0][:, q, :], src[1][:, q, :]]) for q in range(KD)])
                        last.then_inc(z_ready[b], 1)
                    if s >= 2:
                        e = s - 2
                        for q in range(KD):
                            c = first_count(e, 2) + q
                            pe.wait_ge(lo_ready[c % NZ], TURNS * g + c // NZ + 1)
                        for i in range(2):
                            wait_turns(pe, o_added[i], EX * g + e)
                            for t in (2 * i, 2 * i + 1):
                                rows = slice(t * P, (t + 1) * P)
                                last = split_products(o[i][:, t % 2, :],
                                                      [([h_hi[1][:, e % 2, q, rows], h_lo[1][:, e % 2, q, rows]],
                                                        [T.wo[0][:, q, e, :], T.wo[1][:, q, e, :]]) for q in range(KD)])
                            last.then_inc(o_ready[i], 1)
                pipelined(pe, prepare, step)

            @block.scalar
            def _(act):
                def prepare(k, j, par, g):
                    if k == 3:
                        act.wait_ge(var_ready, g + 1)
                        act.activation(std[:, :, :], mv[:, :, 1:2], ACT.Sqrt, bias=T.eps_ln[:, :]).then_inc(std_ready, 1)
                    if k in (4, 5):
                        act.wait_ge(tr_ready, 2 * g + (k - 4) + 1)
                        act.copy(xhi[:, par, k - 4, :], tr[:, :]).then_inc(tr_hi, 1)
                    if k == 7:
                        act.wait_ge(gate_step, 3 * g + 3)
                        act.activation(lg[:, :, :], lg[:, :, :], ACT.Exp).then_inc(exp_ready, 1)
                    if k == 8:
                        act.wait_ge(gate_turned, g + 1)
                        act.copy(gate_t[:, :, :], misc[0:EX, :]).then_inc(gate_t_ready, 1)

                def step(s, j, par, g):
                    for n, layer, e, m in units(s):
                        b = n % NZ
                        col = T.vec_cols[:, 2 * (layer - 1), KD * e + m:KD * e + m + 1]
                        shift = T.vec_cols[:, 2 * (layer - 1) + 1, KD * e + m:KD * e + m + 1]
                        act.wait_ge(z_ready[b], TURNS * g + n // NZ + 1)
                        wait_turns(act, lo_ready[b], TURNS * g + n // NZ)
                        if m == 0:
                            if layer == 1 and e >= 2:
                                for q in range(KD):
                                    c = first_count(e - 2, 2) + q
                                    act.wait_ge(z_ready[c % NZ], TURNS * g + c // NZ + 1)
                            if layer == 2:
                                for i in range(2):
                                    if e >= 2:
                                        act.wait_ge(o_ready[i], EX * g + e - 1)
                                    else:
                                        wait_turns(act, o_ready[i], EX * g)
                            if layer == 1 and e < 2:
                                for c in range(PER - 2 * KD * 1, PER):
                                    wait_turns(act, z_ready[c % NZ], TURNS * g)
                        act.activation(act_f[:, b, :], z[b][:, :], ACT.Relu, bias=shift, scale=col)
                        act.activation(h_hi[layer - 1][:, e % 2, m, :], z[b][:, :], ACT.Relu, bias=shift, scale=col) \
                            .then_inc(z_split[b], 1)
                pipelined(act, prepare, step)

            @block.vector
            def _(dve):
                def prepare(k, j, par, g):
                    if k == 3:
                        dve.wait_ge(part_added[NACC - 2], g + 1)
                        for t in range(TG):
                            last = dve.bn_stats(stats[:, t, :], y[:, par, t, :])
                        last.then_inc(stats_done, 1)
                        dve.wait_ge(stats_done, g + 1)
                        alone(dve, passed)
                        for t in range(TG):
                            last = dve.bn_aggr(mv[:, t, :], stats[:, t, :])
                        last.then_inc(var_ready, 1)
                        dve.wait_ge(var_ready, g + 1)
                        dve.wait_ge(std_ready, g + 1)
                        dve.reciprocal(rstd[:, :, :], std[:, :, :]).then_inc(rstd_ready, 1)
                        dve.wait_ge(rstd_ready, g + 1)
                        wait_turns(dve, tr_ready, 2 * g)
                        for t in range(TG):
                            last = dve.tensor_scalar(xl[:, t, :], y[:, par, t, :], mv[:, t, 0:1], rstd[:, t, :],
                                                     ALU.subtract, ALU.mult)
                        last.then_inc(xl_ready, 1)
                    if k in (4, 5):
                        dve.wait_ge(tr_hi, 2 * g + (k - 4) + 1)
                        dve.tensor_tensor(xlo[:, par, k - 4, :], tr[:, :], xhi[:, par, k - 4, :].bitcast(F32),
                                          ALU.subtract).then_inc(tr_read, 1)
                    if k == 6:
                        def bc(i):
                            return red[:, i, :, :].to_broadcast([P, TG, EX])
                        dve.wait_ge(lg_ready, g + 1)
                        dve.tensor_tensor(lg[:, :, :], misc[:, 0:TG * EX].rearrange("p (t e) -> p t e", e=EX),
                                          T.br_bc[:, :].rearrange("p (a e) -> p a e", a=1).to_broadcast([P, TG, EX]),
                                          ALU.add).then_inc(gate_step, 1)
                        dve.wait_ge(gate_step, 3 * g + 1)
                        dve.tensor_reduce(red[:, 0, :, :], lg[:, :, :], AX, ALU.max).then_inc(gate_step, 1)
                        dve.wait_ge(gate_step, 3 * g + 2)
                        dve.tensor_tensor(lg[:, :, :], lg[:, :, :], bc(0), ALU.subtract).then_inc(gate_step, 1)
                    if k == 7:
                        dve.wait_ge(exp_ready, 3 * g + 1)
                        dve.tensor_reduce(red[:, 1, :, :], lg[:, :, :], AX, ALU.add).then_inc(exp_ready, 1)
                        dve.wait_ge(exp_ready, 3 * g + 2)
                        dve.reciprocal(red[:, 2, :, :], red[:, 1, :, :]).then_inc(exp_ready, 1)
                        dve.wait_ge(exp_ready, 3 * g + 3)
                        dve.tensor_tensor(gate[:, par, :, :], lg[:, :, :], red[:, 2, :, :].to_broadcast([P, TG, EX]),
                                          ALU.mult).then_inc(gate_ready, 1)
                    if k == 9:
                        dve.wait_ge(bo_ready, g + 1)
                        for i, bank in enumerate((tr, misc)):
                            dve.tensor_tensor(y[:, par, 2 * i:2 * i + 2, :],
                                              y[:, par, 2 * i:2 * i + 2, :],
                                              bank[:, :].rearrange("p (t d) -> p t d", d=D), ALU.add) \
                                .then_inc(bo_added, 1)

                def step(s, j, par, g):
                    for n, layer, e, m in units(s):
                        b = n % NZ
                        dve.wait_ge(z_split[b], TURNS * g + n // NZ + 1)
                        dve.tensor_tensor(h_lo[layer - 1][:, e % 2, m, :], act_f[:, b, :],
                                          h_hi[layer - 1][:, e % 2, m, :].bitcast(F32), ALU.subtract) \
                            .then_inc(lo_ready[b], 1)
                    if s >= 2:
                        e = s - 2
                        dve.wait_ge(gate_ready, g + 1)
                        dve.wait_ge(bo_added, 2 * g + 2)
                        for i in range(2):
                            dve.wait_ge(o_ready[i], EX * g + e + 1)
                            wait_turns(dve, o_added[i], EX * g + e)
                            for t in (2 * i, 2 * i + 1):
                                last = dve.scalar_tensor_tensor(out=y[:, par, t, :], in0=o[i][:, t % 2, :],
                                                                scalar=gate[:, par, t, e:e + 1],
                                                                in1=y[:, par, t, :], op0=ALU.mult, op1=ALU.add)
                            last.then_inc(o_added[i], 1)
                pipelined(dve, prepare, step)


class Tensors:
    pass


INPUTS = ("x", "src", "dst", "edge_weight", "L0_gnn_bn_gamma", "L0_gnn_bn_beta", "L0_gnn_W", "L0_gnn_b",
          "L0_ffn_Wr", "L0_ffn_br", "L0_ffn_W1", "L0_ffn_b1", "L0_ffn_g1", "L0_ffn_be1", "L0_ffn_m1", "L0_ffn_v1",
          "L0_ffn_W2", "L0_ffn_b2", "L0_ffn_g2", "L0_ffn_be2", "L0_ffn_m2", "L0_ffn_v2", "L0_ffn_Wo", "L0_ffn_bo")


def gnn_and_mixture(nc, a, out):
    T = Tensors()
    T.x, T.src, T.dst, T.ew, T.gamma, T.beta, T.W, T.b = [a[n] for n in INPUTS[:8]]
    T.Wr, T.br, T.W1, T.W2, T.Wo, T.bo = [a["L0_ffn_" + n] for n in ("Wr", "br", "W1", "W2", "Wo", "bo")]
    T.vec_inputs = [a["L0_ffn_" + n] for n in ("b1", "g1", "be1", "m1", "v1", "b2", "g2", "be2", "m2", "v2")]
    T.out = out
    T.N, T.E, T.EX = T.x.shape[0], T.src.shape[0], T.Wr.shape[1]
    T.OC = T.W.shape[0] // P
    T.NG = (T.N + GROUP - 1) // GROUP
    assert T.NG % 2 == 1 and T.x.shape[1] == D and T.W.shape[0] == BANDS * D
    T.first_row = lambda g: g * GROUP if not isinstance(g, int) else min(g * GROUP, T.N - GROUP)
    T.CHUNKS = -(-T.E // (P * UN)) * UN
    T.EDGE_BLOCKS = -(-T.CHUNKS // (P * PAIR))
    T.ACC_ROWS = T.NG * GROUP
    assert T.ACC_ROWS >= T.N + P and 2 * WIN == P

    T.table = nc.dram_tensor("node_table", [BANDS * T.N, 2 * D], F32, kind="Internal").ap()
    T.acc = [nc.dram_tensor(f"message_sum{i}", [T.ACC_ROWS, D], F32, kind="Internal").ap() for i in range(NACC)]
    T.rows16 = nc.dram_tensor("edge_rows", [T.EDGE_BLOCKS * P * PAIR, 2, P], U16, kind="Internal").ap()
    T.base_dram = nc.dram_tensor("window_rows", [T.EDGE_BLOCKS * P], I32, kind="Internal").ap()

    with Stage(nc) as K:
        T.ident, T.ident_r = K.sb("ident", [P, P]), K.sb("ident_r", [P, P], F32R)
        T.win_row, T.spare = K.sb("win_row", [2 * WIN, 1]), K.sb("spare_row", [P, HALF])
        T.rank, T.unrank = K.sb("rank", [P, 1]), K.sb("unrank", [P, 1])
        T.zeros = K.sb("zeros", [P, TG * D])
        T.eps_ln, T.eps_ffn = K.sb("eps_ln", [P, 1]), K.sb("eps_ffn", [P, 1])
        T.base_row = K.sb("base_row", [1, T.EDGE_BLOCKS * P], I32)
        T.flags = K.sb("flags", [1, 2], I32)
        T.edges = K.sb("edges", [P, T.EDGE_BLOCKS * P * PAIR // HALF, FIELDS, HALF])
        with Stage(nc) as G:
            T.gam, T.bet = G.sb("gamma", [P, KD]), G.sb("beta", [P, KD])
            T.bn_scale, T.bn_shift, T.bn_neg = G.sb("bn_scale", [P, KD]), G.sb("bn_shift", [P, KD]), G.sb("bn_neg", [P, 2 * KD])
            T.bias_bc = G.sb("bias_bc", [P, BANDS * D])
            T.wt = G.sb("w_turned", [P, KD, BANDS * D])
            stage_setup(nc, T)
            stage_edges(nc, T)
            T.xt = G.sb("xt", [P, KD, T.N])
            stage_norm(nc, T)
            stage_stats(nc, T)
            stage_table(nc, T, False)
            stage_table(nc, T, True)
        T.w1, T.w2, T.wo = [[K.sb(f"{n}_{h}", [P, KD, T.EX, D], F32R) for h in ("hi", "lo")] for n in ("w1", "w2", "wo")]
        T.wr = [K.sb(f"wr_{h}", [P, KD, T.EX], F32R) for h in ("hi", "lo")]
        T.br_bc, T.bo_sb = K.sb("br_bc", [P, T.EX]), K.sb("bo_sb", [T.EX, D])
        T.vec_cols = K.sb("vec_cols", [P, 4, T.EX * KD])
        stage_weights(nc, T)
        stage_messages(nc, T)
        stage_mixture(nc, T)


def kernel(**inputs):
    import numpy as _np
    import concourse.bacc as _bacc
    from concourse import mybir as _mybir
    from concourse.bass_utils import run_bass_kernel_spmd as _run

    nc = _bacc.Bacc("TRN2", target_bir_lowering=False, num_devices=1)
    arrays, args = {}, {}
    for name in INPUTS:
        v = _np.ascontiguousarray(inputs[name])
        arrays[f"in_{name}_dram"] = v
        args[name] = nc.dram_tensor(f"in_{name}_dram", v.shape, _mybir.dt.from_np(v.dtype), kind="ExternalInput").ap()
    out = nc.dram_tensor("out_0_dram", inputs["x"].shape, F32, kind="ExternalOutput").ap()
    gnn_and_mixture(nc, args, out)
    r = _run(nc, [arrays], core_ids=[0])
    return r.results[0]["out_0_dram"]
```

```python
from contextlib import ExitStack

import concourse.bass as bass
from concourse import mybir

F32 = mybir.dt.float32
F32R = mybir.dt.float32r
I32 = mybir.dt.int32
U16 = mybir.dt.uint16
ALU = mybir.AluOpType
ACT = mybir.ActivationFunctionType
AX = mybir.AxisListType.X

P = 128
D = 256
KD = D // P
GROUP = 512
TG = GROUP // P
LN_EPS = 1e-5
GNN_EPS = 1e-5
FFN_EPS = 1e-3
NACC = 4
UN = 8
HALF = 4
WIN = 64
PAIR = 2
BANDS = 4
SRC, WGT, DST = range(3)
FIELDS = 3


def wait_turns(eng, sem, n):
    if not isinstance(n, int) or n > 0:
        eng.wait_ge(sem, n)


def in_pairs(eng, n, *ops):
    most = max(lag for lag, _ in ops)

    def one(j, par):
        for lag, op in ops:
            back, parity = (par - lag) // 2, (par - lag) % 2
            g = 2 * (j + back) + parity
            if not isinstance(j, int) or 0 <= g < n:
                op(j + back, parity, g)

    first = 1 + (most + 1) // 2
    for g in range(2 * first):
        one(g // 2, g % 2)
    with eng.Fori(first, n // 2) as j:
        for par in range(2):
            one(j, par)
    for g in range(n - 1, n + most):
        one(g // 2, g % 2)


def fixed(eng, value):
    return value if isinstance(value, int) else eng.snap(value)


def alone(eng, passed):
    eng.sem_inc(passed, 1)


class Stage:

    def __init__(self, nc):
        self.nc = nc
        self.ctx = ExitStack()
        self.semaphores = []

    def __enter__(self):
        self.ctx.__enter__()
        return self

    def __exit__(self, *a):
        if self.semaphores:
            self.nc.clear_and_free_semaphores(self.semaphores)
            self.nc.all_engine_barrier()
        return self.ctx.__exit__(*a)

    def sb(self, name, shape, dt=F32):
        return self.ctx.enter_context(self.nc.sbuf_tensor(name, shape, dt))

    def ps(self, name, shape):
        return self.ctx.enter_context(self.nc.psum_tensor(name, shape, F32))

    def sem(self, name):
        self.semaphores.append(self.nc.alloc_semaphore(name=name))
        return self.semaphores[-1]

    def sems(self, name, n):
        return [self.sem(f"{name}{i}") for i in range(n)]


def stage_setup(nc, T):
    with Stage(nc) as S:
        wl = S.sb("w_rows", [P, T.OC, D])
        ones = S.sb("ones_sq", [P, P])
        ps = S.ps("ps_w", [P, 2, GROUP])
        vectors_loaded, w_loaded, zeroed, ones_set, consts, ident_ready, zero_stored, turned, copied = [
            S.sem(n) for n in ("vectors_loaded", "w_loaded", "zeroed", "ones_set", "consts", "ident_ready",
                               "zero_stored", "turned", "copied")]
        with nc.Block() as block:

            @block.sync
            def _(sp):
                sp.dma_start(wl[:, :, :], T.W.rearrange("(o p) d -> p o d", p=P)).then_inc(w_loaded, 16)
                with nc.allow_non_contiguous_dma(reason="two vectors of 256 as columns"):
                    sp.dma_start(T.gam[:, :], T.gamma.rearrange("(k p) -> p k", p=P)).then_inc(vectors_loaded, 16)
                    sp.dma_start(T.bet[:, :], T.beta.rearrange("(k p) -> p k", p=P)).then_inc(vectors_loaded, 16)
                sp.dma_start(T.bias_bc[:, :], T.b.rearrange("(a n) -> a n", a=1).to_broadcast([P, BANDS * D])) \
                    .then_inc(vectors_loaded, 16)
                sp.wait_ge(zeroed, 1)
                sp.dma_start(T.table[T.N:T.N + WIN, :], T.zeros[0:WIN, 0:2 * D]).then_inc(zero_stored, 16)
                sp.dma_start(T.acc[0][T.N:T.N + P, :], T.zeros[:, 0:D]).then_inc(zero_stored, 16)
                sp.wait_ge(vectors_loaded, 48)
                sp.wait_ge(zero_stored, 32)

            @block.gpsimd
            def _(pool):
                pool.memset(ones[:, :], 1.0).then_inc(ones_set, 1)
                pool.memset(T.zeros[:, :], 0.0).then_inc(zeroed, 1)
                pool.wait_ge(ones_set, 1)
                pool.affine_select(out=T.ident[:, :], in_=ones[:, :], compare_op=ALU.is_equal, fill=0.0, base=0,
                                   pattern=[[-1, P]], channel_multiplier=1).then_inc(ident_ready, 1)
                pool.wait_ge(ident_ready, 1)
                for i in range(2):
                    if i:
                        pool.wait_ge(consts, i)
                    pool.iota(T.win_row[i * WIN:(i + 1) * WIN, :], [[0, 1]], base=0, channel_multiplier=1,
                              allow_small_or_imprecise_dtypes=True).then_inc(consts, 1)
                pool.wait_ge(consts, 2)
                pool.iota(T.spare[:, :], [[0, HALF]], base=T.N, channel_multiplier=1,
                          allow_small_or_imprecise_dtypes=True).then_inc(consts, 1)
                pool.iota(T.rank[:, :].bitcast(I32), [[0, 1]], base=(127 + 63) << 23, channel_multiplier=-(1 << 23)) \
                    .then_inc(consts, 1)
                pool.iota(T.unrank[:, :].bitcast(I32), [[0, 1]], base=(127 - 63) << 23, channel_multiplier=1 << 23) \
                    .then_inc(consts, 1)
                pool.memset(T.eps_ln[:, :], LN_EPS).then_inc(consts, 1)
                pool.memset(T.eps_ffn[:, :], FFN_EPS).then_inc(consts, 1)
                pool.wait_ge(consts, 7)

            @block.tensor
            def _(pe):
                pe.wait_ge(ident_ready, 1)
                pe.wait_ge(w_loaded, 16)
                for o in range(T.OC):
                    if o >= 2:
                        pe.wait_ge(copied, o - 1)
                    for k in range(KD):
                        last = pe.transpose(ps[:, o % 2, k * P:(k + 1) * P], wl[:, o, k * P:(k + 1) * P],
                                            T.ident[:, :])
                    last.then_inc(turned, 1)

            @block.scalar
            def _(act):
                act.wait_ge(ident_ready, 1)
                act.copy(T.ident_r[:, :], T.ident[:, :])
                for o in range(T.OC):
                    act.wait_ge(turned, o + 1)
                    act.copy(T.wt[:, :, o * P:(o + 1) * P],
                             ps[:, o % 2, 0:D].rearrange("p (k n) -> p k n", k=KD)).then_inc(copied, 1)


def zero_rows(sp, T, acc, row, done):
    sp.dma_start(acc[bass.ds(row, GROUP), :].rearrange("(p t) d -> p (t d)", t=TG), T.zeros[:, :]).then_inc(done, 16)


def stage_norm(nc, T):
    with Stage(nc) as S:
        xin = S.sb("ln_x", [P, 2, TG, D])
        xl = S.sb("ln_y", [P, 2, TG, D])
        stats = S.sb("ln_stats", [P, 2, TG, 6])
        mv = S.sb("ln_mv", [P, 2, TG, 2])
        std = S.sb("ln_std", [P, 2, TG, 1])
        rstd = S.sb("ln_rstd", [P, 2, TG, 1])
        ps = S.ps("ps_ln", [P, 4, GROUP])
        x_ready, x_copied, y_ready, turned, bank_copied, stats_done, var_ready, std_ready, rstd_ready = [
            S.sems(n, 2) for n in ("x_ready", "x_copied", "y_ready", "x_turned", "xt_copied", "stats_done",
                                   "var_ready", "std_ready", "rstd_ready")]
        zero_stored, passed, sp_passed = [S.sem(n) for n in ("n_zero_stored", "n_passed", "n_sp_passed")]

        with nc.Block() as block:

            @block.sync
            def _(sp):
                def load(j, par, g):
                    nt, np = T.tiles(g)
                    row = fixed(sp, T.first_row(g))
                    zero_row = 0 if isinstance(g, int) and g == 0 else row + GROUP
                    wait_turns(sp, y_ready[par], j)
                    alone(sp, sp_passed)
                    wait_turns(sp, x_copied[par], 16 * j)
                    sp.dma_start(xin[0:np, par, 0:nt, :], T.group_rows(T.x, row, g)).then_inc(x_ready[par], 16)
                    zero_rows(sp, T, T.acc[1], zero_row, zero_stored)
                in_pairs(sp, T.NG, (0, load))
                sp.wait_ge(zero_stored, 16 * T.NG)

            @block.gpsimd
            def _(pool):
                def copy_x(j, par, g):
                    nt, np = T.tiles(g)
                    pool.wait_ge(x_ready[par], 16 * (j + 1))
                    pool.dma_start(T.group_rows(T.acc[0], T.first_row(g), g), xin[0:np, par, 0:nt, :]) \
                        .then_inc(x_copied[par], 16)
                in_pairs(pool, T.NG, (0, copy_x))
                for par in range(2):
                    pool.wait_ge(x_copied[par], 16 * (T.NG // 2 + 1 - par))

            @block.vector
            def _(dve):
                def measure(j, par, g):
                    nt, np = T.tiles(g)
                    dve.wait_ge(x_ready[par], 16 * (j + 1))
                    for t in range(nt):
                        last = dve.bn_stats(stats[0:np, par, t, :], xin[0:np, par, t, :])
                    last.then_inc(stats_done[par], 1)
                    dve.wait_ge(stats_done[par], j + 1)
                    alone(dve, passed)
                    for t in range(nt):
                        last = dve.bn_aggr(mv[0:np, par, t, :], stats[0:np, par, t, :])
                    last.then_inc(var_ready[par], 1)

                def normalise(j, par, g):
                    nt, np = T.tiles(g)
                    dve.wait_ge(std_ready[par], j + 1)
                    dve.reciprocal(rstd[0:np, par, 0:nt, :], std[0:np, par, 0:nt, :]).then_inc(rstd_ready[par], 1)
                    dve.wait_ge(rstd_ready[par], j + 1)
                    wait_turns(dve, turned[par], KD * j)
                    for t in range(nt):
                        last = dve.tensor_scalar(xl[0:np, par, t, :], xin[0:np, par, t, :], mv[0:np, par, t, 0:1],
                                                 rstd[0:np, par, t, :], ALU.subtract, ALU.mult)
                    last.then_inc(y_ready[par], 1)
                in_pairs(dve, T.NG, (0, measure), (1, normalise))

            @block.tensor
            def _(pe):
                def turn(j, par, g):
                    nt, np = T.tiles(g)
                    pe.wait_ge(y_ready[par], j + 1)
                    wait_turns(pe, bank_copied[par], KD * j)
                    for k in range(KD):
                        for t in range(nt):
                            last = pe.transpose(ps[:, 2 * par + k, t * np:(t + 1) * np],
                                                xl[0:np, par, t, k * P:(k + 1) * P], T.ident[0:np, 0:np])
                        last.then_inc(turned[par], 1)
                in_pairs(pe, T.NG, (0, turn))

            @block.scalar
            def _(act):
                def root(j, par, g):
                    nt, np = T.tiles(g)
                    act.wait_ge(var_ready[par], j + 1)
                    act.activation(std[0:np, par, 0:nt, :], mv[0:np, par, 0:nt, 1:2], ACT.Sqrt,
                                   bias=T.eps_ln[0:np, :]).then_inc(std_ready[par], 1)

                def copy_out(j, par, g):
                    nt, np = T.tiles(g)
                    for k in range(KD):
                        act.wait_ge(turned[par], KD * j + k + 1)
                        act.copy(T.xt[:, k, bass.ds(T.first_row(g), nt * np)].rearrange("f (p t) -> f t p", t=nt),
                                 ps[:, 2 * par + k, 0:nt * np].rearrange("f (t p) -> f t p", t=nt)) \
                            .then_inc(bank_copied[par], 1)
                in_pairs(act, T.NG, (0, root), (1, copy_out))


def stage_edges(nc, T):
    B = T.EDGE_BLOCKS
    L = PAIR * P
    full = T.E // L // P
    whole = T.E // L - full * P
    rest = T.E - (full * P + whole) * L
    assert full == B - 1 and 0 < rest < L and whole < P - 1 and T.N + P < 1 << 15
    with Stage(nc) as S:
        srci, dsti = S.sb("edge_src_i", [P, B, L], I32), S.sb("edge_dst_i", [P, B, L], I32)
        fields = S.sb("edge_fields", [P, FIELDS, B, L])
        rel = S.sb("edge_rel", [P, B, L])
        row16 = S.sb("edge_rows16", [P, B, PAIR, 2, P], U16)
        least, base = S.sb("edge_least", [P, B]), S.sb("edge_base", [P, B])
        most = S.sb("edge_most", [P, 2])
        base_t = S.sb("edge_base_t", [B, P], I32)
        flag_f = S.sb("flag_f", [1, 2])
        ps = S.ps("ps_edges", [P, 2, 4, P])
        ps_small = S.ps("ps_small", [P, GROUP])
        (padded, src_loaded, dst_loaded, w_loaded, filled, step, turned, copied, base_ready, base_stored, base_loaded,
         small, row16_ready, rows_stored, zero_stored) = [
            S.sem("e_" + n) for n in ("padded", "src_loaded", "dst_loaded", "w_loaded", "filled", "step", "turned",
                                      "copied", "base_ready", "base_stored", "base_loaded", "small_turned",
                                      "row16_ready", "rows_stored", "zero_stored")]

        def blocks_of(a):
            return a[0:full * P * L].rearrange("(b c e) -> c b e", c=P, e=L)

        def rows_of(a):
            return a[full * P * L:(full * P + whole) * L].rearrange("(c e) -> c e", e=L)

        def tail_of(a):
            return a[T.E - rest:T.E].rearrange("(a e) -> a e", a=1)

        with nc.Block() as block:

            @block.sync
            def _(sp):
                sp.wait_ge(padded, 3)
                for dst, a, done in ((dsti, T.dst, dst_loaded), (srci, T.src, src_loaded),
                                     (fields[:, WGT], T.ew, w_loaded)):
                    sp.dma_start(dst[:, 0:full, :], blocks_of(a)).then_inc(done, 16)
                    sp.dma_start(dst[0:whole, full, :], rows_of(a)).then_inc(done, 16)
                    sp.dma_start(dst[whole:whole + 1, full, 0:rest], tail_of(a)).then_inc(done, 16)
                    if a is T.dst:
                        sp.dma_start(dsti[whole:whole + 1, full, rest:L],
                                     T.dst[T.E - (L - rest):T.E].rearrange("(a e) -> a e", a=1)).then_inc(done, 16)
                n = 0
                for row in range(0, T.ACC_ROWS, GROUP):
                    zero_rows(sp, T, T.acc[NACC - 1], row, zero_stored)
                    n += 1
                sp.wait_ge(row16_ready, 2)
                sp.dma_start(T.rows16.rearrange("(b c s) f e -> c b (s f e)", c=P, s=PAIR),
                             row16[:, :, :, :, :].rearrange("p b s f e -> p b (s f e)")).then_inc(rows_stored, 16)
                sp.wait_ge(base_ready, 1)
                sp.dma_start(T.base_dram.rearrange("(b c) -> b c", c=P), base_t[:, :]).then_inc(base_stored, 16)
                sp.wait_ge(base_stored, 16)
                sp.dma_start(T.base_row[:, :], T.base_dram.rearrange("(a c) -> a c", a=1)).then_inc(base_loaded, 16)
                sp.wait_ge(base_loaded, 16)
                sp.wait_ge(rows_stored, 16)
                sp.wait_ge(zero_stored, 16 * n)

            @block.vector
            def _(dve):
                dve.memset(srci[:, full, :], T.N).then_inc(padded, 1)
                dve.memset(dsti[:, full, :], 0).then_inc(padded, 1)
                dve.memset(fields[:, WGT, full, :], 0.0).then_inc(padded, 1)
                dve.wait_ge(padded, 3)
                dve.wait_ge(dst_loaded, 64)
                dve.tensor_scalar(fields[:, DST], dsti[:, :, :], BANDS * T.N - 1, None, ALU.min).then_inc(step, 1)
                dve.wait_ge(src_loaded, 48)
                dve.tensor_scalar(fields[:, SRC], srci[:, :, :], T.N, None, ALU.min).then_inc(step, 1)
                dve.wait_ge(step, 2)
                dve.tensor_reduce(least[:, :], fields[:, DST], AX, ALU.min).then_inc(step, 1)
                dve.wait_ge(step, 3)
                dve.tensor_scalar(base[:, :], least[:, :], BANDS * T.N - WIN, None, ALU.min).then_inc(step, 1)
                dve.wait_ge(step, 4)
                dve.tensor_tensor(rel[:, :, :], fields[:, DST],
                                  base[:, :].rearrange("p (b a) -> p b a", a=1).to_broadcast([P, B, L]),
                                  ALU.subtract).then_inc(step, 1)
                dve.wait_ge(step, 5)
                for i, f in enumerate((fields[:, DST], rel[:, :, :])):
                    dve.tensor_reduce(most[:, i:i + 1], f.rearrange("p b e -> p (b e)"), AX, ALU.max) \
                        .then_inc(filled, 1)
                dve.wait_ge(small, 3)
                dve.tensor_copy(base_t[:, :], ps_small[0:B, 0:P]).then_inc(base_ready, 1)
                for i in range(2):
                    dve.tensor_reduce(flag_f[:, i:i + 1], ps_small[0:1, (i + 1) * P:(i + 2) * P], AX, ALU.max) \
                        .then_inc(step, 1)
                dve.wait_ge(step, 7)
                dve.tensor_scalar(T.flags[:, 0:1], flag_f[:, 0:1], T.N, None, ALU.is_ge).then_inc(step, 1)
                dve.tensor_scalar(T.flags[:, 1:2], flag_f[:, 1:2], WIN, None, ALU.is_ge).then_inc(step, 1)
                dve.wait_ge(step, 9)

            @block.gpsimd
            def _(pool):
                pool.wait_ge(step, 5)
                pool.tensor_copy(row16[:, :, :, 0, :], fields[:, SRC].rearrange("p b (s e) -> p b s e", s=PAIR)) \
                    .then_inc(row16_ready, 1)
                pool.tensor_scalar(row16[:, :, :, 1, :], rel[:, :, :].rearrange("p b (s e) -> p b s e", s=PAIR),
                                   float(WIN), None, ALU.min).then_inc(row16_ready, 1)

            @block.tensor
            def _(pe):
                pe.wait_ge(filled, 2)
                pe.wait_ge(w_loaded, 48)
                pe.transpose(ps_small[0:B, 0:P], base[:, :], T.ident[:, :]).then_inc(small, 1)
                for i in range(2):
                    pe.transpose(ps_small[0:1, (i + 1) * P:(i + 2) * P], most[:, i:i + 1], T.ident[:, :]) \
                        .then_inc(small, 1)
                for n in range(B * PAIR):
                    b, s = n // PAIR, n % PAIR
                    if n >= 2:
                        pe.wait_ge(copied, n - 1)
                    for f in range(FIELDS):
                        last = pe.transpose(ps[:, n % 2, f, :], fields[:, f, b, s * P:(s + 1) * P], T.ident[:, :])
                    last.then_inc(turned, 1)

            @block.scalar
            def _(act):
                halves = P * PAIR // HALF
                for n in range(B * PAIR):
                    b, s = n // PAIR, n % PAIR
                    act.wait_ge(turned, n + 1)
                    for a in range(HALF // PAIR):
                        last = act.copy(T.edges[:, b * halves:(b + 1) * halves, :, PAIR * a + s]
                                        .rearrange("p q f -> p f q"),
                                        ps[:, n % 2, 0:FIELDS, :].rearrange("p f (q a) -> p f q a", a=HALF // PAIR)
                                        [:, :, :, a])
                    last.then_inc(copied, 1)


def stage_stats(nc, T):
    NS = 25
    W = T.N // NS
    assert NS * W == T.N and W <= 512
    with Stage(nc) as S:
        stats = S.sb("bn_stats", [P, KD, NS, 6])
        mv = S.sb("bn_mv", [P, KD, 2])
        std, tmp = S.sb("bn_std", [P, KD, 1]), S.sb("bn_tmp", [P, KD, 1])
        step, std_ready = S.sem("bn_step"), S.sem("bn_std_ready")
        with nc.Block() as block:

            @block.vector
            def _(dve):
                for k in range(KD):
                    for n in range(NS):
                        last = dve.bn_stats(stats[:, k, n, :], T.xt[:, k, n * W:(n + 1) * W])
                last.then_inc(step, 1)
                dve.wait_ge(step, 1)
                for k in range(KD):
                    last = dve.bn_aggr(mv[:, k, :], stats[:, k, :, :])
                last.then_inc(step, 1)
                dve.wait_ge(step, 2)
                dve.wait_ge(std_ready, 1)
                dve.reciprocal(tmp[:, :, :], std[:, :, :]).then_inc(step, 1)
                dve.wait_ge(step, 3)
                dve.tensor_tensor(T.bn_scale[:, :], T.gam[:, :], tmp[:, :, 0], ALU.mult).then_inc(step, 1)
                dve.wait_ge(step, 4)
                dve.tensor_tensor(tmp[:, :, 0], mv[:, :, 0], T.bn_scale[:, :], ALU.mult).then_inc(step, 1)
                dve.wait_ge(step, 5)
                dve.tensor_tensor(T.bn_shift[:, :], T.bet[:, :], tmp[:, :, 0], ALU.subtract).then_inc(step, 1)
                dve.wait_ge(step, 6)
                dve.tensor_scalar(T.bn_neg[:, 0:KD], T.bn_scale[:, :], -1.0, None, ALU.mult).then_inc(step, 1)
                dve.tensor_scalar(T.bn_neg[:, KD:2 * KD], T.bn_shift[:, :], -1.0, None, ALU.mult).then_inc(step, 1)
                dve.wait_ge(step, 8)

            @block.scalar
            def _(act):
                act.wait_ge(step, 2)
                act.activation(std[:, :, :], mv[:, :, 1:2], ACT.Sqrt, bias=T.eps_ln[:, :]).then_inc(std_ready, 1)


def stage_table(nc, T, extra):
    tag = "x_" if extra else ""
    per = [T.NG // 2 + 1, T.NG // 2]
    with Stage(nc) as S:
        pos = S.sb(tag + "elu_pos", [P, 2, KD, GROUP])
        neg = S.sb(tag + "elu_neg", [P, 2, KD, GROUP])
        xe = S.sb(tag + "elu", [P, 2, KD, GROUP])
        rows = S.sb(tag + "table_rows", [P, 2, TG, D])
        parts = S.sb(tag + "table_parts", [P, 2, TG, 2, D], F32R)
        ps = S.ps(tag + "ps_table", [P, 4, GROUP])
        neg_ready, elu_parts, elu_ready, products, bank_read, rows_hi, rows_lo, stored = [
            S.sems(tag + n, 2) for n in ("neg_ready", "elu_parts", "elu_ready", "products", "bank_read",
                                         "rows_hi", "rows_lo", "rows_stored")]
        zero_stored = S.sem(tag + "t_zero_stored")

        def bands(eng, run):
            if not extra:
                run(0, (0, 0))
                return
            flag = eng.value_load(T.flags[0:1, 0:1], min_val=0, max_val=1)
            with eng.If(flag):
                for band in range(1, BANDS):
                    run(band, [(band - 1) * per[0], (band - 1) * per[1]])

        with nc.Block() as block:

            @block.scalar
            def _(act):
                def run(band, before):
                    def elu_terms(j, par, g):
                        turn = before[par] + j
                        nt, np = T.tiles(g)
                        w = nt * np
                        cols = bass.ds(T.first_row(g), w)
                        wait_turns(act, elu_ready[par], turn)
                        for k in range(KD):
                            last = act.activation(neg[:, par, k, 0:w], T.xt[:, k, cols], ACT.Relu,
                                                  bias=T.bn_neg[:, KD + k:KD + k + 1], scale=T.bn_neg[:, k:k + 1])
                        last.then_inc(neg_ready[par], 1)
                        for k in range(KD):
                            act.activation(pos[:, par, k, 0:w], T.xt[:, k, cols], ACT.Relu,
                                           bias=T.bn_shift[:, k:k + 1], scale=T.bn_scale[:, k:k + 1])
                        act.wait_ge(neg_ready[par], turn + 1)
                        act.activation(neg[:, par, :, 0:w], neg[:, par, :, 0:w], ACT.Exp, scale=-1.0) \
                            .then_inc(elu_parts[par], 1)

                    def rows_high(j, par, g):
                        turn = before[par] + j
                        nt, np = T.tiles(g)
                        act.wait_ge(bank_read[par], 2 * (turn + 1))
                        wait_turns(act, stored[par], 16 * turn)
                        act.copy(parts[0:np, par, 0:nt, 0, :], rows[0:np, par, 0:nt, :]).then_inc(rows_hi[par], 1)
                    in_pairs(act, T.NG, (0, elu_terms), (2, rows_high))
                bands(act, run)

            @block.vector
            def _(dve):
                def run(band, before):
                    def combine(j, par, g):
                        turn = before[par] + j
                        nt, np = T.tiles(g)
                        w = nt * np
                        dve.wait_ge(elu_parts[par], turn + 1)
                        wait_turns(dve, products[par], 2 * turn)
                        dve.scalar_tensor_tensor(out=xe[:, par, :, 0:w], in0=neg[:, par, :, 0:w], scalar=-1.0,
                                                 in1=pos[:, par, :, 0:w], op0=ALU.add, op1=ALU.add) \
                            .then_inc(elu_ready[par], 1)

                    def add_bias(j, par, g):
                        turn = before[par] + j
                        nt, np = T.tiles(g)
                        bias = T.bias_bc[0:np, band * D:(band + 1) * D].rearrange("p (a d) -> p a d", a=1) \
                            .to_broadcast([np, nt // 2, D])
                        wait_turns(dve, rows_lo[par], turn)
                        for i in range(2):
                            tiles = slice(i * nt // 2, (i + 1) * nt // 2)
                            dve.wait_ge(products[par], 2 * turn + i + 1)
                            dve.tensor_tensor(rows[0:np, par, tiles, :],
                                              ps[0:np, 2 * par + i, 0:nt // 2 * D].rearrange("p (t d) -> p t d", d=D),
                                              bias, ALU.add).then_inc(bank_read[par], 1)
                    in_pairs(dve, T.NG, (0, combine), (1, add_bias))
                bands(dve, run)

            @block.gpsimd
            def _(pool):
                def run(band, before):
                    def rows_low(j, par, g):
                        turn = before[par] + j
                        nt, np = T.tiles(g)
                        pool.wait_ge(rows_hi[par], turn + 1)
                        pool.tensor_tensor(parts[0:np, par, 0:nt, 1, :], rows[0:np, par, 0:nt, :],
                                           parts[0:np, par, 0:nt, 0, :].bitcast(F32), ALU.subtract) \
                            .then_inc(rows_lo[par], 1)
                    in_pairs(pool, T.NG, (0, rows_low))
                bands(pool, run)

            @block.tensor
            def _(pe):
                def run(band, before):
                    def multiply(j, par, g):
                        turn = before[par] + j
                        nt, np = T.tiles(g)
                        pe.wait_ge(elu_ready[par], turn + 1)
                        wait_turns(pe, bank_read[par], 2 * turn)
                        for i in range(2):
                            for n in range(nt // 2):
                                t = i * nt // 2 + n
                                for k in range(KD):
                                    last = pe.matmul(ps[0:np, 2 * par + i, n * D:(n + 1) * D],
                                                     xe[:, par, k, t * np:(t + 1) * np],
                                                     T.wt[:, k, band * D:(band + 1) * D],
                                                     start=(k == 0), stop=(k == KD - 1))
                            last.then_inc(products[par], 1)
                    in_pairs(pe, T.NG, (0, multiply))
                bands(pe, run)

            @block.sync
            def _(sp):
                def run(band, before):
                    def store(j, par, g):
                        turn = before[par] + j
                        nt, np = T.tiles(g)
                        row = T.first_row(g)
                        zero_row = 0 if isinstance(g, int) and g == 0 else row + GROUP
                        row = fixed(sp, band * T.N + row)
                        if not extra:
                            zero_rows(sp, T, T.acc[2], fixed(sp, zero_row), zero_stored)
                        sp.wait_ge(rows_lo[par], turn + 1)
                        sp.dma_start(T.table[bass.ds(row, nt * np), :].rearrange("(t p) d -> p t d", p=np),
                                     parts[0:np, par, 0:nt, :, :].rearrange("p t h d -> p t (h d)").bitcast(F32)) \
                            .then_inc(stored[par], 16)
                    in_pairs(sp, T.NG, (0, store))
                    for par in range(2):
                        sp.wait_ge(stored[par], 16 * (before[par] + per[par]))
                bands(sp, run)
                if not extra:
                    sp.wait_ge(zero_stored, 16 * T.NG)


def stage_weights(nc, T):
    EX = T.EX
    R = EX * KD
    mats = ((T.W1, T.w1), (T.W2, T.w2), (T.Wo, T.wo))
    vecs = T.vec_inputs
    with Stage(nc) as S:
        raw = S.sb("w_raw", [P, 2, EX, D])
        v = S.sb("vectors", [R, 10, P])
        sc = S.sb("vec_scale", [R, 2, P])
        sh = S.sb("vec_shift", [R, 2, P])
        wr = S.sb("wr_raw", [P, KD, EX])
        ps = S.ps("ps_vec", [P, 4, R])
        w_loaded = S.sems("we_loaded", 2)
        hi_ready, lo_ready, v_loaded, step, std_ready, turned, wr_loaded = [
            S.sem(n) for n in ("hi_ready", "lo_ready", "vec_loaded", "vec_step", "vec_std", "vec_turned", "wr_loaded")]
        with nc.Block() as block:

            @block.sync
            def _(sp):
                for i, a in enumerate(vecs):
                    sp.dma_start(v[:, i, :], a.rearrange("e (k p) -> (e k) p", p=P)).then_inc(v_loaded, 16)
                with nc.allow_non_contiguous_dma(reason="gate weights, small"):
                    sp.dma_start(wr[:, :, :], T.Wr.rearrange("(k p) e -> p k e", p=P)).then_inc(wr_loaded, 16)
                sp.dma_start(T.br_bc[:, :], T.br.rearrange("(a n) -> a n", a=1).to_broadcast([P, EX])) \
                    .then_inc(wr_loaded, 16)
                sp.dma_start(T.bo_sb[:, :], T.bo).then_inc(wr_loaded, 16)
                n = 0
                for a, _ in mats:
                    for k in range(KD):
                        if n >= 2:
                            sp.wait_ge(lo_ready, n - 1)
                        sp.dma_start(raw[:, n % 2, :, :], a[:, k * P:(k + 1) * P, :].rearrange("e p h -> p e h")) \
                            .then_inc(w_loaded[n % 2], 16)
                        n += 1

            @block.vector
            def _(dve):
                n = 0
                for _, (hi, lo) in mats:
                    for k in range(KD):
                        dve.wait_ge(hi_ready, n + 1)
                        dve.tensor_tensor(lo[:, k, :, :], raw[:, n % 2, :, :], hi[:, k, :, :].bitcast(F32),
                                          ALU.subtract).then_inc(lo_ready, 1)
                        n += 1
                dve.wait_ge(hi_ready, n + 1)
                dve.tensor_tensor(T.wr[:, :, 1, :], wr[:, :, :], T.wr[:, :, 0, :].bitcast(F32), ALU.subtract) \
                    .then_inc(lo_ready, 1)
                dve.wait_ge(std_ready, 1)
                dve.reciprocal(sh[:, :, :], sc[:, :, :]).then_inc(step, 1)
                dve.wait_ge(step, 1)
                for i in range(2):
                    dve.tensor_tensor(sc[:, i, :], v[:, 5 * i + 1, :], sh[:, i, :], ALU.mult).then_inc(step, 1)
                dve.wait_ge(step, 3)
                for i in range(2):
                    dve.tensor_tensor(sh[:, i, :], v[:, 5 * i, :], v[:, 5 * i + 3, :], ALU.subtract).then_inc(step, 1)
                dve.wait_ge(step, 5)
                for i in range(2):
                    dve.tensor_tensor(sh[:, i, :], sh[:, i, :], sc[:, i, :], ALU.mult).then_inc(step, 1)
                dve.wait_ge(step, 7)
                for i in range(2):
                    dve.tensor_tensor(sh[:, i, :], sh[:, i, :], v[:, 5 * i + 2, :], ALU.add).then_inc(step, 1)
                dve.wait_ge(step, 9)
                dve.wait_ge(turned, 1)
                dve.tensor_copy(T.vec_cols[:, :, :], ps[:, :, :]).then_inc(step, 1)
                dve.wait_ge(step, 10)

            @block.scalar
            def _(act):
                n = 0
                for _, (hi, _) in mats:
                    for k in range(KD):
                        act.wait_ge(w_loaded[n % 2], 16 * (n // 2 + 1))
                        act.copy(hi[:, k, :, :], raw[:, n % 2, :, :]).then_inc(hi_ready, 1)
                        n += 1
                act.wait_ge(wr_loaded, 48)
                act.copy(T.wr[:, :, 0, :], wr[:, :, :]).then_inc(hi_ready, 1)
                act.wait_ge(v_loaded, 160)
                for i in range(2):
                    last = act.activation(sc[:, i, :], v[:, 5 * i + 4, :], ACT.Sqrt, bias=T.eps_ffn[0:R, :])
                last.then_inc(std_ready, 1)

            @block.tensor
            def _(pe):
                pe.wait_ge(step, 9)
                for i in range(2):
                    pe.transpose(ps[:, 2 * i, :], sc[:, i, :], T.ident[0:R, 0:R])
                    last = pe.transpose(ps[:, 2 * i + 1, :], sh[:, i, :], T.ident[0:R, 0:R])
                last.then_inc(turned, 1)


def stage_messages(nc, T):
    ROUNDS = T.CHUNKS // UN
    NH = UN // HALF
    NB = 4
    C = D + 2
    with Stage(nc) as S:
        edge = S.sb("edge_cols", [P, NH, FIELDS, HALF])
        row16 = S.sb("edge_row16", [P, NH, HALF, 2, P], U16)
        same = S.sb("same_target", [P, UN, P], F32R)
        spread = S.sb("spread", [P, UN, P], F32R)
        win = S.sb("window", [P, UN // PAIR, D], F32R)
        gathered = S.sb("gathered", [P, UN, 2, D], F32R)
        w_hi = S.sb("weighted_hi", [P, UN, C], F32R)
        w_lo = S.sb("weighted_lo", [P, UN, C], F32R)
        sums = S.sb("chunk_sums", [P, UN, C])
        later = S.sb("later", [P, NH, HALF])
        own = S.sb("own_target", [P, NH, HALF])
        away = S.sb("away", [P, NH, HALF])
        target = S.sb("target_row", [P, NH, HALF], I32)
        rowi = S.sb("table_row_i", [P, NH, HALF], I32)
        ps_rows = S.ps("ps_rows", [P, NB, GROUP])
        ps_sum = S.ps("ps_sum", [P, NB, GROUP])
        ranked, zero_col = S.sem("ranked"), S.sem("zero_col")

        edge_ready, row16_loaded, target_ready, rowi_ready, later_ready, own_ready, away_ready = [
            S.sems(n, NH) for n in ("edge_ready", "row16_loaded", "target_ready", "rowi_ready", "later_ready",
                                    "own_ready", "away_ready")]
        rows_read, sum_copied = [S.sems(n, NB) for n in ("rows_read", "sum_copied")]
        rows_ready, spread_ready, same_ready, rows_out, hi_ready, sum_ready, added = [
            S.sems(n, UN) for n in ("rows_ready", "spread_ready", "same_ready", "rows_out", "hi_ready",
                                    "sum_ready", "added")]
        passed = S.sem("m_passed")

        def run(windows):
            def slots():
                return [(u, u // HALF, u % HALF, u % NB, u // NB) for u in range(UN)]

            PB = UN // NB

            def rounds(eng, *ops):
                def body(r, first=False):
                    for u in range(UN):
                        for delay, op in ops:
                            if u >= delay:
                                op(r, *slots()[u - delay])
                            elif not first:
                                op(r - 1, *slots()[u - delay + UN])
                written = 1 + any(delay for delay, _ in ops)
                for r in range(written):
                    body(r, r == 0)
                with eng.Fori(written, ROUNDS) as r:
                    body(r)
                for u in range(max(delay for delay, _ in ops)):
                    for delay, op in ops:
                        if u < delay:
                            op(ROUNDS - 1, *slots()[u - delay + UN])

            def sync(sp):
                def load(r, u, h, i, bank, n):
                    if i == 0:
                        chunk = r * UN + h * HALF
                        if not isinstance(chunk, int):
                            chunk = sp.snap(chunk)
                        wait_turns(sp, same_ready[HALF * h + HALF - 1], r)
                        sp.dma_start(row16[:, h, :, :, :].rearrange("p c f e -> p (c f e)"),
                                     T.rows16[bass.ds(chunk, HALF), :, :].rearrange("(a c) f e -> a (c f e)", a=1)
                                     .to_broadcast([P, HALF * 2 * P])).then_inc(row16_loaded[h], 16)
                    if windows and i % PAIR == 0:
                        w = u // PAIR
                        row = sp.value_load(T.base_row[0:1, bass.ds(r * (UN // PAIR) + w, 1)], min_val=0,
                                            max_val=BANDS * T.N - WIN)
                        wait_turns(sp, rows_out[u + PAIR - 1], r)
                        sp.dma_start(win[:, w, :].bitcast(F32),
                                     T.table[bass.ds(row, WIN), :].rearrange("r (k d) -> k r d", k=2)) \
                            .then_inc(rows_ready[u], 16)
                rounds(sp, (0, load))

            def scalar(act):
                def fetch(r, u, h, i, bank, n):
                    if i:
                        return
                    wait_turns(act, rows_read[NB - 1], PB * r + h - 1)
                    act.copy(edge[:, h, :, :], T.edges[:, NH * r + h, :, :]).then_inc(edge_ready[h], 1)

                def weight_rows(r, u, h, i, bank, n):
                    if i == 0:
                        act.wait_ge(edge_ready[h], r + 1)
                    act.wait_ge(rows_out[u], r + 1)
                    wait_turns(act, sum_ready[u], r)
                    act.activation(w_hi[:, u, 0:D], ps_rows[:, bank, 0:D], ACT.Copy, scale=edge[:, h, WGT, i:i + 1]) \
                        .then_inc(hi_ready[u], 1)

                def sum_out(r, u, h, i, bank, n):
                    act.wait_ge(sum_ready[u], r + 1)
                    wait_turns(act, added[u], 16 * r)
                    act.copy(sums[:, u, 0:D + 1], ps_sum[:, bank, 0:D + 1]).then_inc(sum_copied[bank], 1)

                rounds(act, (0, fetch), (1, weight_rows), (6, sum_out))

            def tensor(pe):
                def bring_rows(r, u, h, i, bank, n):
                    wait_turns(pe, rows_read[bank], PB * r + n)
                    if windows:
                        pe.wait_ge(spread_ready[u], r + 1)
                        if i % PAIR == 0:
                            pe.wait_ge(rows_ready[u], 16 * (r + 1))
                        mm = pe.matmul(ps_rows[:, bank, 0:D], spread[:, u, :], win[:, u // PAIR, :],
                                       start=True, stop=True)
                    else:
                        pe.wait_ge(rows_ready[u], 16 * (r + 1))
                        pe.matmul(ps_rows[:, bank, 0:D], T.ident_r[:, :], gathered[:, u, 0, :], start=True, stop=False)
                        mm = pe.matmul(ps_rows[:, bank, 0:D], T.ident_r[:, :], gathered[:, u, 1, :],
                                       start=False, stop=True)
                    mm.then_inc(rows_out[u], 1)

                def sum_rows(r, u, h, i, bank, n):
                    wait_turns(pe, sum_copied[bank], PB * r + n)
                    pe.wait_ge(same_ready[u], r + 1)
                    pe.wait_ge(rows_read[bank], PB * r + n + 1)
                    pe.matmul(ps_sum[:, bank, 0:C], same[:, u, :], w_hi[:, u, :], start=True, stop=False)
                    pe.matmul(ps_sum[:, bank, 0:C], same[:, u, :], w_lo[:, u, :], start=False, stop=True) \
                        .then_inc(sum_ready[u], 1)

                pe.wait_ge(zero_col, 1)
                pe.wait_ge(ranked, 1)
                rounds(pe, (0, bring_rows), (4, sum_rows))

            def vector(dve):
                def compare(r, u, h, i, bank, n):
                    if i == 0:
                        dve.wait_ge(edge_ready[h], r + 1)
                        dve.wait_ge(row16_loaded[h], 16 * (r + 1))
                        if not windows:
                            for k in range(HALF):
                                wait_turns(dve, rows_ready[HALF * h + k], 16 * r)
                            dve.tensor_copy(rowi[:, h, :], edge[:, h, DST, :]).then_inc(rowi_ready[h], 1)
                    if windows:
                        wait_turns(dve, rows_out[u], r)
                        dve.tensor_scalar(spread[:, u, :], row16[:, h, i, 1, :], T.win_row[:, :], None, ALU.is_equal) \
                            .then_inc(spread_ready[u], 1)
                    wait_turns(dve, sum_ready[u], r)
                    dve.tensor_scalar(same[:, u, :], row16[:, h, i, 0, :], edge[:, h, SRC, i:i + 1], None,
                                      ALU.is_equal).then_inc(same_ready[u], 1)

                def keep(r, u, h, i, bank, n):
                    if i == 0:
                        wait_turns(dve, target_ready[h], r)
                        dve.tensor_copy(own[:, h, :], edge[:, h, SRC, :]).then_inc(own_ready[h], 1)
                        dve.tensor_tensor(away[:, h, :], T.spare[:, :], edge[:, h, SRC, :], ALU.subtract) \
                            .then_inc(away_ready[h], 1)

                def weight_low(r, u, h, i, bank, n):
                    dve.wait_ge(hi_ready[u], r + 1)
                    dve.scalar_tensor_tensor(out=w_lo[:, u, 0:D], in0=ps_rows[:, bank, 0:D],
                                             scalar=edge[:, h, WGT, i:i + 1], in1=w_hi[:, u, 0:D].bitcast(F32),
                                             op0=ALU.mult, op1=ALU.subtract).then_inc(rows_read[bank], 1)

                def targets(r, u, h, i, bank, n):
                    if i < HALF - 1:
                        return
                    for _, hh, _, b, m in slots():
                        if hh == h:
                            dve.wait_ge(sum_copied[b], PB * r + m + 1)
                    ranks = sums[:, HALF * h:HALF * (h + 1), D]
                    dve.tensor_scalar(later[:, h, :], ranks, T.unrank[:, :], 2.5, ALU.mult, ALU.is_ge) \
                        .then_inc(later_ready[h], 1)
                    dve.wait_ge(later_ready[h], r + 1)
                    dve.wait_ge(away_ready[h], 2 * r + 1)
                    dve.tensor_tensor(away[:, h, :], away[:, h, :], later[:, h, :], ALU.mult) \
                        .then_inc(away_ready[h], 1)
                    dve.wait_ge(away_ready[h], 2 * r + 2)
                    for k in range(HALF):
                        wait_turns(dve, added[HALF * h + k], 16 * r)
                    dve.tensor_tensor(target[:, h, :], away[:, h, :], own[:, h, :], ALU.add) \
                        .then_inc(target_ready[h], 1)

                rounds(dve, (0, compare), (7, targets), (3, keep), (3, weight_low))

            def gpsimd(pool):
                def gather(r, u, h, i, bank, n):
                    if i == 0:
                        pool.wait_ge(rowi_ready[h], r + 1)
                    wait_turns(pool, rows_out[u], r)
                    alone(pool, passed)
                    pool.indirect_dma_start(gathered[:, u, :, :].rearrange("p h d -> p (h d)").bitcast(F32), None, T.table,
                                            bass.IndirectOffsetOnAxis(ap=rowi[:, h, i:i + 1], axis=0)) \
                        .then_inc(rows_ready[u], 16)

                def add(r, u, h, i, bank, n):
                    if i == 0:
                        pool.wait_ge(target_ready[h], r + 1)
                    if u < NACC:
                        wait_turns(pool, added[u + NACC], 16 * r)
                    else:
                        pool.wait_ge(added[u - NACC], 16 * (r + 1))
                    alone(pool, passed)
                    pool.indirect_dma_start(T.acc[u % NACC], bass.IndirectOffsetOnAxis(ap=target[:, h, i:i + 1], axis=0),
                                            sums[:, u, 0:D], None, compute_op=ALU.add).then_inc(added[u], 16)

                if windows:
                    rounds(pool, (0, add))
                else:
                    rounds(pool, (0, gather), (UN, add))
                for u in range(UN):
                    pool.wait_ge(added[u], 16 * ROUNDS)

            return sync, scalar, tensor, vector, gpsimd

        one_by_one = run(False)
        by_window = run(True)

        def either(eng, k):
            flag = eng.value_load(T.flags[0:1, 1:2], min_val=0, max_val=1)
            with eng.If(flag):
                one_by_one[k](eng)
            with eng.Else():
                by_window[k](eng)

        with nc.Block() as block:

            @block.sync
            def _(sp):
                either(sp, 0)

            @block.scalar
            def _(act):
                act.copy(w_hi[:, :, D:D + 1], T.rank[:, :].rearrange("p (a b) -> p a b", a=1).to_broadcast([P, UN, 1])) \
                    .then_inc(ranked, 1)
                either(act, 1)

            @block.tensor
            def _(pe):
                either(pe, 2)

            @block.vector
            def _(dve):
                zero = T.zeros[:, 0:2 * UN].rearrange("p (u c) -> p u c", u=UN)
                dve.tensor_copy(w_hi[:, :, D + 1:C], zero[:, :, 0:1])
                dve.tensor_copy(w_lo[:, :, D:C], zero).then_inc(zero_col, 1)
                either(dve, 3)

            @block.gpsimd
            def _(pool):
                either(pool, 4)


def stage_mixture(nc, T):
    EX, NZ = T.EX, 4
    STEPS = EX + 2
    AMONG = 4
    with Stage(nc) as S:
        y = S.sb("y", [P, 2, TG, D])
        spent = T.edges[:, :, :, :].rearrange("p q f i -> p (q f i)")
        part = spent[:, 0:(NACC - 1) * TG * D].rearrange("p (s t d) -> p s t d", s=NACC - 1, t=TG)
        act_f = S.sb("act_f", [P, NZ, GROUP])
        xl = S.sb("xl", [P, TG, D])
        xhi = S.sb("xl_t_hi", [P, 2, KD, GROUP], F32R)
        xlo = S.sb("xl_t_lo", [P, 2, KD, GROUP], F32R)
        h_hi = [S.sb(f"h{l}_hi", [P, 2, KD, GROUP], F32R) for l in (1, 2)]
        h_lo = [S.sb(f"h{l}_lo", [P, 2, KD, GROUP], F32R) for l in (1, 2)]
        stats, mv = S.sb("m_stats", [P, TG, 6]), S.sb("m_mv", [P, TG, 2])
        std, rstd = S.sb("m_std", [P, TG, 1]), S.sb("m_rstd", [P, TG, 1])
        lg = S.sb("logits", [P, TG, EX])
        red = S.sb("gate_red", [P, 3, TG, 1])
        gate = S.sb("gate", [P, 2, TG, EX])
        gate_t = S.sb("gate_t", [EX, TG, P])
        z = [S.ps(f"z{i}", [P, GROUP]) for i in range(NZ)]
        o = [S.ps(f"o{i}", [P, 2, D]) for i in range(2)]
        tr = S.ps("tr", [P, GROUP])
        misc = S.ps("misc", [P, GROUP])

        x_loaded, y_ready, stored = [S.sems(n, 2) for n in ("mx_loaded", "my_ready", "m_stored")]
        part_loaded, part_added = S.sems("part_loaded", NACC - 1), S.sems("part_added", NACC - 1)
        z_ready, z_split, lo_ready = [S.sems(n, NZ) for n in ("z_ready", "z_split", "lo_ready")]
        o_ready, o_added = S.sems("o_ready", 2), S.sems("o_added", 2)
        passed = S.sem("mix_passed")
        (stats_done, var_ready, std_ready, rstd_ready, xl_ready, tr_ready, tr_hi, tr_read, lg_ready, gate_step, exp_ready,
         gate_ready, gate_turned, gate_t_ready, bo_ready, bo_added, l2_done, l3_done) = [
            S.sem("m_" + n) for n in ("stats_done", "var_ready", "std_ready", "rstd_ready", "xl_ready", "tr_ready",
                                      "tr_hi", "tr_read", "lg_ready", "gate_step", "exp_ready", "gate_ready",
                                      "gate_turned", "gate_t_ready", "bo_ready", "bo_added", "l2_done", "l3_done")]

        def units(s):
            n = max(0, 4 * s - 2) if s > 0 else 0
            found = []
            if s < EX:
                found += [(1, s, m) for m in range(KD)]
            if 1 <= s <= EX:
                found += [(2, s - 1, m) for m in range(KD)]
            return [(n + i, *f) for i, f in enumerate(found)]

        PER = 2 * KD * EX
        TURNS = PER // NZ
        assert [u[0] for s in range(STEPS) for u in units(s)] == list(range(PER))

        def first_count(e, layer):
            return next(u[0] for s in range(STEPS) for u in units(s) if u[1:3] == (layer, e))

        def pipelined(eng, prepare, step):
            for k in range(STEPS - AMONG):
                prepare(k, 0, 0, 0)

            def pair(j):
                for par in range(2):
                    for s in range(STEPS):
                        step(s, j, par, 2 * j + par)
                        if isinstance(j, int) and par == 0 and s < 2:
                            for k in range(AMONG // 2):
                                prepare(STEPS - AMONG + AMONG // 2 * s + k, 0, 0, 0)
                        prepare(s, j + par, 1 - par, 2 * j + par + 1)
            pair(0)
            with eng.Fori(1, T.NG // 2) as j:
                pair(j)
            for s in range(STEPS):
                step(s, T.NG // 2, 0, T.NG - 1)

        with nc.Block() as block:

            @block.sync
            def _(sp):
                def load(j, par, g):
                    nt, np = T.tiles(g)
                    row = fixed(sp, T.first_row(g))
                    wait_turns(sp, stored[par], 16 * j)
                    sp.dma_start(y[0:np, par, 0:nt, :], T.group_rows(T.acc[0], row, g)).then_inc(x_loaded[par], 16)
                    for k in range(NACC - 1):
                        wait_turns(sp, part_added[k], g)
                        sp.dma_start(part[0:np, k, 0:nt, :], T.group_rows(T.acc[k + 1], row, g)) \
                            .then_inc(part_loaded[k], 16)

                def store(j, par, g):
                    nt, np = T.tiles(g)
                    row = fixed(sp, T.first_row(g))
                    for i in range(2):
                        sp.wait_ge(o_added[i], EX * (g + 1))
                    sp.dma_start(T.group_rows(T.out, row, g), y[0:np, par, 0:nt, :]).then_inc(stored[par], 16)

                load(0, 0, 0)
                load(0, 1, 1)
                for par in range(2):
                    store(0, par, par)
                    load(1, par, par + 2)
                with sp.Fori(1, T.NG // 2 - 1) as j:
                    for par in range(2):
                        store(j, par, 2 * j + par)
                        load(j + 1, par, 2 * j + par + 2)
                n = T.NG // 2 - 1
                store(n, 0, 2 * n)
                load(n + 1, 0, 2 * n + 2)
                store(n, 1, 2 * n + 1)
                store(n + 1, 0, 2 * n + 2)
                sp.wait_ge(stored[1], 16 * (n + 1))
                sp.wait_ge(stored[0], 16 * (n + 2))

            @block.gpsimd
            def _(pool):
                def add_parts(j, par, g):
                    nt, np = T.tiles(g)
                    pool.wait_ge(x_loaded[par], 16 * (j + 1))
                    for k in range(NACC - 1):
                        pool.wait_ge(part_loaded[k], 16 * (g + 1))
                        if k:
                            pool.wait_ge(part_added[k - 1], g + 1)
                        pool.tensor_tensor(y[0:np, par, 0:nt, :], y[0:np, par, 0:nt, :], part[0:np, k, 0:nt, :], ALU.add) \
                            .then_inc(part_added[k], 1)
                in_pairs(pool, T.NG, (0, add_parts))

            @block.tensor
            def _(pe):
                def split_products(out, pairs):
                    passes = [(l[a], r[b]) for l, r in pairs for a, b in ((0, 0), (1, 0), (0, 1))]
                    for n, (l, r) in enumerate(passes):
                        last = pe.matmul(out, l, r, start=(n == 0), stop=(n == len(passes) - 1))
                    return last

                def prepare(k, j, par, g):
                    nt, np = T.tiles(g)
                    if k in (4, 5):
                        half = k - 4
                        pe.wait_ge(xl_ready, g + 1)
                        if half == 0:
                            wait_turns(pe, bo_added, 2 * g)
                        else:
                            pe.wait_ge(tr_read, 2 * g + 1)
                        for t in range(nt):
                            last = pe.transpose(tr[:, t * np:(t + 1) * np], xl[0:np, t, half * P:(half + 1) * P],
                                                T.ident[0:np, 0:np])
                        last.then_inc(tr_ready, 1)
                    if k == 6:
                        pe.wait_ge(tr_read, 2 * g + 2)
                        for t in range(nt):
                            cols = slice(t * np, (t + 1) * np)
                            for q in range(KD):
                                pe.matmul(misc[0:np, 2 * t * EX:2 * (t + 1) * EX], xhi[:, par, q, cols],
                                          T.wr[:, q, :, :].rearrange("p h e -> p (h e)"), start=(q == 0), stop=False)
                                last = pe.matmul(misc[0:np, 2 * t * EX:(2 * t + 1) * EX], xlo[:, par, q, cols],
                                                 T.wr[:, q, 0, :], start=False, stop=(q == KD - 1))
                        last.then_inc(lg_ready, 1)
                    if k == 8:
                        pe.wait_ge(gate_ready, g + 1)
                        for t in range(nt):
                            last = pe.transpose(misc[0:EX, t * P:t * P + np], gate[0:np, par, t, :],
                                                T.ident[0:np, 0:np])
                        last.then_inc(gate_turned, 1)
                    if k == 9:
                        pe.wait_ge(gate_t_ready, g + 1)
                        for i, bank in enumerate((tr, misc)):
                            for n in range(nt // 2):
                                last = pe.matmul(bank[0:np, n * D:(n + 1) * D], gate_t[:, i * nt // 2 + n, 0:np],
                                                 T.bo_sb[:, :], start=True, stop=True)
                        last.then_inc(bo_ready, 1)

                def step(s, j, par, g):
                    nt, np = T.tiles(g)
                    w = nt * np
                    for n, layer, e, m in units(s):
                        b = n % NZ
                        cols = slice(m * P, (m + 1) * P)
                        if layer == 1:
                            mat, src = T.w1, (xhi[:, par], xlo[:, par])
                            pe.wait_ge(tr_read, 2 * g + 2)
                        else:
                            mat, src = T.w2, (h_hi[0][:, e % 2], h_lo[0][:, e % 2])
                            if m == 0:
                                for q in range(KD):
                                    c = first_count(e, 1) + q
                                    pe.wait_ge(lo_ready[c % NZ], TURNS * g + c // NZ + 1)
                        wait_turns(pe, z_split[b], TURNS * g + n // NZ)
                        last = split_products(z[b][:, 0:w], [([mat[0][:, q, e, cols], mat[1][:, q, e, cols]],
                                                              [src[0][:, q, 0:w], src[1][:, q, 0:w]])
                                                             for q in range(KD)])
                        last.then_inc(z_ready[b], 1)
                    if s >= 2:
                        e = s - 2
                        for q in range(KD):
                            c = first_count(e, 2) + q
                            pe.wait_ge(lo_ready[c % NZ], TURNS * g + c // NZ + 1)
                        for i in range(2):
                            wait_turns(pe, o_added[i], EX * g + e)
                            for n in range(nt // 2):
                                t = i * nt // 2 + n
                                rows = slice(t * np, (t + 1) * np)
                                last = split_products(o[i][0:np, n, :],
                                                      [([h_hi[1][:, e % 2, q, rows], h_lo[1][:, e % 2, q, rows]],
                                                        [T.wo[0][:, q, e, :], T.wo[1][:, q, e, :]]) for q in range(KD)])
                            last.then_inc(o_ready[i], 1)
                pipelined(pe, prepare, step)

            @block.scalar
            def _(act):
                def prepare(k, j, par, g):
                    nt, np = T.tiles(g)
                    w = nt * np
                    if k == 3:
                        act.wait_ge(var_ready, g + 1)
                        act.activation(std[0:np, 0:nt, :], mv[0:np, 0:nt, 1:2], ACT.Sqrt, bias=T.eps_ln[0:np, :]) \
                            .then_inc(std_ready, 1)
                    if k in (4, 5):
                        act.wait_ge(tr_ready, 2 * g + (k - 4) + 1)
                        act.copy(xhi[:, par, k - 4, 0:w], tr[:, 0:w]).then_inc(tr_hi, 1)
                    if k == 7:
                        act.wait_ge(gate_step, 4 * g + 4)
                        act.activation(lg[0:np, 0:nt, :], lg[0:np, 0:nt, :], ACT.Exp).then_inc(exp_ready, 1)
                    if k == 8:
                        act.wait_ge(gate_turned, g + 1)
                        act.copy(gate_t[:, 0:nt, 0:np],
                                 misc[0:EX, 0:nt * P].rearrange("e (t p) -> e t p", p=P)[:, :, 0:np]) \
                            .then_inc(gate_t_ready, 1)

                def step(s, j, par, g):
                    nt, np = T.tiles(g)
                    w = nt * np
                    for n, layer, e, m in units(s):
                        b = n % NZ
                        col = T.vec_cols[:, 2 * (layer - 1), KD * e + m:KD * e + m + 1]
                        shift = T.vec_cols[:, 2 * (layer - 1) + 1, KD * e + m:KD * e + m + 1]
                        act.wait_ge(z_ready[b], TURNS * g + n // NZ + 1)
                        wait_turns(act, lo_ready[b], TURNS * g + n // NZ)
                        if m == 0:
                            if layer == 1 and e >= 2:
                                for q in range(KD):
                                    c = first_count(e - 2, 2) + q
                                    act.wait_ge(z_ready[c % NZ], TURNS * g + c // NZ + 1)
                            if layer == 2:
                                for i in range(2):
                                    if e >= 2:
                                        act.wait_ge(o_ready[i], EX * g + e - 1)
                                    else:
                                        wait_turns(act, o_ready[i], EX * g)
                            if layer == 1 and e < 2:
                                for c in range(PER - 2 * KD, PER):
                                    wait_turns(act, z_ready[c % NZ], TURNS * g)
                        act.activation(act_f[:, b, 0:w], z[b][:, 0:w], ACT.Relu, bias=shift, scale=col)
                        act.activation(h_hi[layer - 1][:, e % 2, m, 0:w], z[b][:, 0:w], ACT.Relu, bias=shift,
                                       scale=col) \
                            .then_inc(z_split[b], 1)
                pipelined(act, prepare, step)

            @block.vector
            def _(dve):
                def prepare(k, j, par, g):
                    nt, np = T.tiles(g)
                    w = nt * np
                    tiles = slice(0, nt)

                    def wide(a):
                        return a.to_broadcast([np, nt, EX])
                    if k == 3:
                        dve.wait_ge(part_added[NACC - 2], g + 1)
                        for t in range(nt):
                            last = dve.bn_stats(stats[0:np, t, :], y[0:np, par, t, :])
                        last.then_inc(stats_done, 1)
                        dve.wait_ge(stats_done, g + 1)
                        alone(dve, passed)
                        for t in range(nt):
                            last = dve.bn_aggr(mv[0:np, t, :], stats[0:np, t, :])
                        last.then_inc(var_ready, 1)
                        dve.wait_ge(var_ready, g + 1)
                        dve.wait_ge(std_ready, g + 1)
                        dve.reciprocal(rstd[0:np, tiles, :], std[0:np, tiles, :]).then_inc(rstd_ready, 1)
                        dve.wait_ge(rstd_ready, g + 1)
                        wait_turns(dve, tr_ready, 2 * g)
                        for t in range(nt):
                            last = dve.tensor_scalar(xl[0:np, t, :], y[0:np, par, t, :], mv[0:np, t, 0:1],
                                                     rstd[0:np, t, :], ALU.subtract, ALU.mult)
                        last.then_inc(xl_ready, 1)
                    if k in (4, 5):
                        dve.wait_ge(tr_hi, 2 * g + (k - 4) + 1)
                        dve.tensor_tensor(xlo[:, par, k - 4, 0:w], tr[:, 0:w], xhi[:, par, k - 4, 0:w].bitcast(F32),
                                          ALU.subtract).then_inc(tr_read, 1)
                    if k == 6:
                        found = misc[0:np, 0:nt * 2 * EX].rearrange("p (t h e) -> p t h e", h=2, e=EX)
                        logits = lg[0:np, tiles, :]
                        dve.wait_ge(lg_ready, g + 1)
                        dve.tensor_tensor(logits, found[:, :, 0, :],
                                          wide(T.br_bc[0:np, :].rearrange("p (a e) -> p a e", a=1)),
                                          ALU.add).then_inc(gate_step, 1)
                        dve.wait_ge(gate_step, 4 * g + 1)
                        dve.tensor_tensor(logits, logits, found[:, :, 1, :], ALU.add).then_inc(gate_step, 1)
                        dve.wait_ge(gate_step, 4 * g + 2)
                        dve.tensor_reduce(red[0:np, 0, tiles, :], logits, AX, ALU.max).then_inc(gate_step, 1)
                        dve.wait_ge(gate_step, 4 * g + 3)
                        dve.tensor_tensor(logits, logits, wide(red[0:np, 0, tiles, :]), ALU.subtract) \
                            .then_inc(gate_step, 1)
                    if k == 7:
                        dve.wait_ge(exp_ready, 3 * g + 1)
                        dve.tensor_reduce(red[0:np, 1, tiles, :], lg[0:np, tiles, :], AX, ALU.add).then_inc(exp_ready, 1)
                        dve.wait_ge(exp_ready, 3 * g + 2)
                        dve.reciprocal(red[0:np, 2, tiles, :], red[0:np, 1, tiles, :]).then_inc(exp_ready, 1)
                        dve.wait_ge(exp_ready, 3 * g + 3)
                        dve.tensor_tensor(gate[0:np, par, tiles, :], lg[0:np, tiles, :], wide(red[0:np, 2, tiles, :]),
                                          ALU.mult).then_inc(gate_ready, 1)
                    if k == 9:
                        dve.wait_ge(bo_ready, g + 1)
                        for i, bank in enumerate((tr, misc)):
                            half = slice(i * nt // 2, (i + 1) * nt // 2)
                            dve.tensor_tensor(y[0:np, par, half, :], y[0:np, par, half, :],
                                              bank[0:np, 0:nt // 2 * D].rearrange("p (t d) -> p t d", d=D), ALU.add) \
                                .then_inc(bo_added, 1)

                def step(s, j, par, g):
                    nt, np = T.tiles(g)
                    w = nt * np
                    for n, layer, e, m in units(s):
                        b = n % NZ
                        dve.wait_ge(z_split[b], TURNS * g + n // NZ + 1)
                        dve.tensor_tensor(h_lo[layer - 1][:, e % 2, m, 0:w], act_f[:, b, 0:w],
                                          h_hi[layer - 1][:, e % 2, m, 0:w].bitcast(F32), ALU.subtract) \
                            .then_inc(lo_ready[b], 1)
                    if s >= 2:
                        e = s - 2
                        dve.wait_ge(gate_ready, g + 1)
                        dve.wait_ge(bo_added, 2 * g + 2)
                        for i in range(2):
                            dve.wait_ge(o_ready[i], EX * g + e + 1)
                            wait_turns(dve, o_added[i], EX * g + e)
                            for n in range(nt // 2):
                                t = i * nt // 2 + n
                                last = dve.scalar_tensor_tensor(out=y[0:np, par, t, :], in0=o[i][0:np, n, :],
                                                                scalar=gate[0:np, par, t, e:e + 1],
                                                                in1=y[0:np, par, t, :], op0=ALU.mult, op1=ALU.add)
                            last.then_inc(o_added[i], 1)
                pipelined(dve, prepare, step)


class Tensors:
    pass


INPUTS = ("x", "src", "dst", "edge_weight", "L0_gnn_bn_gamma", "L0_gnn_bn_beta", "L0_gnn_W", "L0_gnn_b",
          "L0_ffn_Wr", "L0_ffn_br", "L0_ffn_W1", "L0_ffn_b1", "L0_ffn_g1", "L0_ffn_be1", "L0_ffn_m1", "L0_ffn_v1",
          "L0_ffn_W2", "L0_ffn_b2", "L0_ffn_g2", "L0_ffn_be2", "L0_ffn_m2", "L0_ffn_v2", "L0_ffn_Wo", "L0_ffn_bo")


def gnn_and_mixture(nc, a, out):
    T = Tensors()
    T.x, T.src, T.dst, T.ew, T.gamma, T.beta, T.W, T.b = [a[n] for n in INPUTS[:8]]
    T.Wr, T.br, T.W1, T.W2, T.Wo, T.bo = [a["L0_ffn_" + n] for n in ("Wr", "br", "W1", "W2", "Wo", "bo")]
    T.vec_inputs = [a["L0_ffn_" + n] for n in ("b1", "g1", "be1", "m1", "v1", "b2", "g2", "be2", "m2", "v2")]
    T.out = out
    T.N, T.E, T.EX = T.x.shape[0], T.src.shape[0], T.Wr.shape[1]
    T.OC = T.W.shape[0] // P
    T.NG = (T.N + GROUP - 1) // GROUP
    assert T.NG % 2 == 1 and T.x.shape[1] == D and T.W.shape[0] == BANDS * D
    T.REST = T.N - (T.NG - 1) * GROUP
    assert T.REST % 2 == 0 and T.REST <= 2 * P
    T.first_row = lambda g: T.N - T.REST if isinstance(g, int) and g == 0 else (g - 1) * GROUP
    T.tiles = lambda g: (2, T.REST // 2) if isinstance(g, int) and g == 0 else (TG, P)

    def group_rows(a, row, g):
        nt, np = T.tiles(g)
        return a[bass.ds(row, nt * np), :].rearrange("(p t) d -> p t d", t=nt)
    T.group_rows = group_rows
    T.CHUNKS = -(-T.E // (P * UN)) * UN
    T.EDGE_BLOCKS = -(-T.CHUNKS // (P * PAIR))
    T.ACC_ROWS = T.NG * GROUP
    assert T.ACC_ROWS >= T.N + P and 2 * WIN == P

    T.table = nc.dram_tensor("node_table", [BANDS * T.N, 2 * D], F32, kind="Internal").ap()
    T.acc = [nc.dram_tensor(f"message_sum{i}", [T.ACC_ROWS, D], F32, kind="Internal").ap() for i in range(NACC)]
    T.rows16 = nc.dram_tensor("edge_rows", [T.EDGE_BLOCKS * P * PAIR, 2, P], U16, kind="Internal").ap()
    T.base_dram = nc.dram_tensor("window_rows", [T.EDGE_BLOCKS * P], I32, kind="Internal").ap()

    with Stage(nc) as K:
        T.ident, T.ident_r = K.sb("ident", [P, P]), K.sb("ident_r", [P, P], F32R)
        T.win_row, T.spare = K.sb("win_row", [2 * WIN, 1]), K.sb("spare_row", [P, HALF])
        T.rank, T.unrank = K.sb("rank", [P, 1]), K.sb("unrank", [P, 1])
        T.zeros = K.sb("zeros", [P, TG * D])
        T.eps_ln, T.eps_ffn = K.sb("eps_ln", [P, 1]), K.sb("eps_ffn", [P, 1])
        T.base_row = K.sb("base_row", [1, T.EDGE_BLOCKS * P], I32)
        T.flags = K.sb("flags", [1, 2], I32)
        T.edges = K.sb("edges", [P, T.EDGE_BLOCKS * P * PAIR // HALF, FIELDS, HALF])
        with Stage(nc) as G:
            T.gam, T.bet = G.sb("gamma", [P, KD]), G.sb("beta", [P, KD])
            T.bn_scale, T.bn_shift, T.bn_neg = G.sb("bn_scale", [P, KD]), G.sb("bn_shift", [P, KD]), G.sb("bn_neg", [P, 2 * KD])
            T.bias_bc = G.sb("bias_bc", [P, BANDS * D])
            T.wt = G.sb("w_turned", [P, KD, BANDS * D])
            stage_setup(nc, T)
            stage_edges(nc, T)
            T.xt = G.sb("xt", [P, KD, T.N])
            stage_norm(nc, T)
            stage_stats(nc, T)
            stage_table(nc, T, False)
            stage_table(nc, T, True)
        T.w1, T.w2, T.wo = [[K.sb(f"{n}_{h}", [P, KD, T.EX, D], F32R) for h in ("hi", "lo")] for n in ("w1", "w2", "wo")]
        T.wr = K.sb("wr_parts", [P, KD, 2, T.EX], F32R)
        T.br_bc, T.bo_sb = K.sb("br_bc", [P, T.EX]), K.sb("bo_sb", [T.EX, D])
        T.vec_cols = K.sb("vec_cols", [P, 4, T.EX * KD])
        stage_weights(nc, T)
        stage_messages(nc, T)
        stage_mixture(nc, T)


def kernel(**inputs):
    import numpy as _np
    import concourse.bacc as _bacc
    from concourse import mybir as _mybir
    from concourse.bass_utils import run_bass_kernel_spmd as _run

    nc = _bacc.Bacc("TRN2", target_bir_lowering=False, num_devices=1)
    arrays, args = {}, {}
    for name in INPUTS:
        v = _np.ascontiguousarray(inputs[name])
        arrays[f"in_{name}_dram"] = v
        args[name] = nc.dram_tensor(f"in_{name}_dram", v.shape, _mybir.dt.from_np(v.dtype), kind="ExternalInput").ap()
    out = nc.dram_tensor("out_0_dram", inputs["x"].shape, F32, kind="ExternalOutput").ap()
    gnn_and_mixture(nc, args, out)
    r = _run(nc, [arrays], core_ids=[0])
    return r.results[0]["out_0_dram"]
```
